# Optimizing a Trainium2 kernel written in Bass

```python
import numpy as np
import jax
import jax.numpy as jnp

def _softmax(x, axis=-1):
    return jax.nn.softmax(x, axis=axis)

def _gelu(x):
    return jax.nn.gelu(x, approximate=True)

def _silu(x):
    return jax.nn.silu(x)

def _sigmoid(x):
    return jax.nn.sigmoid(x)

def _layernorm(x, axis=-1, eps=1e-05):
    m = jnp.mean(x, axis=axis, keepdims=True)
    v = jnp.var(x, axis=axis, keepdims=True)
    return (x - m) / jnp.sqrt(v + eps)

def _scatter_add(tgt, idx, src, axis=0):
    return tgt.at[idx].add(src)

def _segment_sum(src, seg, n):
    return jax.ops.segment_sum(src, seg, n)
kernel_name = 'mk_vit_tower_d1_tok_img1024_r4_01c2d8'

def setup_inputs(seed: int=0):
    np.random.seed(seed)
    _w = jnp.asarray

    def _rec_inputs():
        import jax
        import jax.numpy as jnp
        _rk = jax.random.key(seed)
        x = -0.00150118 + 0.499729 * jax.random.normal(jax.random.fold_in(_rk, 1), (8, 256, 64, 2), jnp.float32)
        return x
    x = _rec_inputs()

    def _L0_tok_setup():
        import jax, jax.numpy as jnp
        import numpy as np
        import math
        H = 256
        N = 64
        CH = 1
        SEQ_L = 256
        key = jax.random.key(seed)
        k1, k2, k3, k4 = jax.random.split(key, 4)
        log_dt = jax.random.uniform(k1, (H,), dtype=jnp.float32, minval=math.log(0.001), maxval=math.log(0.1))
        inv_A_real = jnp.log(0.5 * jnp.ones((H, N), jnp.float32)) + 0.1 * jax.random.normal(k2, (H, N), dtype=jnp.float32)
        A_imag = jnp.broadcast_to(math.pi * jnp.arange(N, dtype=jnp.float32), (H, N)).copy()
        B_ri = jax.random.normal(k3, (H, N, 2), dtype=jnp.float32) * 0.5
        C_ri = jax.random.normal(k4, (CH, H, N, 2), dtype=jnp.float32) * 0.5
        return {'log_dt': log_dt, 'inv_A_real': inv_A_real, 'A_imag': A_imag, 'B_ri': B_ri, 'C_ri': C_ri, 'L': SEQ_L}
    _L0_tok_all = _L0_tok_setup()
    _L0_tok_in = {k: v for k, v in _L0_tok_all.items() if k in ('log_dt', 'inv_A_real', 'A_imag', 'B_ri')}
    del _L0_tok_all

    def _L0_attn_setup():
        import jax, jax.numpy as jnp
        import numpy as np
        B, T, C = (4, 512, 256)
        NH = 16
        HS = C // NH

        def _rope_tables(seq_len, dim):
            inv_freq = 1.0 / 1000.0 ** (jnp.arange(0, dim, 2, dtype=jnp.float32) / dim)
            t = jnp.arange(seq_len, dtype=jnp.float32)[:, None] * inv_freq[None, :]
            return (jnp.sin(t), jnp.cos(t))

        def _apply_rope(q, k, sin, cos):
            qe, qo = (q[..., ::2], q[..., 1::2])
            ke, ko = (k[..., ::2], k[..., 1::2])
            q_rot = jnp.concatenate([qe * cos - qo * sin, qo * cos + qe * sin], axis=-1)
            k_rot = jnp.concatenate([ke * cos - ko * sin, ko * cos + ke * sin], axis=-1)
            return (q_rot, k_rot)
        key = jax.random.key(seed)
        k1, k2, k3, k4, k5 = jax.random.split(key, 5)
        x = jax.random.normal(k1, (B, T, C), dtype=jnp.float32)
        s = 1.0 / np.sqrt(C)
        W_attn = jax.random.uniform(k2, (3 * C, C), jnp.float32, -s, s)
        b_attn = jax.random.uniform(k3, (3 * C,), jnp.float32, -s, s)
        W_o = jax.random.uniform(k4, (C, C), jnp.float32, -s, s)
        b_o = jax.random.uniform(k5, (C,), jnp.float32, -s, s)
        return {'x': x, 'W_attn': W_attn, 'b_attn': b_attn, 'W_o': W_o, 'b_o': b_o}
    _L0_attn_all = _L0_attn_setup()
    _L0_attn_in = {k: v for k, v in _L0_attn_all.items() if k in ('W_attn', 'b_attn', 'W_o', 'b_o')}
    del _L0_attn_all

    def _L0_ffn_setup():
        import jax, jax.numpy as jnp
        import numpy as np
        D = 256
        H = 512
        E = 8
        TOP_K = 2
        N_SHARED = 1
        B, S = (2, 256)
        key = jax.random.key(seed)
        ks = jax.random.split(key, 12)
        sc = 0.02
        return {'hidden': jax.random.normal(ks[0], (B, S, D), jnp.float32), 'router_w': jax.random.normal(ks[1], (D, E), jnp.float32) * sc, 'router_b': jnp.zeros((E,), jnp.float32), 'sw1': jax.random.normal(ks[2], (D, H), jnp.float32) * sc, 'sb1': jnp.zeros((H,), jnp.float32), 'sw2': jax.random.normal(ks[3], (H, D), jnp.float32) * sc, 'sb2': jnp.zeros((D,), jnp.float32), 'rw1': jax.random.normal(ks[4], (E, D, H), jnp.float32) * sc, 'rb1': jnp.zeros((E, H), jnp.float32), 'rw2': jax.random.normal(ks[5], (E, H, D), jnp.float32) * sc, 'rb2': jnp.zeros((E, D), jnp.float32)}
    _L0_ffn_all = _L0_ffn_setup()
    _L0_ffn_in = {k: v for k, v in _L0_ffn_all.items() if k in ('router_w', 'router_b', 'sw1', 'sb1', 'sw2', 'sb2', 'rw1', 'rb1', 'rw2', 'rb2')}
    del _L0_ffn_all
    return {'x': x, 'L0_tok_log_dt': _L0_tok_in['log_dt'], 'L0_tok_inv_A_real': _L0_tok_in['inv_A_real'], 'L0_tok_A_imag': _L0_tok_in['A_imag'], 'L0_tok_B_ri': _L0_tok_in['B_ri'], 'L0_attn_W_attn': _L0_attn_in['W_attn'], 'L0_attn_b_attn': _L0_attn_in['b_attn'], 'L0_attn_W_o': _L0_attn_in['W_o'], 'L0_attn_b_o': _L0_attn_in['b_o'], 'L0_ffn_router_w': _L0_ffn_in['router_w'], 'L0_ffn_router_b': _L0_ffn_in['router_b'], 'L0_ffn_sw1': _L0_ffn_in['sw1'], 'L0_ffn_sb1': _L0_ffn_in['sb1'], 'L0_ffn_sw2': _L0_ffn_in['sw2'], 'L0_ffn_sb2': _L0_ffn_in['sb2'], 'L0_ffn_rw1': _L0_ffn_in['rw1'], 'L0_ffn_rb1': _L0_ffn_in['rb1'], 'L0_ffn_rw2': _L0_ffn_in['rw2'], 'L0_ffn_rb2': _L0_ffn_in['rb2']}

def reference(x, L0_tok_log_dt, L0_tok_inv_A_real, L0_tok_A_imag, L0_tok_B_ri, L0_attn_W_attn, L0_attn_b_attn, L0_attn_W_o, L0_attn_b_o, L0_ffn_router_w, L0_ffn_router_b, L0_ffn_sw1, L0_ffn_sb1, L0_ffn_sw2, L0_ffn_sb2, L0_ffn_rw1, L0_ffn_rb1, L0_ffn_rw2, L0_ffn_rb2):
    import jax
    import jax.numpy as jnp

    def _L0_tok_ref(log_dt, inv_A_real, A_imag, B_ri, C_ri, L):
        import jax, jax.numpy as jnp
        import numpy as np
        import math
        H = 256
        N = 64
        CH = 1
        SEQ_L = 256
        dt = jnp.exp(log_dt)
        A = -jnp.exp(inv_A_real) + 1j * A_imag
        B = B_ri[..., 0] + 1j * B_ri[..., 1]
        C = C_ri[..., 0] + 1j * C_ri[..., 1]
        dtA = A * dt[:, None]
        dA = (1.0 + dtA / 2) / (1.0 - dtA / 2)
        C_term = C * B[None]
        log_dA = jnp.log(dA)
        V = jnp.exp(log_dA[:, :, None] * jnp.arange(L))
        K = 2.0 * jnp.einsum('chn,hnl->chl', C_term, V).real
        return K.astype(jnp.float32)

    def _L0_attn_ref(x, W_attn, b_attn, W_o, b_o):
        import jax, jax.numpy as jnp
        import numpy as np
        B, T, C = (4, 512, 256)
        NH = 16
        HS = C // NH

        def _rope_tables(seq_len, dim):
            inv_freq = 1.0 / 1000.0 ** (jnp.arange(0, dim, 2, dtype=jnp.float32) / dim)
            t = jnp.arange(seq_len, dtype=jnp.float32)[:, None] * inv_freq[None, :]
            return (jnp.sin(t), jnp.cos(t))

        def _apply_rope(q, k, sin, cos):
            qe, qo = (q[..., ::2], q[..., 1::2])
            ke, ko = (k[..., ::2], k[..., 1::2])
            q_rot = jnp.concatenate([qe * cos - qo * sin, qo * cos + qe * sin], axis=-1)
            k_rot = jnp.concatenate([ke * cos - ko * sin, ko * cos + ke * sin], axis=-1)
            return (q_rot, k_rot)
        Bx, Tx, Cx = x.shape
        qkv = x @ W_attn.T + b_attn
        q, k, v = jnp.split(qkv, 3, axis=2)

        def to_heads(t):
            return t.reshape(Bx, Tx, NH, HS).transpose(0, 2, 1, 3)
        q, k, v = (to_heads(q), to_heads(k), to_heads(v))
        sin, cos = _rope_tables(Tx, HS)
        q, k = _apply_rope(q, k, sin, cos)
        scores = jnp.einsum('bhqd,bhkd->bhqk', q, k) / jnp.sqrt(jnp.float32(HS))
        causal = jnp.tril(jnp.ones((Tx, Tx), dtype=bool))
        scores = jnp.where(causal, scores, -jnp.inf)
        w = jax.nn.softmax(scores, axis=-1)
        y = jnp.einsum('bhqk,bhkd->bhqd', w, v)
        y = y.transpose(0, 2, 1, 3).reshape(Bx, Tx, Cx)
        return y @ W_o.T + b_o

    def _L0_ffn_ref(hidden, router_w, router_b, sw1, sb1, sw2, sb2, rw1, rb1, rw2, rb2):
        import jax, jax.numpy as jnp
        import numpy as np
        D = 256
        H = 512
        E = 8
        TOP_K = 2
        N_SHARED = 1
        B, S = (2, 256)
        b, s, d = hidden.shape
        T = b * s
        flat = hidden.reshape(T, d)
        router_logits = flat @ router_w + router_b
        router_probs = jax.nn.softmax(router_logits, axis=-1)
        topk_probs, topk_idx = jax.lax.top_k(router_probs, TOP_K)
        weights = jnp.zeros_like(router_probs).at[jnp.arange(T)[:, None], topk_idx].add(topk_probs)
        sh = jax.nn.gelu(flat @ sw1 + sb1, approximate=False)
        shared_out = (sh @ sw2 + sb2) / N_SHARED
        h1 = jax.nn.gelu(jnp.einsum('td,edh->teh', flat, rw1) + rb1[None], approximate=False)
        expert_out = jnp.einsum('teh,ehd->ted', h1, rw2) + rb2[None]
        mixed = jnp.einsum('ted,te->td', expert_out, weights)
        return (shared_out + mixed).reshape(b, s, d)
    h = _L0_tok_ref(L0_tok_log_dt, L0_tok_inv_A_real, L0_tok_A_imag, L0_tok_B_ri, x, 256)
    h = h + _L0_attn_ref(_layernorm(h, axis=-1), L0_attn_W_attn, L0_attn_b_attn, L0_attn_W_o, L0_attn_b_o)
    h = h + _L0_ffn_ref(_layernorm(h, axis=-1), L0_ffn_router_w, L0_ffn_router_b, L0_ffn_sw1, L0_ffn_sb1, L0_ffn_sw2, L0_ffn_sb2, L0_ffn_rw1, L0_ffn_rb1, L0_ffn_rw2, L0_ffn_rb2)
    return h

_drawn_inputs = setup_inputs


def setup_inputs(seed=0):
    import zlib

    import numpy as np

    out = dict(_drawn_inputs(seed))
    spreads = {'L0_ffn_router_b': (0.0, 0.8),
     'L0_ffn_sb1': (0.0, 0.8),
     'L0_ffn_sb2': (0.0, 0.319),
     'L0_ffn_rb1': (0.0, 0.8),
     'L0_ffn_rb2': (0.0, 0.8)}
    factors = {'L0_attn_W_attn': 4.452,
     'L0_attn_b_attn': 8.0,
     'L0_attn_W_o': 4.097,
     'L0_attn_b_o': 6.751,
     'L0_ffn_router_w': 8.0,
     'L0_ffn_sw1': 3.135,
     'L0_ffn_sw2': 2.92,
     'L0_ffn_rw1': 8.0,
     'L0_ffn_rw2': 8.0}
    for name, (base, spread) in spreads.items():
        noise = np.random.default_rng([zlib.crc32(name.encode()), seed]).standard_normal(out[name].shape)
        drawn = base * np.exp(spread * noise) if base else spread * noise
        out[name] = jnp.asarray(drawn.astype(out[name].dtype))
    for name, factor in factors.items():
        out[name] = (out[name] * factor).astype(out[name].dtype)
    return out
```

```python
import math
from contextlib import ExitStack

import concourse.bass as bass
from concourse import mybir

F32 = mybir.dt.float32
F32R = mybir.dt.float32r
BF16 = mybir.dt.bfloat16
I32 = mybir.dt.int32
ALU = mybir.AluOpType
ACT = mybir.ActivationFunctionType
AX_X = mybir.AxisListType.X

P = 128
NB = 8
SEQ = 256
DM = 256
NS = 64
L0 = 32
L1 = DM // L0
CHUNK = 32
NCHUNK = SEQ // CHUNK
QUADS = CHUNK // 4
AHEAD = 2

LOG2E = 1.0 / math.log(2.0)
LN2_HI = 355.0 / 512.0
LN2_LO = math.log(2.0) - LN2_HI


def s4d_phase(nc, x_t, a_real_t, a_imag_t, b_t, log_dt, ident, h_dram):
    HALF = P // 2
    with ExitStack() as ctx:
        def sb(name, shape, dt=F32):
            return ctx.enter_context(nc.sbuf_tensor(name, shape, dt))

        def sem(name):
            return ctx.enter_context(nc.semaphore(name))

        idn = sb("s4_ident", [P, P])
        c_re = sb("s4_c_re", [P, SEQ, NB])
        c_im = sb("s4_c_im", [P, SEQ, NB])
        logs = sb("s4_logs", [P, 2, SEQ])
        aimag = sb("s4_aimag", [P, SEQ])
        ex = [sb(f"s4_ex{i}", [P, 2, SEQ]) for i in range(3)]
        ex_int = sb("s4_ex_int", [P, 2, SEQ], I32)
        tmp = [sb(f"s4_tmp{i}", [P, SEQ]) for i in range(4)]
        b_r = sb("s4_b_r", [P, SEQ])
        b_i = sb("s4_b_i", [P, SEQ])
        zr = sb("s4_zr", [P, 8, SEQ])
        zi = sb("s4_zi", [P, 8, SEQ])
        u = sb("s4_u", [P, SEQ, 16])
        w = sb("s4_w", [P, SEQ, 16])
        p1 = sb("s4_p1", [P, SEQ, L1])
        p2 = sb("s4_p2", [P, SEQ, L1])
        t_dve = [sb(f"s4_tdve{i}", [P, SEQ * 8]) for i in range(2)]
        t_pool = [sb(f"s4_tpool{i}", [P, SEQ * 4]) for i in range(2)]
        t_fin = [sb(f"s4_tfin{i}", [P, CHUNK, 16]) for i in range(2)]
        zc = [sb(f"s4_zc{i}", [P, CHUNK, L0]) for i in range(2)]
        a_re = [sb(f"s4_a_re{i}", [P, CHUNK, NB, L1]) for i in range(2)]
        a_im = [sb(f"s4_a_im{i}", [P, CHUNK, NB, L1]) for i in range(2)]
        k_sb = sb("s4_k", [P, NB // 2, L1, 2, SEQ // 4])
        h_sb = sb("s4_h", [P, NB // 2, 4, DM])
        ps = [ctx.enter_context(nc.psum_tensor(f"s4_ps{i}", [P, 512], F32)) for i in range(8)]

        par_in = sem("s4_par_in")
        x_in = sem("s4_x_in")
        dve = sem("s4_dve")
        pool = sem("s4_pool")
        squares = sem("s4_squares")
        b_ready = sem("s4_b_ready")
        u_done = sem("s4_u_done")
        z_low = sem("s4_z_low")
        z_high = sem("s4_z_high")
        are_done = sem("s4_are_done")
        aim_done = sem("s4_aim_done")
        mm_done = sem("s4_mm_done")
        k_done = sem("s4_k_done")
        tr_done = sem("s4_tr_done")
        h_v = sem("s4_h_v")
        h_a = sem("s4_h_a")
        h_out = sem("s4_h_out")

        block = ctx.enter_context(nc.Block())

        @block.sync
        def _(sp):
            sp.dma_start(logs[:, 0], log_dt.unsqueeze(0).to_broadcast([P, SEQ])).then_inc(par_in, 16)
            for d in range(2):
                rows = slice(HALF * d, HALF * (d + 1))
                sp.dma_start(logs[rows, 1], a_real_t).then_inc(par_in, 16)
                sp.dma_start(aimag[rows, :], a_imag_t).then_inc(par_in, 16)
                sp.dma_start(b_r[rows, :], b_t[:, d]).then_inc(par_in, 16)
                sp.dma_start(b_i[rows, :], b_t[:, 1 - d]).then_inc(par_in, 16)
            sp.dma_start(idn[:], ident).then_inc(par_in, 16)
            for d in range(2):
                rows = slice(HALF * d, HALF * (d + 1))
                sp.dma_start(c_re[rows], x_t[:, 0]).then_inc(x_in, 16)
                sp.dma_start(c_im[rows], x_t[:, 1]).then_inc(x_in, 16)
            for bp in range(NB // 2):
                sp.wait_ge(h_v, bp + 1)
                sp.wait_ge(h_a, bp + 1)
                for s in range(2):
                    sp.dma_start(
                        h_dram[2 * bp + s].rearrange("(j q) l -> q j l", j=4),
                        h_sb[HALF * s:HALF * (s + 1), bp],
                    ).then_inc(h_out, 16)
            sp.wait_ge(h_out, 16 * NB)

        @block.scalar
        def _(act):
            act.sem_inc(k_done, 2 * AHEAD)
            act.wait_ge(u_done, 1)
            with act.Fori(0, NCHUNK // 2) as i:
                for half in range(2):
                    c = i * 2 + half
                    act.wait_ge(mm_done, c + 1)
                    act.copy(zc[half][:, :, 0:16], u[:, bass.ds(c * CHUNK, CHUNK), :]).then_inc(z_low, 1)
                    act.wait_ge(mm_done, c + 1 + AHEAD)
                    src = ps[half][:].rearrange("p (q b s l) -> p q b s l", q=QUADS, s=2, l=L1)
                    for s in range(2):
                        dst = k_sb[:, :, :, s, bass.ds(c * QUADS, QUADS)].rearrange("p b l q -> p q b l")
                        act.copy(dst, src[:, :, :, s, :]).then_inc(k_done, 1)
            for n in range(1, 8, 2):
                act.wait_ge(tr_done, n + 1)
                bp, g = n // 2, n % 2
                act.copy(h_sb[:, bp, :, g * 128:(g + 1) * 128].rearrange("p j (g l) -> p g j l", g=4),
                         ps[n][:].rearrange("p (g j l) -> p g j l", g=4, j=4)).then_inc(h_a, 1)

        @block.vector
        def _(v):
            count = [0]

            def link(ins):
                count[0] += 1
                ins.then_inc(dve, 1)
                v.wait_ge(dve, count[0])

            hdt, xr, y, t = tmp
            one_x, n2 = t_dve[0][:, 0:SEQ], t_dve[0][:, SEQ:2 * SEQ]
            v.memset(u[0:HALF, :, 0:1], 1.0)
            v.memset(u[HALF:P, :, 0:1], 0.0)
            v.memset(w[0:HALF, :, 0:1], 0.0)
            link(v.memset(w[HALF:P, :, 0:1], 1.0))
            v.wait_ge(par_in, 16 * 10)
            x_, r_, e_ = ex
            link(v.tensor_scalar(x_[:], logs[:], -87.0, 88.0, ALU.max, ALU.min))
            link(v.tensor_scalar(ex_int[:], x_[:], LOG2E, None, ALU.mult))
            link(v.tensor_copy(e_[:], ex_int[:]))
            link(v.scalar_tensor_tensor(out=r_[:], in0=e_[:], scalar=-LN2_HI, in1=x_[:],
                                        op0=ALU.mult, op1=ALU.add))
            link(v.scalar_tensor_tensor(out=r_[:], in0=e_[:], scalar=-LN2_LO, in1=r_[:],
                                        op0=ALU.mult, op1=ALU.add))
            v.tensor_scalar(ex_int[:], e_[:], 127.0, float(1 << 23), ALU.add, ALU.mult)
            link(v.tensor_scalar(x_[:], r_[:], 1.0 / math.factorial(7), None, ALU.mult))
            for k in range(6, 0, -1):
                link(v.scalar_tensor_tensor(out=x_[:], in0=x_[:], scalar=1.0 / math.factorial(k), in1=r_[:],
                                            op0=ALU.add, op1=ALU.mult))
            link(v.scalar_tensor_tensor(out=x_[:], in0=x_[:], scalar=1.0, in1=ex_int[:].bitcast(F32),
                                        op0=ALU.add, op1=ALU.mult))
            dt_, areal = x_[:, 0], x_[:, 1]
            v.tensor_scalar(p1[:, :, 0], b_r[:], 2.0, None, ALU.mult)
            v.tensor_scalar(p2[0:HALF, :, 0], b_i[0:HALF, :], -2.0, None, ALU.mult)
            v.tensor_scalar(p2[HALF:P, :, 0], b_i[HALF:P, :], 2.0, None, ALU.mult).then_inc(b_ready, 1)
            link(v.tensor_scalar(hdt[:], dt_, 0.5, None, ALU.mult))
            v.tensor_tensor(y[:], aimag[:], hdt[:], ALU.mult)
            link(v.scalar_tensor_tensor(out=xr[:], in0=areal, scalar=-1.0, in1=hdt[:],
                                        op0=ALU.mult, op1=ALU.mult))
            v.tensor_scalar(one_x, xr[:], -1.0, 1.0, ALU.mult, ALU.add)
            v.tensor_tensor(t[:], y[:], y[:], ALU.mult)
            link(v.tensor_tensor(n2, xr[:], xr[:], ALU.mult))
            link(v.tensor_tensor(one_x, one_x, one_x, ALU.mult))
            v.tensor_tensor(n2, n2, t[:], ALU.add)
            link(v.tensor_tensor(one_x, one_x, t[:], ALU.add))
            v.tensor_scalar(n2, n2, -1.0, 1.0, ALU.mult, ALU.add)
            link(v.reciprocal(one_x, one_x))
            v.tensor_tensor(zr[:, 0], n2, one_x, ALU.mult)
            link(v.scalar_tensor_tensor(out=zi[:, 0], in0=y[:], scalar=2.0, in1=one_x,
                                        op0=ALU.mult, op1=ALU.mult))
            for k in range(7):
                v.tensor_tensor(xr[:], zr[:, k], zr[:, k], ALU.mult)
                v.tensor_tensor(y[:], zi[:, k], zi[:, k], ALU.mult)
                link(v.scalar_tensor_tensor(out=zi[:, k + 1], in0=zr[:, k], scalar=2.0, in1=zi[:, k],
                                            op0=ALU.mult, op1=ALU.mult))
                ins = v.tensor_tensor(zr[:, k + 1], xr[:], y[:], ALU.subtract)
                link(ins)
            v.sem_inc(squares, 1)
            for k in range(4):
                m = 1 << k
                ta = t_dve[0][:, 0:SEQ * m].rearrange("p (h l) -> p h l", l=m)
                tb = t_dve[1][:, 0:SEQ * m].rearrange("p (h l) -> p h l", l=m)
                zr_m = zr[:, k].unsqueeze(2).to_broadcast([P, SEQ, m])
                zi_m = zi[:, k].unsqueeze(2).to_broadcast([P, SEQ, m])
                v.tensor_tensor(ta, u[:, :, 0:m], zr_m, ALU.mult)
                link(v.tensor_tensor(tb, w[:, :, 0:m], zi_m, ALU.mult))
                link(v.tensor_tensor(u[:, :, m:2 * m], ta, tb, ALU.subtract))
                v.tensor_tensor(ta, u[:, :, 0:m], zi_m, ALU.mult)
                link(v.tensor_tensor(tb, w[:, :, 0:m], zr_m, ALU.mult))
                link(v.tensor_tensor(w[:, :, m:2 * m], ta, tb, ALU.add))
            v.sem_inc(u_done, 1)
            v.wait_ge(x_in, 64)
            v.wait_ge(pool, 18)
            start = count[0]
            v.sem_inc(z_high, 1)
            with v.Fori(0, NCHUNK // 2) as i:
                for half in range(2):
                    c = i * 2 + half
                    hs = bass.ds(c * CHUNK, CHUNK)
                    zr16 = zr[:, 4, hs].unsqueeze(2).to_broadcast([P, CHUNK, 16])
                    zi16 = zi[:, 4, hs].unsqueeze(2).to_broadcast([P, CHUNK, 16])
                    v.wait_ge(z_high, c + 1)
                    v.tensor_tensor(t_fin[0][:], u[:, hs, :], zr16, ALU.mult)
                    v.tensor_tensor(t_fin[1][:], w[:, hs, :], zi16, ALU.mult).then_inc(dve, 1)
                    v.wait_ge(mm_done, c + 1)
                    v.wait_ge(dve, c + start + 1)
                    v.tensor_tensor(zc[half][:, :, 16:32], t_fin[0][:], t_fin[1][:],
                                    ALU.subtract).then_inc(z_high, 1)
                    v.tensor_tensor(
                        a_re[half][:],
                        c_re[:, hs, :].unsqueeze(3).to_broadcast([P, CHUNK, NB, L1]),
                        p1[:, hs, :].unsqueeze(2).to_broadcast([P, CHUNK, NB, L1]),
                        ALU.mult).then_inc(are_done, 1)
            for n in range(0, 8, 2):
                v.wait_ge(tr_done, n + 1)
                bp, g = n // 2, n % 2
                v.tensor_copy(h_sb[:, bp, :, g * 128:(g + 1) * 128].rearrange("p j (g l) -> p g j l", g=4),
                              ps[n][:].rearrange("p (g j l) -> p g j l", g=4, j=4)).then_inc(h_v, 1)

        @block.gpsimd
        def _(g):
            count = [0]

            def link(ins):
                count[0] += 1
                ins.then_inc(pool, 1)
                g.wait_ge(pool, count[0])

            g.wait_ge(b_ready, 1)
            g.wait_ge(squares, 1)
            for k in range(3):
                m = 1 << k
                ta = t_pool[0][:, 0:SEQ * m].rearrange("p (h l) -> p h l", l=m)
                tb = t_pool[1][:, 0:SEQ * m].rearrange("p (h l) -> p h l", l=m)
                zr_m = zr[:, k + 5].unsqueeze(2).to_broadcast([P, SEQ, m])
                zi_m = zi[:, k + 5].unsqueeze(2).to_broadcast([P, SEQ, m])
                link(g.tensor_tensor(ta, p1[:, :, 0:m], zr_m, ALU.mult))
                link(g.tensor_tensor(tb, p2[:, :, 0:m], zi_m, ALU.mult))
                link(g.tensor_tensor(p1[:, :, m:2 * m], ta, tb, ALU.add))
                link(g.tensor_tensor(ta, p2[:, :, 0:m], zr_m, ALU.mult))
                link(g.tensor_tensor(tb, p1[:, :, 0:m], zi_m, ALU.mult))
                link(g.tensor_tensor(p2[:, :, m:2 * m], ta, tb, ALU.subtract))
            g.wait_ge(x_in, 64)
            with g.Fori(0, NCHUNK // 2) as i:
                for half in range(2):
                    c = i * 2 + half
                    hs = bass.ds(c * CHUNK, CHUNK)
                    g.wait_ge(mm_done, c + 1)
                    g.tensor_tensor(
                        a_im[half][:],
                        c_im[:, hs, :].unsqueeze(3).to_broadcast([P, CHUNK, NB, L1]),
                        p2[:, hs, :].unsqueeze(2).to_broadcast([P, CHUNK, NB, L1]),
                        ALU.mult).then_inc(aim_done, 1)

        @block.tensor
        def _(pe):
            pe.sem_inc(mm_done, AHEAD)
            with pe.Fori(0, NCHUNK // 2) as i:
                for half in range(2):
                    c = i * 2 + half
                    pe.wait_ge(z_low, c + 1)
                    pe.wait_ge(z_high, c + 2)
                    pe.wait_ge(are_done, c + 1)
                    pe.wait_ge(aim_done, c + 1)
                    pe.wait_ge(k_done, 2 * c + 2)
                    for q in range(QUADS):
                        for a in (a_re, a_im):
                            for j in range(4):
                                last = pe.matmul(ps[half][32 * j:32 * j + 32, 64 * q:64 * q + 64],
                                                 zc[half][:, 4 * q + j, :],
                                                 a[half][:, 4 * q + j].rearrange("p b l -> p (b l)"),
                                                 start=a is a_re, stop=a is a_im)
                    last.then_inc(mm_done, 1)
            pe.wait_ge(k_done, 2 * (NCHUNK + AHEAD))
            for n in range(8):
                bp, g = n // 2, n % 2
                for k in range(4):
                    last = pe.transpose(ps[n][:, 128 * k:128 * k + 128],
                                        k_sb[:, bp, 4 * g + k].rearrange("p s q -> p (s q)"), idn[:])
                last.then_inc(tr_done, 1)


NH = 16
HS = DM // NH
NT = SEQ // P
TILES = NB * NT
KC = DM // P
NG = NH // 4
EPS = 1e-5
GW = 4 * SEQ


def attention_phase(nc, h_dram, w_qkv, w_o, b_qkv, b_o, rope, ident, ident_b, mask_b, select_b, h_all):
    with ExitStack() as ctx:
        def sb(name, shape, dt=F32):
            return ctx.enter_context(nc.sbuf_tensor(name, shape, dt))

        def sem(name):
            return ctx.enter_context(nc.semaphore(name))

        idn = sb("at_ident", [P, P])
        idb = sb("at_ident_b", [P, P], BF16)
        maskb = sb("at_mask_b", [P, 4 * P], BF16)
        selb = sb("at_select_b", [P, NH, P], BF16)
        cs = sb("at_rope", [P, NT, 2, HS])
        bq = sb("at_b_qkv", [P, 3 * DM])
        bo = sb("at_b_o", [P, DM])
        w_in = sb("at_w_in", [P, KC, 4 * DM])
        w_hi = sb("at_w_hi", [P, KC, 4 * DM], F32R)
        w_lo = sb("at_w_lo", [P, KC, 4 * DM], F32R)
        xn = sb("at_xn", [P, NT, DM])
        stats = sb("at_stats", [P, TILES, 6])
        mv = sb("at_mv", [P, TILES, 2])
        rstd = sb("at_rstd", [P, TILES])
        vare = sb("at_vare", [P, TILES])
        mhalf = sb("at_mhalf", [P, TILES])
        x_hi = sb("at_x_hi", [P, KC, SEQ], F32R)
        x_lo = sb("at_x_lo", [P, KC, SEQ], F32R)
        qk = sb("at_qk", [P, NT, 2 * NH, HS])
        m1 = sb("at_m1", [P, NT, 2 * NH, HS])
        m2 = sb("at_m2", [P, NT, 2 * NH, HS])
        vx = sb("at_v", [P, NT, NH, 32])
        st_q = sb("at_st_q", [P, NT, NH, 2, HS])
        st_ka = sb("at_st_ka", [P, NT, NH, 2, HS])
        st_kb = sb("at_st_kb", [P, NT, NH, 2, HS])
        qc = sb("at_qc", [P, NG, SEQ], F32R)
        ka = sb("at_ka", [P, NG, SEQ], F32R)
        kb = sb("at_kb", [P, NG, SEQ], F32R)
        qm = sb("at_qm", [P, NG, 4, SEQ], F32R)
        km = sb("at_km", [P, NG, 4, SEQ], F32R)
        cm = sb("at_cm", [P, NT, NH])
        cb = sb("at_cb", [P, NT, 2, NH], BF16)
        cz = sb("at_cz", [P, SEQ], BF16)
        pt = [sb(f"at_pt{i}", [P, 3 * 512]) for i in range(2)]
        ot = sb("at_ot", [P, NG, SEQ])
        rc = sb("at_rc", [P, NT, NH])
        yv = sb("at_y", [P, NT, DM])
        y_hi = sb("at_y_hi", [P, KC, SEQ], F32R)
        y_lo = sb("at_y_lo", [P, KC, SEQ], F32R)
        ps = ctx.enter_context(nc.psum_tensor("at_ps", [P, 8, 512], F32))

        const_in = sem("at_const_in")
        h_in = sem("at_h_in")
        w_split = sem("at_w_split")
        prep = sem("at_prep")
        g_chain = sem("at_g_chain")
        dve = sem("at_dve")
        mean_var = sem("at_mean_var")
        rstd_done = sem("at_rstd_done")
        xn_done = sem("at_xn_done")
        xt_ps = sem("at_xt_ps")
        xhi_s = sem("at_xhi_s")
        xlo_s = sem("at_xlo_s")
        qkv_ps = sem("at_qkv_ps")
        qkv_sb = sem("at_qkv_sb")
        rot1 = sem("at_rot1")
        rot2 = sem("at_rot2")
        rot = sem("at_rot")
        st_hi = sem("at_st_hi")
        st_lo = sem("at_st_lo")
        hd_ps = sem("at_hd_ps")
        hd_a = sem("at_hd_a")
        hd_v = sem("at_hd_v")
        qm_in = sem("at_qm_in")
        km_in = sem("at_km_in")
        mx_ps = sem("at_mx_ps")
        mx_v = sem("at_mx_v")
        cb_v = sem("at_cb_v")
        cz_ps = sem("at_cz_ps")
        cz_a = sem("at_cz_a")
        sc_ps = sem("at_sc_ps")
        ex_a = sem("at_ex_a")
        msk_g = sem("at_msk_g")
        pv_ps = sem("at_pv_ps")
        ot_a = sem("at_ot_a")
        ot_ps = sem("at_ot_ps")
        y_v = sem("at_y_v")
        yt_ps = sem("at_yt_ps")
        yhi_s = sem("at_yhi_s")
        ylo_s = sem("at_ylo_s")
        o_ps = sem("at_o_ps")
        o_b = sem("at_o_b")
        o_v = sem("at_o_v")

        block = ctx.enter_context(nc.Block())

        @block.sync
        def _(sp):
            for b in range(NB):
                sp.dma_start(h_all[:, 2 * b:2 * b + 2, :],
                             h_dram[b].rearrange("(t p) l -> p t l", p=P)).then_inc(h_in, 16)
            for dst, src in ((idn[:], ident), (idb[:], ident_b), (maskb[:], mask_b), (cs[:], rope),
                             (selb[:], select_b),
                             (w_in[:, :, 0:3 * DM], w_qkv.rearrange("(k p) n -> p k n", p=P)),
                             (w_in[:, :, 3 * DM:], w_o.rearrange("(k p) n -> p k n", p=P)),
                             (bq[:], b_qkv.unsqueeze(0).to_broadcast([P, 3 * DM])),
                             (bo[:], b_o.unsqueeze(0).to_broadcast([P, DM]))):
                sp.dma_start(dst, src).then_inc(const_in, 16)
            sp.wait_ge(prep, 6)
            with sp.Fori(0, NB) as b:
                sp.wait_ge(hd_a, 3 * b + 3)
                sp.wait_ge(hd_v, 3 * b + 3)
                for j in range(4):
                    rows = slice(32 * j, 32 * j + 32)
                    sp.dma_start(km[rows, :, j, :].bitcast(F32), ka[rows].bitcast(F32)).then_inc(km_in, 16)
                for j in range(4):
                    rows = slice(32 * j, 32 * j + 32)
                    sp.dma_start(qm[rows, :, j, :].bitcast(F32), qc[rows].bitcast(F32)).then_inc(qm_in, 16)

        @block.gpsimd
        def _(g):
            g.memset(mhalf[:], -0.5).then_inc(prep, 1)
            g.memset(cz[:], 0.0).then_inc(prep, 1)
            g.memset(vx[:, :, :, HS:32], 1.0).then_inc(prep, 1)
            g.memset(qm[:].bitcast(F32), 0.0).then_inc(prep, 1)
            g.memset(km[:].bitcast(F32), 0.0).then_inc(prep, 1)
            g.memset(st_kb[:, :, :, 1, :], 0.0).then_inc(prep, 1)
            g.wait_ge(mean_var, 1)
            g.wait_ge(prep, 1)
            g.tensor_tensor(rstd[:], vare[:], mhalf[:], ALU.pow).then_inc(rstd_done, 1)
            g.wait_ge(const_in, 16 * 9)
            with g.Fori(0, NB) as b:
                for t in range(NT):
                    g.wait_ge(qkv_sb, b * 4 + 2 * t + 1)
                    sgn = cs[:, t, 1, :].rearrange("p (i e) -> p i e", e=2)
                    src = qk[:, t].rearrange("p h (i e) -> p h i e", e=2)
                    dst = m2[:, t].rearrange("p h (i e) -> p h i e", e=2)
                    for e in range(2):
                        g.tensor_tensor(dst[:, :, :, e], src[:, :, :, 1 - e],
                                        sgn[:, :, e].unsqueeze(1).to_broadcast([P, 2 * NH, HS // 2]),
                                        ALU.mult).then_inc(rot2, 1)
                for n in range(NG):
                    g.wait_ge(ex_a, b * NG + n + 1)
                    g.sem_inc(g_chain, 1)
                    for ofs, width in ((0, SEQ), (GW, P)):
                        d = pt[n % 2][:, ofs:ofs + 4 * width].rearrange("p (h q) -> p h q", h=4)[:, :, 0:P]
                        g.affine_select(out=d, in_=d, compare_op=ALU.is_ge, fill=0.0, base=0,
                                        pattern=[[0, 4], [1, P]], channel_multiplier=-1).then_inc(msk_g, 1)

        @block.scalar
        def _(act):
            act.wait_ge(const_in, 16 * 9)
            act.copy(w_hi[:], w_in[:]).then_inc(w_split, 1)
            with act.Fori(0, NB) as b:
                act.wait_ge(xt_ps, b + 1)
                act.copy(x_hi[:].rearrange("p k t -> p (k t)"), ps[:, 7, :]).then_inc(xhi_s, 1)
                for t in range(NT):
                    act.wait_ge(rot, b * NT + t + 1)
                    q, k = m1[:, t, 0:NH, :], m1[:, t, NH:, :]
                    act.copy(st_q[:, t, :, 0, :].bitcast(F32R), q).then_inc(st_hi, 1)
                    act.copy(st_ka[:, t].bitcast(F32R), k.unsqueeze(2).to_broadcast([P, NH, 2, HS])).then_inc(st_hi, 1)
                for t in range(NT):
                    act.wait_ge(hd_ps, b * NT + t + 1)
                    act.copy(ka[:, :, t * P:(t + 1) * P], ps[:, 3 * t + 1].rearrange("p (g t) -> p g t", g=NG)).then_inc(hd_a, 1)
                    if t == 0:
                        act.copy(kb[:, :, t * P:(t + 1) * P], ps[:, 3 * t + 2].rearrange("p (g t) -> p g t", g=NG)).then_inc(hd_a, 1)
                act.wait_ge(cz_ps, b + 1)
                act.copy(cz[0:32, :], ps[0:32, 7, 0:P].bitcast(BF16)).then_inc(cz_a, 1)
                for n in range(NG):
                    act.wait_ge(sc_ps, b * NG + n + 1)
                    if n >= 2:
                        act.wait_ge(pv_ps, b * NG + n - 1)
                    act.activation(pt[n % 2][:], ps[:, 3 * (n % 2):3 * (n % 2) + 3, :].rearrange("p c x -> p (c x)"),
                                   ACT.Exp, scale=1.0 / math.sqrt(HS)).then_inc(ex_a, 1)
                    if n >= 1:
                        act.wait_ge(pv_ps, b * NG + n)
                        act.copy(ot[:, n - 1, :], ps[:, 6 + (n - 1) % 2, 0:SEQ]).then_inc(ot_a, 1)
                act.wait_ge(pv_ps, b * NG + NG)
                act.copy(ot[:, NG - 1, :], ps[:, 6 + (NG - 1) % 2, 0:SEQ]).then_inc(ot_a, 1)
                act.wait_ge(yt_ps, b + 1)
                act.copy(y_hi[:].rearrange("p k t -> p (k t)"), ps[:, 7, :]).then_inc(yhi_s, 1)

        @block.vector
        def _(v):
            count = [0]

            def link(ins):
                count[0] += 1
                ins.then_inc(dve, 1)
                v.wait_ge(dve, count[0])

            for b in range(NB):
                v.wait_ge(h_in, 16 * NB)
                for t in range(NT):
                    ins = v.bn_stats(stats[:, 2 * b + t, :], h_all[:, 2 * b + t, :])
            link(ins)
            for n in range(TILES):
                ins = v.bn_aggr(mv[:, n, :], stats[:, n, :])
            link(ins)
            v.tensor_scalar(vare[:], mv[:, :, 1], EPS, None, ALU.add).then_inc(mean_var, 1)
            v.wait_ge(const_in, 16 * 9)
            v.wait_ge(w_split, 1)
            v.tensor_tensor(w_lo[:], w_in[:], w_hi[:].bitcast(F32), ALU.subtract).then_inc(w_split, 1)
            v.wait_ge(rstd_done, 1)
            v.wait_ge(prep, 6)
            with v.Fori(0, NB) as b:
                for t in range(NT):
                    n = b * NT + t
                    ht = h_all[:, bass.ds(n, 1), :].rearrange("p o d -> p (o d)")
                    v.tensor_scalar(xn[:, t, :], ht, mv[:, bass.ds(n, 1), 0:1].rearrange("p o d -> p (o d)"),
                                    rstd[:, bass.ds(n, 1)], ALU.subtract, ALU.mult).then_inc(xn_done, 1)
                v.wait_ge(xhi_s, b + 1)
                v.tensor_tensor(x_lo[:].rearrange("p k t -> p (k t)"), ps[:, 7, :],
                                x_hi[:].rearrange("p k t -> p (k t)").bitcast(F32), ALU.subtract).then_inc(xlo_s, 1)
                for t in range(NT):
                    v.wait_ge(qkv_ps, b * NT + t + 1)
                    v.tensor_tensor(qk[:, t].rearrange("p h d -> p (h d)"), ps[:, 3 * t, :], bq[:, 0:2 * DM],
                                    ALU.add).then_inc(qkv_sb, 1)
                    v.tensor_tensor(vx[:, t, :, 0:HS], ps[:, 3 * t + 1, 0:DM].rearrange("p (h d) -> p h d", h=NH),
                                    bq[:, 2 * DM:].rearrange("p (h d) -> p h d", h=NH), ALU.add).then_inc(qkv_sb, 1)
                    v.wait_ge(qkv_sb, b * 4 + 2 * t + 1)
                    v.tensor_tensor(m1[:, t], qk[:, t], cs[:, t, 0, :].unsqueeze(1).to_broadcast([P, 2 * NH, HS]),
                                    ALU.mult).then_inc(rot1, 1)
                for t in range(NT):
                    v.wait_ge(rot1, b * NT + t + 1)
                    v.wait_ge(rot2, b * 4 + 2 * t + 2)
                    v.tensor_tensor(m1[:, t], m1[:, t], m2[:, t], ALU.add).then_inc(rot, 1)
                for t in range(NT):
                    v.wait_ge(st_hi, b * 4 + 2 * t + 2)
                    v.tensor_tensor(st_q[:, t, :, 1, :].bitcast(F32R), m1[:, t, 0:NH, :], st_q[:, t, :, 0, :],
                                    ALU.subtract).then_inc(st_lo, 1)
                    v.tensor_tensor(st_kb[:, t, :, 0, :].bitcast(F32R), m1[:, t, NH:, :], st_ka[:, t, :, 0, :],
                                    ALU.subtract).then_inc(st_lo, 1)
                for t in range(NT):
                    v.wait_ge(hd_ps, b * NT + t + 1)
                    v.tensor_copy(qc[:, :, t * P:(t + 1) * P], ps[:, 3 * t].rearrange("p (g t) -> p g t", g=NG)).then_inc(hd_v, 1)
                    if t == 1:
                        v.tensor_copy(kb[:, :, t * P:(t + 1) * P], ps[:, 3 * t + 2].rearrange("p (g t) -> p g t", g=NG)).then_inc(hd_v, 1)
                for n in range(NG):
                    v.wait_ge(mx_ps, b * NG + n + 1)
                    r = 3 * (n % 2)
                    v.tensor_reduce(cm[:, 0, 4 * n:4 * n + 4], ps[:, r].rearrange("p (h k) -> p h k", h=4), AX_X, ALU.max).then_inc(mx_v, 1)
                    v.tensor_reduce(cm[:, 1, 4 * n:4 * n + 4],
                                    ps[:, r + 1:r + 3].rearrange("p c (h k) -> p (c h) k", h=2), AX_X, ALU.max).then_inc(mx_v, 1)
                v.wait_ge(mx_v, b * 2 * NG + 2 * NG)
                v.tensor_scalar(cb[:, :, 0, :], cm[:], -1.0, None, ALU.mult).then_inc(cb_v, 1)
                v.wait_ge(cb_v, b * 2 + 1)
                v.scalar_tensor_tensor(out=cb[:, :, 1, :], in0=cm[:], scalar=-1.0, in1=cb[:, :, 0, :],
                                       op0=ALU.mult, op1=ALU.subtract).then_inc(cb_v, 1)
                v.wait_ge(ot_ps, b + 1)
                acc = ps[:, 0:NT].rearrange("p t (h d) -> p t h d", h=NH)
                v.reciprocal(rc[:], acc[:, :, :, HS]).then_inc(y_v, 1)
                v.wait_ge(y_v, b * 3 + 1)
                for t in range(NT):
                    v.tensor_tensor(yv[:, t].rearrange("p (h d) -> p h d", h=NH), acc[:, t, :, 0:HS],
                                    rc[:, t].unsqueeze(2).to_broadcast([P, NH, HS]), ALU.mult).then_inc(y_v, 1)
                v.wait_ge(yhi_s, b + 1)
                v.tensor_tensor(y_lo[:].rearrange("p k t -> p (k t)"), ps[:, 7, :],
                                y_hi[:].rearrange("p k t -> p (k t)").bitcast(F32), ALU.subtract).then_inc(ylo_s, 1)
                for t in range(NT):
                    v.wait_ge(o_ps, b * NT + t + 1)
                    v.tensor_tensor(yv[:, t], ps[:, 3 * t, 0:DM], bo[:], ALU.add).then_inc(o_b, 1)
                for t in range(NT):
                    v.wait_ge(o_b, b * NT + t + 1)
                    ht = h_all[:, bass.ds(b * NT + t, 1), :].rearrange("p o d -> p (o d)")
                    v.tensor_tensor(ht, yv[:, t], ht, ALU.add).then_inc(o_v, 1)

        @block.tensor
        def _(pe):
            def split_product(out, pairs):
                n = len(pairs)
                for i, (x, y) in enumerate(pairs):
                    last = pe.matmul(out, x, y, start=i == 0, stop=i == n - 1)
                return last

            pe.wait_ge(const_in, 16 * 9)
            pe.wait_ge(w_split, 2)
            pe.wait_ge(prep, 6)
            with pe.Fori(0, NB) as b:
                pe.wait_ge(xn_done, b * NT + NT)
                for k in range(KC):
                    for t in range(NT):
                        last = pe.transpose(ps[:, 7, k * SEQ + t * P:k * SEQ + (t + 1) * P],
                                            xn[:, t, k * P:(k + 1) * P], idn[:])
                last.then_inc(xt_ps, 1)
                pe.wait_ge(xhi_s, b + 1)
                pe.wait_ge(xlo_s, b + 1)
                for t in range(NT):
                    rows = slice(t * P, (t + 1) * P)
                    for out, cols in ((ps[:, 3 * t, :], slice(0, 2 * DM)), (ps[:, 3 * t + 1, 0:DM], slice(2 * DM, 3 * DM))):
                        last = split_product(out, [(x[:, k, rows], w[:, k, cols]) for k in range(KC)
                                                   for x, w in ((x_hi, w_hi), (x_hi, w_lo), (x_lo, w_hi))])
                    last.then_inc(qkv_ps, 1)
                for t in range(NT):
                    pe.wait_ge(st_hi, b * 4 + 2 * t + 2)
                    pe.wait_ge(st_lo, b * 4 + 2 * t + 2)
                    for i, st in enumerate((st_q, st_ka, st_kb)):
                        for n in range(NG):
                            last = pe.transpose(ps[:, 3 * t + i, n * P:(n + 1) * P],
                                                st[:, t, 4 * n:4 * n + 4].rearrange("p h c d -> p (h c d)"), idn[:])
                    last.then_inc(hd_ps, 1)
                for n in range(NG):
                    if n == 0:
                        pe.wait_ge(hd_a, b * 3 + 3)
                        pe.wait_ge(hd_v, b * 3 + 3)
                        pe.wait_ge(km_in, 64 * b + 64)
                    if n >= 2:
                        pe.wait_ge(mx_v, b * 2 * NG + 2 * n - 2)
                    r = 3 * (n % 2)
                    pe.matmul(ps[:, r, :], qc[:, n, 0:P], km[:, n, :, 0:P], start=True, stop=False)
                    pe.matmul(ps[:, r, :], idb[:], maskb[:], start=False, stop=True)
                    for c in range(2):
                        pe.matmul(ps[:, r + 1 + c, :], qc[:, n, P:SEQ], km[:, n, 2 * c:2 * c + 2, :], start=True, stop=False)
                        last = pe.matmul(ps[:, r + 1 + c, :].rearrange("p (h k) -> p h k", h=2)[:, :, P:SEQ], idb[:],
                                         maskb[:, 0:2 * P].rearrange("p (h k) -> p h k", h=2), start=False, stop=True)
                    last.then_inc(mx_ps, 1)
                pe.wait_ge(cb_v, b * 2 + 2)
                for t in range(NT):
                    last = pe.transpose(ps[0:32, 7, t * P // 2:(t + 1) * P // 2].bitcast(BF16),
                                        cb[:, t].rearrange("p c h -> p (c h)"), idb[:])
                last.then_inc(cz_ps, 1)
                pe.wait_ge(cz_a, b + 1)
                pe.wait_ge(qm_in, 64 * b + 64)
                for n in range(NG + 1):
                    if n < NG:
                        if n < 2:
                            pe.wait_ge(mx_v, b * 2 * NG + 2 * NG)
                        else:
                            pe.wait_ge(ex_a, b * NG + n - 1)
                        r = 3 * (n % 2)
                        for c in range(3):
                            out = ps[:, r + c, :]
                            keys = slice(0, P) if c < 2 else slice(P, SEQ)
                            x = qm[:, n, 2 * c:2 * c + 2, :] if c < 2 else qm[:, n, :, P:SEQ]
                            heads = (2 * c, 2 * c + 1) if c < 2 else range(4)
                            width = SEQ if c < 2 else P
                            for i, j in enumerate(heads):
                                pe.matmul(out[:, i * width:(i + 1) * width], selb[:, 4 * n + j, :],
                                          cz[:, SEQ - width:SEQ], start=i == 0, stop=False, skip_group_check=True)
                            pe.matmul(out, ka[:, n, keys], x, start=False, stop=False, skip_group_check=True)
                            last = pe.matmul(out, kb[:, n, keys], x, start=False, stop=True, skip_group_check=True)
                        last.then_inc(sc_ps, 1)
                    if n >= 1:
                        m = n - 1
                        pe.wait_ge(msk_g, b * 2 * NG + 2 * m + 2)
                        if m >= 2:
                            pe.wait_ge(ot_a, b * NG + m - 1)
                        for t in range(NT):
                            width = SEQ if t == 0 else P
                            for j in range(4):
                                ofs = t * GW + j * width
                                last = pe.matmul(ps[32 * j:32 * j + 32, 6 + m % 2, SEQ - width:SEQ],
                                                 vx[:, t, 4 * m + j, :], pt[m % 2][:, ofs:ofs + width],
                                                 start=t == 0, stop=t == 1, skip_group_check=True)
                        last.then_inc(pv_ps, 1)
                pe.wait_ge(ot_a, b * NG + NG)
                for t in range(NT):
                    for n in range(NG):
                        last = pe.transpose(ps[:, t, n * P:(n + 1) * P], ot[:, n, t * P:(t + 1) * P], idn[:])
                last.then_inc(ot_ps, 1)
                pe.wait_ge(y_v, b * 3 + 3)
                for k in range(KC):
                    for t in range(NT):
                        last = pe.transpose(ps[:, 7, k * SEQ + t * P:k * SEQ + (t + 1) * P],
                                            yv[:, t, k * P:(k + 1) * P], idn[:])
                last.then_inc(yt_ps, 1)
                pe.wait_ge(yhi_s, b + 1)
                pe.wait_ge(ylo_s, b + 1)
                for t in range(NT):
                    rows = slice(t * P, (t + 1) * P)
                    split_product(ps[:, 3 * t, 0:DM], [(x[:, k, rows], w[:, k, 3 * DM:]) for k in range(KC)
                                  for x, w in ((y_hi, w_hi), (y_hi, w_lo), (y_lo, w_hi))]).then_inc(o_ps, 1)


NE = 8
FF = 512
FC = FF // P
SLOT_TILES = (2 * NB * SEQ + NE * (P - 1)) // P
NSTEP = TILES + SLOT_TILES
TOK = NB * SEQ
BIG = 4.0
U32 = mybir.dt.uint32


def routing_phase(nc, h_all, h2_dram, slots_dram, router_w, router_b, ident, tri_b, rank8, tile_no,
                  w1_all, w2_all, w1, w2, pos_i, w_top, step_expert):
    with ExitStack() as ctx:
        def sb(name, shape, dt=F32):
            return ctx.enter_context(nc.sbuf_tensor(name, shape, dt))

        def sem(name):
            return ctx.enter_context(nc.semaphore(name))

        idn = sb("ro_ident", [P, P])
        tri = sb("ro_tri", [P, P], BF16)
        ones = sb("ro_ones", [P, P], BF16)
        rk = sb("ro_rank8", [P, NE])
        tno = sb("ro_tile_no", [P, SLOT_TILES])
        zero = sb("ro_zero", [P, DM])
        rw_in = sb("ro_rw_in", [P, KC, NE])
        rw_hi = sb("ro_rw_hi", [P, KC, NE], F32R)
        rw_lo = sb("ro_rw_lo", [P, KC, NE], F32R)
        rb = sb("ro_rb", [NE, 1])
        stats = sb("ro_stats", [P, TILES, 6])
        mv = sb("ro_mv", [P, TILES, 2])
        vare = sb("ro_vare", [P, TILES])
        rstd = sb("ro_rstd", [P, TILES])
        mhalf = sb("ro_mhalf", [P, TILES])
        xn = sb("ro_xn", [P, TILES, DM])
        x_hi = sb("ro_x_hi", [P, KC, 512], F32R)
        x_lo = sb("ro_x_lo", [P, KC, 512], F32R)
        lg_t = sb("ro_lg_t", [NE, 2, 512])
        S3 = [P, TILES, NE]
        pr, a3, b3, c3, oh1, oh2 = (sb(f"ro_m{i}", S3) for i in range(6))
        sel_b = sb("ro_sel_b", S3, BF16)
        s1 = sb("ro_s1", [P, TILES])
        s2 = sb("ro_s2", [P, TILES])
        e1, e2, e3 = (sb(f"ro_e{i}", [P, NE]) for i in range(3))
        ei = sb("ro_ei", [P, NE], I32)
        te = sb("ro_te", [P, SLOT_TILES, NE])
        tf = sb("ro_tf", [P, SLOT_TILES])
        pf = sb("ro_pf", [P, 2, TILES])
        wst = [sb(f"ro_wst{i}", [P, KC * FF]) for i in range(2)]
        ps = ctx.enter_context(nc.psum_tensor("ro_ps", [P, 8, 512], F32))

        const_in = sem("ro_const_in")
        w_in = [sem(f"ro_w_in{i}") for i in range(2)]
        w_hi_done = sem("ro_w_hi_done")
        w_lo_done = sem("ro_w_lo_done")
        prep = sem("ro_prep")
        dve = sem("ro_dve")
        mean_var = sem("ro_mean_var")
        rstd_done = sem("ro_rstd_done")
        xn_done = sem("ro_xn_done")
        stored = sem("ro_stored")
        xt_ps = sem("ro_xt_ps")
        xhi_s = sem("ro_xhi_s")
        xlo_s = sem("ro_xlo_s")
        rw_s = sem("ro_rw_s")
        lg_ps = sem("ro_lg_ps")
        lg_s = sem("ro_lg_s")
        lgt_ps = sem("ro_lgt_ps")
        sub_done = sem("ro_sub_done")
        exp_done = sem("ro_exp_done")
        sel_done = sem("ro_sel_done")
        rank_ps = sem("ro_rank_ps")
        pos_done = sem("ro_pos_done")
        scat = sem("ro_scat")

        block = ctx.enter_context(nc.Block())

        @block.sync
        def _(sp):
            for dst, src in ((idn[:], ident), (tri[:], tri_b), (rk[:], rank8.unsqueeze(0).to_broadcast([P, NE])),
                             (tno[:], tile_no.unsqueeze(0).to_broadcast([P, SLOT_TILES])),
                             (rw_in[:], router_w.rearrange("(k p) e -> p k e", p=P)),
                             (rb[:], router_b.unsqueeze(1))):
                sp.dma_start(dst, src).then_inc(const_in, 16)
            sp.dma_start(h2_dram.rearrange("(n p) d -> p n d", p=P), h_all[:]).then_inc(stored, 16)
            sp.wait_ge(prep, 1)
            sp.dma_start(slots_dram[TOK:, :].rearrange("(n p) d -> p n d", p=P),
                         zero[:].unsqueeze(1).to_broadcast([P, SLOT_TILES + 1, DM])).then_inc(stored, 16)
            sp.wait_ge(xn_done, TILES)
            sp.dma_start(slots_dram[0:TOK, :].rearrange("(n p) d -> p n d", p=P), xn[:]).then_inc(stored, 16)
            for n in range(2 * (NE + 1)):
                e, second = n // 2, n % 2
                if n >= 2:
                    sp.wait_ge(w_lo_done, n - 1)
                    sp.wait_ge(w_hi_done, n - 1)
                if second:
                    src = w2[e].rearrange("(k p) n -> p k n", p=P)
                    dst = wst[1][:, 0:FC * DM].rearrange("p (k n) -> p k n", k=FC)
                else:
                    src = w1[e].rearrange("(k p) n -> p k n", p=P)
                    dst = wst[0][:, 0:KC * FF].rearrange("p (k n) -> p k n", k=KC)
                sp.dma_start(dst, src).then_inc(w_in[second], 16)
            sp.wait_ge(stored, 48)

        def scatter(g):
            g.wait_ge(pos_done, 2)
            g.wait_ge(stored, 48)
            for n in range(TILES):
                for k in range(2):
                    g.indirect_dma_start(out=slots_dram, out_offset=bass.IndirectOffsetOnAxis(ap=pos_i[:, k, n:n + 1], axis=0),
                                         in_=xn[:, n, :], in_offset=None).then_inc(scat, 16)

        @block.gpsimd
        def _(g):
            g.memset(zero[:], 0.0).then_inc(prep, 1)
            g.memset(mhalf[:], -0.5).then_inc(prep, 1)
            g.memset(ones[:], 1.0).then_inc(prep, 1)
            g.wait_ge(mean_var, 1)
            g.wait_ge(prep, 2)
            g.tensor_tensor(rstd[:], vare[:], mhalf[:], ALU.pow).then_inc(rstd_done, 1)
            for n in range(2 * (NE + 1)):
                e, second = n // 2, n % 2
                if n == 10:
                    scatter(g)
                g.wait_ge(w_in[second], 16 * (n // 2 + 1))
                g.wait_ge(w_hi_done, n + 1)
                hi = (w2_all if second else w1_all)[:, 0, e]
                lo = (w2_all if second else w1_all)[:, 1, e]
                n_el = 1024
                g.tensor_tensor(lo.rearrange("p k n -> p (k n)"), wst[second][:, 0:n_el],
                                hi.rearrange("p k n -> p (k n)").bitcast(F32), ALU.subtract).then_inc(w_lo_done, 1)
            g.wait_ge(scat, 16 * 2 * TILES)

        @block.scalar
        def _(act):
            act.wait_ge(const_in, 16 * 6)
            act.copy(rw_hi[:], rw_in[:]).then_inc(rw_s, 1)
            for n in range(4):
                act.wait_ge(xt_ps, n + 1)
                if n >= 1:
                    act.wait_ge(lg_ps, n)
                for k in range(KC):
                    act.copy(x_hi[:, k, :], ps[:, 2 * (n % 2) + k, :]).then_inc(xhi_s, 1)
                act.wait_ge(lg_ps, n + 1)
                if n >= 2:
                    act.wait_ge(lgt_ps, n - 1)
                act.activation(lg_t[:, n % 2, :], ps[0:NE, 4 + n % 2, :], ACT.Identity,
                               bias=rb[:, 0:1]).then_inc(lg_s, 1)
            act.wait_ge(sub_done, 1)
            act.activation(pr[:], pr[:], ACT.Exp).then_inc(exp_done, 1)
            for n in range(2 * (NE + 1)):
                e, second = n // 2, n % 2
                act.wait_ge(w_in[second], 16 * (n // 2 + 1))
                hi = (w2_all if second else w1_all)[:, 0, e]
                act.copy(hi.rearrange("p k n -> p (k n)"), wst[second][:, 0:1024]).then_inc(w_hi_done, 1)

        @block.vector
        def _(v):
            count = [0]

            def link(ins):
                count[0] += 1
                ins.then_inc(dve, 1)
                v.wait_ge(dve, count[0])

            for n in range(TILES):
                ins = v.bn_stats(stats[:, n, :], h_all[:, n, :])
            link(ins)
            for n in range(TILES):
                ins = v.bn_aggr(mv[:, n, :], stats[:, n, :])
            link(ins)
            v.tensor_scalar(vare[:], mv[:, :, 1], EPS, None, ALU.add).then_inc(mean_var, 1)
            v.wait_ge(const_in, 16 * 6)
            v.wait_ge(rw_s, 1)
            v.tensor_tensor(rw_lo[:], rw_in[:], rw_hi[:].bitcast(F32), ALU.subtract).then_inc(rw_s, 1)
            v.wait_ge(rstd_done, 1)
            for n in range(TILES):
                v.tensor_scalar(xn[:, n, :], h_all[:, n, :], mv[:, n, 0:1], rstd[:, n:n + 1],
                                ALU.subtract, ALU.mult).then_inc(xn_done, 1)
            for n in range(4):
                v.wait_ge(xhi_s, KC * n + KC)
                if n >= 1:
                    v.wait_ge(lg_ps, n)
                for k in range(KC):
                    v.tensor_tensor(x_lo[:, k, :], ps[:, 2 * (n % 2) + k, :], x_hi[:, k, :].bitcast(F32),
                                    ALU.subtract).then_inc(xlo_s, 1)
            v.wait_ge(lgt_ps, 4)
            lg = ps[:, 6, 0:TILES * NE].rearrange("p (n e) -> p n e", e=NE)
            over = lambda s: s.unsqueeze(2).to_broadcast(S3)
            link(v.tensor_reduce(s1[:], lg, AX_X, ALU.max))
            v.tensor_tensor(pr[:], lg, over(s1[:]), ALU.subtract).then_inc(sub_done, 1)
            v.wait_ge(exp_done, 1)
            link(v.tensor_reduce(s1[:], pr[:], AX_X, ALU.add))
            link(v.reciprocal(s1[:], s1[:]))
            link(v.tensor_tensor(pr[:], pr[:], over(s1[:]), ALU.mult))
            rank = rk[:].unsqueeze(1).to_broadcast(S3)
            cur = pr
            for k, oh in enumerate((oh1, oh2)):
                top = w_top[:, k, :]
                link(v.tensor_reduce(top, cur[:], AX_X, ALU.max))
                link(v.tensor_tensor(b3[:], cur[:], over(top), ALU.is_equal))
                link(v.tensor_tensor(b3[:], b3[:], rank, ALU.mult))
                link(v.tensor_reduce(s2[:], b3[:], AX_X, ALU.max))
                link(v.tensor_tensor(oh[:], b3[:], over(s2[:]), ALU.is_equal))
                if k == 0:
                    link(v.scalar_tensor_tensor(out=a3[:], in0=oh[:], scalar=-BIG, in1=pr[:], op0=ALU.mult, op1=ALU.add))
                    cur = a3
            v.tensor_tensor(sel_b[:], oh1[:], oh2[:], ALU.add).then_inc(sel_done, 1)
            v.wait_ge(rank_ps, 1)
            within = ps[:, 6, 0:TILES * NE].rearrange("p (n e) -> p n e", e=NE)
            totals = ps[:, 7, 0:TILES * NE].rearrange("p (n e) -> p n e", e=NE)
            link(v.tensor_copy(a3[:], totals))
            src, dst = a3, b3
            for k in range(4):
                m = 1 << k
                v.tensor_copy(dst[:, 0:m], src[:, 0:m])
                link(v.tensor_tensor(dst[:, m:], src[:, m:], src[:, 0:TILES - m], ALU.add))
                src, dst = dst, (c3 if k == 0 else src)
            incl = src
            link(v.tensor_tensor(dst[:], incl[:], totals, ALU.subtract))
            link(v.tensor_tensor(dst[:], dst[:], within, ALU.add))
            ranks = dst
            link(v.tensor_scalar(ei[:], incl[:, TILES - 1, :], float(P - 1), None, ALU.add))
            link(v.tensor_scalar(ei[:], ei[:], 7, None, ALU.arith_shift_right))
            link(v.tensor_copy(e1[:], ei[:]))
            src, dst = e1, e2
            for k in range(3):
                m = 1 << k
                v.tensor_copy(dst[:, 0:m], src[:, 0:m])
                link(v.tensor_tensor(dst[:, m:], src[:, m:], src[:, 0:NE - m], ALU.add))
                src, dst = dst, (e3 if k == 0 else src)
            ends = src
            v.tensor_tensor(te[:], tno[:].unsqueeze(2).to_broadcast([P, SLOT_TILES, NE]),
                            ends[:].unsqueeze(1).to_broadcast([P, SLOT_TILES, NE]), ALU.is_ge)
            link(v.tensor_tensor(dst[:], ends[:], e1[:], ALU.subtract))
            link(v.tensor_reduce(tf[:], te[:], AX_X, ALU.add))
            v.memset(step_expert[:, 0:TILES], NE)
            v.tensor_scalar(step_expert[:, TILES:NSTEP], tf[:], float(NE - 1), None, ALU.min)
            link(v.tensor_scalar(dst[:], dst[:], float(P), float(TOK), ALU.mult, ALU.add))
            link(v.tensor_tensor(ranks[:], ranks[:], dst[:].unsqueeze(1).to_broadcast(S3), ALU.add))
            for k, oh in enumerate((oh1, oh2)):
                link(v.tensor_tensor(pr[:], oh[:], ranks[:], ALU.mult))
                link(v.tensor_reduce(pf[:, k, :], pr[:], AX_X, ALU.add))
                v.tensor_copy(pos_i[:, k, :], pf[:, k, :]).then_inc(pos_done, 1)

        @block.tensor
        def _(pe):
            pe.wait_ge(const_in, 16 * 6)
            pe.wait_ge(rw_s, 2)
            for n in range(4):
                pe.wait_ge(xn_done, 4 * n + 4)
                if n >= 2:
                    pe.wait_ge(xlo_s, KC * (n - 1))
                for k in range(KC):
                    for t in range(4):
                        last = pe.transpose(ps[:, 2 * (n % 2) + k, t * P:(t + 1) * P],
                                            xn[:, 4 * n + t, k * P:(k + 1) * P], idn[:])
                last.then_inc(xt_ps, 1)
                if n >= 2:
                    pe.wait_ge(lg_s, n - 1)
                pe.wait_ge(xhi_s, KC * n + KC)
                pe.wait_ge(xlo_s, KC * n + KC)
                pairs = [(x[:, k, :], w[:, k, :]) for k in range(KC)
                         for x, w in ((rw_hi, x_hi), (rw_hi, x_lo), (rw_lo, x_hi))]
                for i, (x, w) in enumerate(pairs):
                    last = pe.matmul(ps[0:NE, 4 + n % 2, :], x, w, start=i == 0, stop=i == 5)
                last.then_inc(lg_ps, 1)
                pe.wait_ge(lg_s, n + 1)
                for t in range(4):
                    m = 4 * n + t
                    last = pe.transpose(ps[:, 6, m * NE:(m + 1) * NE], lg_t[:, n % 2, t * P:(t + 1) * P],
                                        idn[0:NE, 0:NE])
                last.then_inc(lgt_ps, 1)
            pe.wait_ge(sel_done, 1)
            pe.wait_ge(prep, 3)
            sel = sel_b[:].rearrange("p n e -> p (n e)")
            pe.matmul(ps[:, 6, 0:TILES * NE], tri[:], sel, start=True, stop=True)
            pe.matmul(ps[:, 7, 0:TILES * NE], ones[:], sel, start=True, stop=True).then_inc(rank_ps, 1)


def expert_phase(nc, slots_dram, y_dram, b1_all, b2_all, ident, w1_all, w2_all, step_expert):
    with ExitStack() as ctx:
        def sb(name, shape, dt=F32):
            return ctx.enter_context(nc.sbuf_tensor(name, shape, dt))

        def sem(name):
            return ctx.enter_context(nc.semaphore(name))

        idn = sb("ex_ident", [P, P])
        b1 = sb("ex_b1", [P, NE + 1, FF])
        b2 = sb("ex_b2", [P, NE + 1, DM])
        xin = [sb(f"ex_xin{i}", [P, DM]) for i in range(2)]
        x_hi = [sb(f"ex_x_hi{i}", [P, DM], F32R) for i in range(2)]
        x_lo = [sb(f"ex_x_lo{i}", [P, DM], F32R) for i in range(2)]
        hb = [sb(f"ex_hb{i}", [P, FF]) for i in range(2)]
        h_hi = [sb(f"ex_h_hi{i}", [P, FF], F32R) for i in range(2)]
        h_lo = [sb(f"ex_h_lo{i}", [P, FF], F32R) for i in range(2)]
        yo = [sb(f"ex_y{i}", [P, DM]) for i in range(2)]
        ps = ctx.enter_context(nc.psum_tensor("ex_ps", [P, 8, 512], F32))

        const_in = sem("ex_const_in")
        x_in = [sem(f"ex_x_in{i}") for i in range(2)]
        y_out = [sem(f"ex_y_out{i}") for i in range(2)]
        xt_ps = sem("ex_xt_ps")
        xhi_s = sem("ex_xhi_s")
        xlo_s = sem("ex_xlo_s")
        h_ps = sem("ex_h_ps")
        hb_v = sem("ex_hb_v")
        gelu_a = sem("ex_gelu_a")
        ht_ps = sem("ex_ht_ps")
        hhi_a = sem("ex_hhi_a")
        hlo_v = sem("ex_hlo_v")
        y_ps = sem("ex_y_ps")
        y_v = sem("ex_y_v")

        block = ctx.enter_context(nc.Block())
        PAIRS = (NSTEP - 1) // 2
        assert NSTEP == 1 + 2 * PAIRS

        def in_pairs(eng, body):
            body(1, 1, 0)
            body(2, 0, 1)
            with eng.Fori(1, PAIRS) as n:
                body(n * 2 + 1, 1, n)
                body(n * 2 + 2, 0, n + 1)

        def wait_reuse(eng, semaphore, value):
            if not isinstance(value, int) or value > 0:
                eng.wait_ge(semaphore, value)

        def rows(i):
            return bass.ds(i * P, P)

        def expert_of(eng, i):
            at = slice(i, i + 1) if isinstance(i, int) else bass.ds(i, 1)
            return eng.value_load(step_expert[0:1, at], min_val=0, max_val=NE)

        @block.sync
        def _(sp):
            sp.dma_start(idn[:], ident).then_inc(const_in, 16)
            sp.dma_start(b1[:], b1_all.unsqueeze(0).to_broadcast([P, NE + 1, FF])).then_inc(const_in, 16)
            sp.dma_start(b2[:], b2_all.unsqueeze(0).to_broadcast([P, NE + 1, DM])).then_inc(const_in, 16)
            sp.dma_start(xin[0][:], slots_dram[0:P, :]).then_inc(x_in[0], 16)
            sp.dma_start(xin[1][:], slots_dram[P:2 * P, :]).then_inc(x_in[1], 16)

            def step(i, par, k):
                sp.wait_ge(xt_ps, i)
                sp.dma_start(xin[1 - par][:], slots_dram[rows(i + 1), :]).then_inc(x_in[1 - par], 16)
                sp.wait_ge(y_v, i)
                sp.dma_start(y_dram[rows(i - 1), :], yo[1 - par][:]).then_inc(y_out[1 - par], 16)

            in_pairs(sp, step)
            sp.wait_ge(y_v, NSTEP)
            sp.dma_start(y_dram[(NSTEP - 1) * P:NSTEP * P, :], yo[0][:]).then_inc(y_out[0], 16)
            sp.wait_ge(y_out[0], 16 * (PAIRS + 1))
            sp.wait_ge(y_out[1], 16 * PAIRS)

        @block.tensor
        def _(pe):
            def turn_x(i, par, k):
                pe.wait_ge(x_in[par], 16 * k + 16)
                for c in range(KC):
                    last = pe.transpose(ps[:, 6 + par, c * P:(c + 1) * P], xin[par][:, c * P:(c + 1) * P], idn[:])
                last.then_inc(xt_ps, 1)

            def first_layer(i, par, free=None):
                e = expert_of(pe, i)
                if free is not None:
                    wait_reuse(pe, hb_v, free)
                pe.wait_ge(xhi_s, i + 1)
                pe.wait_ge(xlo_s, i + 1)
                pairs = [(x[par][:, c * P:(c + 1) * P], w1_all[:, part, bass.ds(e, 1), c, :].rearrange("p o n -> p (o n)"))
                         for c in range(KC) for x, part in ((x_hi, 0), (x_hi, 1), (x_lo, 0))]
                for n, (x, w) in enumerate(pairs):
                    last = pe.matmul(ps[:, par, :], x, w, start=n == 0, stop=n == len(pairs) - 1)
                last.then_inc(h_ps, 1)

            def turn_h(i, par):
                pe.wait_ge(gelu_a, i + 1)
                for c in range(FC):
                    last = pe.transpose(ps[:, 2 + par, c * P:(c + 1) * P], hb[par][:, c * P:(c + 1) * P], idn[:])
                last.then_inc(ht_ps, 1)

            def second_layer(i, par, free=None):
                e = expert_of(pe, i)
                if free is not None:
                    wait_reuse(pe, y_v, free)
                pe.wait_ge(hhi_a, i + 1)
                pe.wait_ge(hlo_v, i + 1)
                pairs = [(x[par][:, c * P:(c + 1) * P], w2_all[:, part, bass.ds(e, 1), c, :].rearrange("p o n -> p (o n)"))
                         for c in range(FC) for x, part in ((h_hi, 0), (h_hi, 1), (h_lo, 0))]
                for n, (x, w) in enumerate(pairs):
                    last = pe.matmul(ps[:, 4 + par, 0:DM], x, w, start=n == 0, stop=n == len(pairs) - 1)
                last.then_inc(y_ps, 1)

            pe.wait_ge(const_in, 48)
            turn_x(0, 0, 0)
            first_layer(0, 0)
            turn_x(1, 1, 0)
            turn_h(0, 0)

            def step(i, par, k):
                first_layer(i, par, i - 1)
                pe.wait_ge(xlo_s, i)
                turn_x(i + 1, 1 - par, k + par)
                second_layer(i - 1, 1 - par, i - 1)
                wait_reuse(pe, hlo_v, i - 1)
                turn_h(i, par)

            in_pairs(pe, step)
            second_layer(NSTEP - 1, 0, NSTEP - 1)

        @block.scalar
        def _(act):
            def x_high(i, par):
                act.wait_ge(xt_ps, i + 1)
                act.copy(x_hi[par][:], ps[:, 6 + par, 0:DM]).then_inc(xhi_s, 1)

            def gelu(i, par):
                act.wait_ge(hb_v, i + 1)
                act.activation(hb[par][:], hb[par][:], ACT.Gelu).then_inc(gelu_a, 1)

            def h_high(i, par):
                act.wait_ge(ht_ps, i + 1)
                act.copy(h_hi[par][:], ps[:, 2 + par, :]).then_inc(hhi_a, 1)

            x_high(0, 0)
            x_high(1, 1)
            gelu(0, 0)
            h_high(0, 0)

            def step(i, par, k):
                act.wait_ge(h_ps, i)
                x_high(i + 1, 1 - par)
                gelu(i, par)
                wait_reuse(act, y_ps, i - 1)
                h_high(i, par)

            in_pairs(act, step)

        @block.vector
        def _(v):
            def bias(b, i):
                return b[:, bass.ds(expert_of(v, i), 1), :].rearrange("p o n -> p (o n)")

            def x_low(i, par):
                v.wait_ge(xhi_s, i + 1)
                v.tensor_tensor(x_lo[par][:], ps[:, 6 + par, 0:DM], x_hi[par][:].bitcast(F32),
                                ALU.subtract).then_inc(xlo_s, 1)

            def h_bias(i, par, turned=None):
                b = bias(b1, i)
                if turned is not None:
                    wait_reuse(v, ht_ps, turned)
                v.wait_ge(h_ps, i + 1)
                v.tensor_tensor(hb[par][:], ps[:, par, :], b, ALU.add).then_inc(hb_v, 1)

            def h_low(i, par):
                v.wait_ge(hhi_a, i + 1)
                v.tensor_tensor(h_lo[par][:], ps[:, 2 + par, :], h_hi[par][:].bitcast(F32),
                                ALU.subtract).then_inc(hlo_v, 1)

            def y_bias(i, par, stored=None):
                b = bias(b2, i)
                if stored is not None:
                    wait_reuse(v, y_out[par], stored)
                v.wait_ge(y_ps, i + 1)
                v.tensor_tensor(yo[par][:], ps[:, 4 + par, 0:DM], b, ALU.add).then_inc(y_v, 1)

            v.wait_ge(const_in, 48)
            x_low(0, 0)
            h_bias(0, 0)
            x_low(1, 1)
            h_low(0, 0)

            def step(i, par, k):
                h_bias(i, par, i - 1)
                v.wait_ge(h_ps, i)
                x_low(i + 1, 1 - par)
                y_bias(i - 1, 1 - par, k * 16 - (0 if par else 16))
                wait_reuse(v, y_ps, i - 1)
                h_low(i, par)

            in_pairs(v, step)
            y_bias(NSTEP - 1, 0, PAIRS * 16)


def combine_phase(nc, h2_dram, y_dram, pos_i, w_top, out):
    with ExitStack() as ctx:
        def sb(name, n):
            return [ctx.enter_context(nc.sbuf_tensor(f"co_{name}{i}", [P, DM], F32)) for i in range(n)]

        BUF = 4
        hh, ys, ya, yb = sb("h", BUF), sb("ys", BUF), sb("ya", BUF), sb("yb", BUF)
        load = [ctx.enter_context(nc.semaphore(f"co_load{i}")) for i in range(BUF)]
        gath = [ctx.enter_context(nc.semaphore(f"co_gather{i}")) for i in range(BUF)]
        store = [ctx.enter_context(nc.semaphore(f"co_store{i}")) for i in range(BUF)]
        added = ctx.enter_context(nc.semaphore("co_added"))
        block = ctx.enter_context(nc.Block())
        tok = out.rearrange("b t d -> (b t) d")

        @block.sync
        def _(sp):
            for n in range(TILES):
                if n >= BUF:
                    sp.wait_ge(store[n % BUF], 16 * (n // BUF))
                rows = slice(n * P, (n + 1) * P)
                sp.dma_start(hh[n % BUF][:], h2_dram[rows, :]).then_inc(load[n % BUF], 16)
                sp.dma_start(ys[n % BUF][:], y_dram[rows, :]).then_inc(load[n % BUF], 16)

        @block.gpsimd
        def _(g):
            for n in range(TILES):
                if n >= BUF:
                    g.wait_ge(added, 3 * (n - BUF + 1))
                for k, dst in enumerate((ya, yb)):
                    g.indirect_dma_start(out=dst[n % BUF][:], out_offset=None, in_=y_dram,
                                         in_offset=bass.IndirectOffsetOnAxis(ap=pos_i[:, k, n:n + 1], axis=0)
                                         ).then_inc(gath[n % BUF], 16)

        @block.scalar
        def _(act):
            for n in range(TILES):
                act.wait_ge(added, 3 * n + 3)
                act.dma_start(tok[n * P:(n + 1) * P, :], hh[n % BUF][:]).then_inc(store[n % BUF], 16)
            for i in range(BUF):
                act.wait_ge(store[i], 16 * (TILES // BUF))

        @block.vector
        def _(v):
            for n in range(TILES):
                i = n % BUF
                v.wait_ge(load[i], 32 * (n // BUF + 1))
                v.tensor_tensor(hh[i][:], hh[i][:], ys[i][:], ALU.add).then_inc(added, 1)
                v.wait_ge(added, 3 * n + 1)
                v.wait_ge(gath[i], 32 * (n // BUF + 1))
                v.scalar_tensor_tensor(out=hh[i][:], in0=ya[i][:], scalar=w_top[:, 0, n:n + 1], in1=hh[i][:],
                                       op0=ALU.mult, op1=ALU.add).then_inc(added, 1)
                v.wait_ge(added, 3 * n + 2)
                v.scalar_tensor_tensor(out=hh[i][:], in0=yb[i][:], scalar=w_top[:, 1, n:n + 1], in1=hh[i][:],
                                       op0=ALU.mult, op1=ALU.add).then_inc(added, 1)


def tower_kernel(nc, x_t, a_real_t, a_imag_t, b_t, log_dt, w_qkv, b_qkv, w_o, b_o, router_w, router_b,
                 sw1, sw2, rw1, rw2, b1_all, b2_all, rope, ident, ident_b, mask_b, select_b, tri_b,
                 rank8, tile_no, out):
    h_dram = nc.dram_tensor("h_scratch", (NB, SEQ, DM), F32, kind="Internal").ap()
    h2_dram = nc.dram_tensor("h2_scratch", (TOK, DM), F32, kind="Internal").ap()
    slots_dram = nc.dram_tensor("slots_scratch", ((NSTEP + 1) * P, DM), F32, kind="Internal").ap()
    y_dram = nc.dram_tensor("y_scratch", (NSTEP * P, DM), F32, kind="Internal").ap()
    w1 = [rw1[e] for e in range(NE)] + [sw1]
    w2 = [rw2[e] for e in range(NE)] + [sw2]

    s4d_phase(nc, x_t, a_real_t, a_imag_t, b_t, log_dt, ident, h_dram)
    with ExitStack() as ctx:
        def sb(name, shape, dt=F32):
            return ctx.enter_context(nc.sbuf_tensor(name, shape, dt))

        pos_i = sb("pos_i", [P, 2, TILES], U32)
        w_top = sb("w_top", [P, 2, TILES])
        step_expert = sb("step_expert", [P, NSTEP], I32)
        with ExitStack() as early:
            h_all = early.enter_context(nc.sbuf_tensor("h_all", [P, TILES, DM], F32, side="right"))
            attention_phase(nc, h_dram, w_qkv, w_o, b_qkv, b_o, rope, ident, ident_b, mask_b, select_b, h_all)
            w1_all = sb("w1_all", [P, 2, NE + 1, KC, FF], F32R)
            w2_all = sb("w2_all", [P, 2, NE + 1, FC, DM], F32R)
            routing_phase(nc, h_all, h2_dram, slots_dram, router_w, router_b, ident, tri_b, rank8, tile_no,
                          w1_all, w2_all, w1, w2, pos_i, w_top, step_expert)
        expert_phase(nc, slots_dram, y_dram, b1_all, b2_all, ident, w1_all, w2_all, step_expert)
        combine_phase(nc, h2_dram, y_dram, pos_i, w_top, out)


def kernel(**inputs):
    import ml_dtypes
    import numpy as np
    import concourse.bacc as bacc
    from concourse.bass_utils import run_bass_kernel_spmd

    def channels(a):
        return a.reshape(4, SEQ // 4, *a.shape[1:]).swapaxes(0, 1).reshape(a.shape)

    i = {name: np.asarray(a) for name, a in inputs.items()}
    bf16 = ml_dtypes.bfloat16
    freq = 1.0 / 1000.0 ** (np.arange(0, HS, 2, dtype=np.float32) / HS)
    angle = np.arange(SEQ, dtype=np.float32)[:, None] * freq[None]
    rope = np.empty((SEQ, 2, HS), np.float32)
    rope[:, 0, 0::2] = rope[:, 0, 1::2] = np.cos(angle)
    rope[:, 1, 0::2] = -np.sin(angle)
    rope[:, 1, 1::2] = np.sin(angle)
    causal = np.triu(np.full((P, P), -1e30, np.float32), 1)
    select = np.zeros((P, NH, P), np.float32)
    for h in range(NH):
        select[[h, NH + h], h] = 1.0
    arrays = dict(
        x_t=channels(i["x"].transpose(1, 2, 3, 0)).transpose(1, 2, 0, 3),
        a_real_t=channels(i["L0_tok_inv_A_real"]).T,
        a_imag_t=channels(i["L0_tok_A_imag"]).T,
        b_t=channels(i["L0_tok_B_ri"]).transpose(1, 2, 0),
        log_dt=channels(i["L0_tok_log_dt"]),
        w_qkv=i["L0_attn_W_attn"].T, b_qkv=i["L0_attn_b_attn"],
        w_o=i["L0_attn_W_o"].T, b_o=i["L0_attn_b_o"],
        router_w=i["L0_ffn_router_w"], router_b=i["L0_ffn_router_b"],
        sw1=i["L0_ffn_sw1"], sw2=i["L0_ffn_sw2"], rw1=i["L0_ffn_rw1"], rw2=i["L0_ffn_rw2"],
        b1_all=np.concatenate([i["L0_ffn_rb1"], i["L0_ffn_sb1"][None]]),
        b2_all=np.concatenate([i["L0_ffn_rb2"], i["L0_ffn_sb2"][None]]),
        rope=rope.reshape(NT, P, 2, HS).transpose(1, 0, 2, 3),
        ident=np.eye(P, dtype=np.float32), ident_b=np.eye(P).astype(bf16),
        mask_b=np.tile(causal, (1, 4)).astype(bf16), select_b=select.astype(bf16),
        tri_b=np.triu(np.ones((P, P)), 1).astype(bf16),
        rank8=(NE - np.arange(NE)).astype(np.float32),
        tile_no=np.arange(SLOT_TILES).astype(np.float32))
    arrays = {f"in_{name}": np.ascontiguousarray(a) for name, a in arrays.items()}

    nc = bacc.Bacc("TRN2", target_bir_lowering=False, num_devices=1)
    args = [nc.dram_tensor(name, a.shape, mybir.dt.from_np(a.dtype), kind="ExternalInput").ap()
            for name, a in arrays.items()]
    out = nc.dram_tensor("out", (NB, SEQ, DM), F32, kind="ExternalOutput").ap()
    tower_kernel(nc, *args, out)
    result = run_bass_kernel_spmd(nc, [arrays], core_ids=[0])
    return result.results[0]["out"]
```

```python
import math
from contextlib import ExitStack

import concourse.bass as bass
from concourse import mybir

F32 = mybir.dt.float32
F32R = mybir.dt.float32r
BF16 = mybir.dt.bfloat16
I32 = mybir.dt.int32
ALU = mybir.AluOpType
ACT = mybir.ActivationFunctionType
AX_X = mybir.AxisListType.X

P = 128
NB = 8
SEQ = 256
DM = 256
NS = 64
L0 = 32
L1 = DM // L0
CHUNK = 32
NCHUNK = SEQ // CHUNK
QUADS = CHUNK // 4
AHEAD = 2

LOG2E = 1.0 / math.log(2.0)
LN2_HI = 355.0 / 512.0
LN2_LO = math.log(2.0) - LN2_HI


def s4d_phase(nc, x_t, a_real_t, a_imag_t, b_t, log_dt, ident, h_dram):
    HALF = P // 2
    with ExitStack() as ctx:
        def sb(name, shape, dt=F32):
            return ctx.enter_context(nc.sbuf_tensor(name, shape, dt))

        def sem(name):
            return ctx.enter_context(nc.semaphore(name))

        idn = sb("s4_ident", [P, P])
        c_re = sb("s4_c_re", [P, SEQ, NB])
        c_im = sb("s4_c_im", [P, SEQ, NB])
        logs = sb("s4_logs", [P, 2, SEQ])
        aimag = sb("s4_aimag", [P, SEQ])
        ex = [sb(f"s4_ex{i}", [P, 2, SEQ]) for i in range(3)]
        ex_int = sb("s4_ex_int", [P, 2, SEQ], I32)
        tmp = [sb(f"s4_tmp{i}", [P, SEQ]) for i in range(4)]
        b_r = sb("s4_b_r", [P, SEQ])
        b_i = sb("s4_b_i", [P, SEQ])
        zr = sb("s4_zr", [P, 8, SEQ])
        zi = sb("s4_zi", [P, 8, SEQ])
        u = sb("s4_u", [P, SEQ, 16])
        w = sb("s4_w", [P, SEQ, 16])
        p1 = sb("s4_p1", [P, SEQ, L1])
        p2 = sb("s4_p2", [P, SEQ, L1])
        t_dve = [sb(f"s4_tdve{i}", [P, SEQ * 8]) for i in range(2)]
        t_pool = [sb(f"s4_tpool{i}", [P, SEQ * 4]) for i in range(2)]
        t_fin = [sb(f"s4_tfin{i}", [P, CHUNK, 16]) for i in range(2)]
        zc = [sb(f"s4_zc{i}", [P, CHUNK, L0]) for i in range(2)]
        a_re = [sb(f"s4_a_re{i}", [P, CHUNK, NB, L1]) for i in range(2)]
        a_im = [sb(f"s4_a_im{i}", [P, CHUNK, NB, L1]) for i in range(2)]
        k_sb = sb("s4_k", [P, NB // 2, L1, 2, SEQ // 4])
        h_sb = sb("s4_h", [P, NB // 2, 4, DM])
        ps = [ctx.enter_context(nc.psum_tensor(f"s4_ps{i}", [P, 512], F32)) for i in range(8)]

        par_in = sem("s4_par_in")
        x_in = sem("s4_x_in")
        dve = sem("s4_dve")
        pool = sem("s4_pool")
        squares = sem("s4_squares")
        b_ready = sem("s4_b_ready")
        u_done = sem("s4_u_done")
        z_low = sem("s4_z_low")
        z_high = sem("s4_z_high")
        are_done = sem("s4_are_done")
        aim_done = sem("s4_aim_done")
        mm_done = sem("s4_mm_done")
        k_done = sem("s4_k_done")
        tr_done = sem("s4_tr_done")
        h_v = sem("s4_h_v")
        h_a = sem("s4_h_a")
        h_out = sem("s4_h_out")

        block = ctx.enter_context(nc.Block())

        @block.sync
        def _(sp):
            sp.dma_start(logs[:, 0], log_dt.unsqueeze(0).to_broadcast([P, SEQ])).then_inc(par_in, 16)
            for d in range(2):
                rows = slice(HALF * d, HALF * (d + 1))
                sp.dma_start(logs[rows, 1], a_real_t).then_inc(par_in, 16)
                sp.dma_start(aimag[rows, :], a_imag_t).then_inc(par_in, 16)
                sp.dma_start(b_r[rows, :], b_t[:, d]).then_inc(par_in, 16)
                sp.dma_start(b_i[rows, :], b_t[:, 1 - d]).then_inc(par_in, 16)
            sp.dma_start(idn[:], ident).then_inc(par_in, 16)
            for d in range(2):
                rows = slice(HALF * d, HALF * (d + 1))
                sp.dma_start(c_re[rows], x_t[:, 0]).then_inc(x_in, 16)
                sp.dma_start(c_im[rows], x_t[:, 1]).then_inc(x_in, 16)
            for bp in range(NB // 2):
                sp.wait_ge(h_v, bp + 1)
                sp.wait_ge(h_a, bp + 1)
                for s in range(2):
                    sp.dma_start(
                        h_dram[2 * bp + s].rearrange("(j q) l -> q j l", j=4),
                        h_sb[HALF * s:HALF * (s + 1), bp],
                    ).then_inc(h_out, 16)
            sp.wait_ge(h_out, 16 * NB)

        @block.scalar
        def _(act):
            act.sem_inc(k_done, 2 * AHEAD)
            act.wait_ge(u_done, 1)
            with act.Fori(0, NCHUNK // 2) as i:
                for half in range(2):
                    c = i * 2 + half
                    act.wait_ge(mm_done, c + 1)
                    act.copy(zc[half][:, :, 0:16], u[:, bass.ds(c * CHUNK, CHUNK), :]).then_inc(z_low, 1)
                    act.wait_ge(mm_done, c + 1 + AHEAD)
                    src = ps[half][:].rearrange("p (q b s l) -> p q b s l", q=QUADS, s=2, l=L1)
                    for s in range(2):
                        dst = k_sb[:, :, :, s, bass.ds(c * QUADS, QUADS)].rearrange("p b l q -> p q b l")
                        act.copy(dst, src[:, :, :, s, :]).then_inc(k_done, 1)
            for n in range(1, 8, 2):
                act.wait_ge(tr_done, n + 1)
                bp, g = n // 2, n % 2
                act.copy(h_sb[:, bp, :, g * 128:(g + 1) * 128].rearrange("p j (g l) -> p g j l", g=4),
                         ps[n][:].rearrange("p (g j l) -> p g j l", g=4, j=4)).then_inc(h_a, 1)

        @block.vector
        def _(v):
            count = [0]

            def link(ins):
                count[0] += 1
                ins.then_inc(dve, 1)
                v.wait_ge(dve, count[0])

            hdt, xr, y, t = tmp
            one_x, n2 = t_dve[0][:, 0:SEQ], t_dve[0][:, SEQ:2 * SEQ]
            v.memset(u[0:HALF, :, 0:1], 1.0)
            v.memset(u[HALF:P, :, 0:1], 0.0)
            v.memset(w[0:HALF, :, 0:1], 0.0)
            link(v.memset(w[HALF:P, :, 0:1], 1.0))
            v.wait_ge(par_in, 16 * 10)
            x_, r_, e_ = ex
            link(v.tensor_scalar(x_[:], logs[:], -87.0, 88.0, ALU.max, ALU.min))
            link(v.tensor_scalar(ex_int[:], x_[:], LOG2E, None, ALU.mult))
            link(v.tensor_copy(e_[:], ex_int[:]))
            link(v.scalar_tensor_tensor(out=r_[:], in0=e_[:], scalar=-LN2_HI, in1=x_[:],
                                        op0=ALU.mult, op1=ALU.add))
            link(v.scalar_tensor_tensor(out=r_[:], in0=e_[:], scalar=-LN2_LO, in1=r_[:],
                                        op0=ALU.mult, op1=ALU.add))
            v.tensor_scalar(ex_int[:], e_[:], 127.0, float(1 << 23), ALU.add, ALU.mult)
            link(v.tensor_scalar(x_[:], r_[:], 1.0 / math.factorial(7), None, ALU.mult))
            for k in range(6, 0, -1):
                link(v.scalar_tensor_tensor(out=x_[:], in0=x_[:], scalar=1.0 / math.factorial(k), in1=r_[:],
                                            op0=ALU.add, op1=ALU.mult))
            link(v.scalar_tensor_tensor(out=x_[:], in0=x_[:], scalar=1.0, in1=ex_int[:].bitcast(F32),
                                        op0=ALU.add, op1=ALU.mult))
            dt_, areal = x_[:, 0], x_[:, 1]
            v.tensor_scalar(p1[:, :, 0], b_r[:], 2.0, None, ALU.mult)
            v.tensor_scalar(p2[0:HALF, :, 0], b_i[0:HALF, :], -2.0, None, ALU.mult)
            v.tensor_scalar(p2[HALF:P, :, 0], b_i[HALF:P, :], 2.0, None, ALU.mult).then_inc(b_ready, 1)
            link(v.tensor_scalar(hdt[:], dt_, 0.5, None, ALU.mult))
            v.tensor_tensor(y[:], aimag[:], hdt[:], ALU.mult)
            link(v.scalar_tensor_tensor(out=xr[:], in0=areal, scalar=-1.0, in1=hdt[:],
                                        op0=ALU.mult, op1=ALU.mult))
            v.tensor_scalar(one_x, xr[:], -1.0, 1.0, ALU.mult, ALU.add)
            v.tensor_tensor(t[:], y[:], y[:], ALU.mult)
            link(v.tensor_tensor(n2, xr[:], xr[:], ALU.mult))
            link(v.tensor_tensor(one_x, one_x, one_x, ALU.mult))
            v.tensor_tensor(n2, n2, t[:], ALU.add)
            link(v.tensor_tensor(one_x, one_x, t[:], ALU.add))
            v.tensor_scalar(n2, n2, -1.0, 1.0, ALU.mult, ALU.add)
            link(v.reciprocal(one_x, one_x))
            v.tensor_tensor(zr[:, 0], n2, one_x, ALU.mult)
            link(v.scalar_tensor_tensor(out=zi[:, 0], in0=y[:], scalar=2.0, in1=one_x,
                                        op0=ALU.mult, op1=ALU.mult))
            for k in range(7):
                v.tensor_tensor(xr[:], zr[:, k], zr[:, k], ALU.mult)
                v.tensor_tensor(y[:], zi[:, k], zi[:, k], ALU.mult)
                link(v.scalar_tensor_tensor(out=zi[:, k + 1], in0=zr[:, k], scalar=2.0, in1=zi[:, k],
                                            op0=ALU.mult, op1=ALU.mult))
                ins = v.tensor_tensor(zr[:, k + 1], xr[:], y[:], ALU.subtract)
                link(ins)
            v.sem_inc(squares, 1)
            for k in range(4):
                m = 1 << k
                ta = t_dve[0][:, 0:SEQ * m].rearrange("p (h l) -> p h l", l=m)
                tb = t_dve[1][:, 0:SEQ * m].rearrange("p (h l) -> p h l", l=m)
                zr_m = zr[:, k].unsqueeze(2).to_broadcast([P, SEQ, m])
                zi_m = zi[:, k].unsqueeze(2).to_broadcast([P, SEQ, m])
                v.tensor_tensor(ta, u[:, :, 0:m], zr_m, ALU.mult)
                link(v.tensor_tensor(tb, w[:, :, 0:m], zi_m, ALU.mult))
                link(v.tensor_tensor(u[:, :, m:2 * m], ta, tb, ALU.subtract))
                v.tensor_tensor(ta, u[:, :, 0:m], zi_m, ALU.mult)
                link(v.tensor_tensor(tb, w[:, :, 0:m], zr_m, ALU.mult))
                link(v.tensor_tensor(w[:, :, m:2 * m], ta, tb, ALU.add))
            v.sem_inc(u_done, 1)
            v.wait_ge(x_in, 64)
            v.wait_ge(pool, 18)
            start = count[0]
            v.sem_inc(z_high, 1)
            with v.Fori(0, NCHUNK // 2) as i:
                for half in range(2):
                    c = i * 2 + half
                    hs = bass.ds(c * CHUNK, CHUNK)
                    zr16 = zr[:, 4, hs].unsqueeze(2).to_broadcast([P, CHUNK, 16])
                    zi16 = zi[:, 4, hs].unsqueeze(2).to_broadcast([P, CHUNK, 16])
                    v.wait_ge(z_high, c + 1)
                    v.tensor_tensor(t_fin[0][:], u[:, hs, :], zr16, ALU.mult)
                    v.tensor_tensor(t_fin[1][:], w[:, hs, :], zi16, ALU.mult).then_inc(dve, 1)
                    v.wait_ge(mm_done, c + 1)
                    v.wait_ge(dve, c + start + 1)
                    v.tensor_tensor(zc[half][:, :, 16:32], t_fin[0][:], t_fin[1][:],
                                    ALU.subtract).then_inc(z_high, 1)
                    v.tensor_tensor(
                        a_re[half][:],
                        c_re[:, hs, :].unsqueeze(3).to_broadcast([P, CHUNK, NB, L1]),
                        p1[:, hs, :].unsqueeze(2).to_broadcast([P, CHUNK, NB, L1]),
                        ALU.mult).then_inc(are_done, 1)
            for n in range(0, 8, 2):
                v.wait_ge(tr_done, n + 1)
                bp, g = n // 2, n % 2
                v.tensor_copy(h_sb[:, bp, :, g * 128:(g + 1) * 128].rearrange("p j (g l) -> p g j l", g=4),
                              ps[n][:].rearrange("p (g j l) -> p g j l", g=4, j=4)).then_inc(h_v, 1)

        @block.gpsimd
        def _(g):
            count = [0]

            def link(ins):
                count[0] += 1
                ins.then_inc(pool, 1)
                g.wait_ge(pool, count[0])

            g.wait_ge(b_ready, 1)
            g.wait_ge(squares, 1)
            for k in range(3):
                m = 1 << k
                ta = t_pool[0][:, 0:SEQ * m].rearrange("p (h l) -> p h l", l=m)
                tb = t_pool[1][:, 0:SEQ * m].rearrange("p (h l) -> p h l", l=m)
                zr_m = zr[:, k + 5].unsqueeze(2).to_broadcast([P, SEQ, m])
                zi_m = zi[:, k + 5].unsqueeze(2).to_broadcast([P, SEQ, m])
                link(g.tensor_tensor(ta, p1[:, :, 0:m], zr_m, ALU.mult))
                link(g.tensor_tensor(tb, p2[:, :, 0:m], zi_m, ALU.mult))
                link(g.tensor_tensor(p1[:, :, m:2 * m], ta, tb, ALU.add))
                link(g.tensor_tensor(ta, p2[:, :, 0:m], zr_m, ALU.mult))
                link(g.tensor_tensor(tb, p1[:, :, 0:m], zi_m, ALU.mult))
                link(g.tensor_tensor(p2[:, :, m:2 * m], ta, tb, ALU.subtract))
            g.wait_ge(x_in, 64)
            with g.Fori(0, NCHUNK // 2) as i:
                for half in range(2):
                    c = i * 2 + half
                    hs = bass.ds(c * CHUNK, CHUNK)
                    g.wait_ge(mm_done, c + 1)
                    g.tensor_tensor(
                        a_im[half][:],
                        c_im[:, hs, :].unsqueeze(3).to_broadcast([P, CHUNK, NB, L1]),
                        p2[:, hs, :].unsqueeze(2).to_broadcast([P, CHUNK, NB, L1]),
                        ALU.mult).then_inc(aim_done, 1)

        @block.tensor
        def _(pe):
            pe.sem_inc(mm_done, AHEAD)
            with pe.Fori(0, NCHUNK // 2) as i:
                for half in range(2):
                    c = i * 2 + half
                    pe.wait_ge(z_low, c + 1)
                    pe.wait_ge(z_high, c + 2)
                    pe.wait_ge(are_done, c + 1)
                    pe.wait_ge(aim_done, c + 1)
                    pe.wait_ge(k_done, 2 * c + 2)
                    for q in range(QUADS):
                        for a in (a_re, a_im):
                            for j in range(4):
                                last = pe.matmul(ps[half][32 * j:32 * j + 32, 64 * q:64 * q + 64],
                                                 zc[half][:, 4 * q + j, :],
                                                 a[half][:, 4 * q + j].rearrange("p b l -> p (b l)"),
                                                 start=a is a_re, stop=a is a_im)
                    last.then_inc(mm_done, 1)
            pe.wait_ge(k_done, 2 * (NCHUNK + AHEAD))
            for n in range(8):
                bp, g = n // 2, n % 2
                for k in range(4):
                    last = pe.transpose(ps[n][:, 128 * k:128 * k + 128],
                                        k_sb[:, bp, 4 * g + k].rearrange("p s q -> p (s q)"), idn[:])
                last.then_inc(tr_done, 1)


NH = 16
HS = DM // NH
NT = SEQ // P
TILES = NB * NT
KC = DM // P
NG = NH // 4
EPS = 1e-5
GW = 4 * SEQ
PREP = 8


def wait_reuse(eng, semaphore, value):
    if not isinstance(value, int) or value > 0:
        eng.wait_ge(semaphore, value)


def attention_phase(nc, h_dram, w_qkv, w_o, b_qkv, b_o, rope, ident, ident_b, mask_b, select_b, h_all):
    with ExitStack() as ctx:
        def sb(name, shape, dt=F32):
            return ctx.enter_context(nc.sbuf_tensor(name, shape, dt))

        def sem(name):
            return ctx.enter_context(nc.semaphore(name))

        idn = sb("at_ident", [P, P])
        idb = sb("at_ident_b", [P, P], BF16)
        maskb = sb("at_mask_b", [P, 4 * P], BF16)
        selb = sb("at_select_b", [P, NH, P], BF16)
        cs = sb("at_rope", [P, NT, 2, HS])
        bq = sb("at_b_qkv", [P, 3 * DM])
        bo = sb("at_b_o", [P, DM])
        w_in = sb("at_w_in", [P, KC, 4 * DM])
        w_hi = sb("at_w_hi", [P, KC, 4 * DM], F32R)
        w_lo = sb("at_w_lo", [P, KC, 4 * DM], F32R)
        xn = sb("at_xn", [P, NT, DM])
        stats = sb("at_stats", [P, TILES, 6])
        mv = sb("at_mv", [P, TILES, 2])
        rstd = sb("at_rstd", [P, TILES])
        vare = sb("at_vare", [P, TILES])
        mhalf = sb("at_mhalf", [P, TILES])
        x_hi = sb("at_x_hi", [P, KC, SEQ], F32R)
        x_lo = sb("at_x_lo", [P, KC, SEQ], F32R)
        qk = sb("at_qk", [P, NT, 2 * NH, HS])
        m1 = sb("at_m1", [P, NT, 2 * NH, HS])
        m2 = sb("at_m2", [P, NT, 2 * NH, HS])
        vx = [sb(f"at_v{i}", [P, NT, NH, 32]) for i in range(2)]
        st_q = sb("at_st_q", [P, NT, NH, 2, HS])
        st_ka = sb("at_st_ka", [P, NT, NH, 2, HS])
        st_kb = sb("at_st_kb", [P, NT, NH, 2, HS])
        qc = sb("at_qc", [P, NG, SEQ], F32R)
        ka = [sb(f"at_ka{i}", [P, NG, SEQ], F32R) for i in range(2)]
        kb = [sb(f"at_kb{i}", [P, NG, SEQ], F32R) for i in range(2)]
        qm = [sb(f"at_qm{i}", [P, NG, 4, SEQ], F32R) for i in range(2)]
        km = sb("at_km", [P, NG, 4, SEQ], F32R)
        cm = sb("at_cm", [P, NT, NH])
        cb = sb("at_cb", [P, NT, 2, NH], BF16)
        cz = sb("at_cz", [P, SEQ], BF16)
        pt = [sb(f"at_pt{i}", [P, 3 * 512]) for i in range(2)]
        ot = sb("at_ot", [P, NG, SEQ])
        rc = sb("at_rc", [P, NT, NH])
        yv = sb("at_y", [P, NT, DM])
        y_hi = sb("at_y_hi", [P, KC, SEQ], F32R)
        y_lo = sb("at_y_lo", [P, KC, SEQ], F32R)
        ps = ctx.enter_context(nc.psum_tensor("at_ps", [P, 8, 512], F32))

        const_in = sem("at_const_in")
        h_in = sem("at_h_in")
        w_split = sem("at_w_split")
        prep = sem("at_prep")
        dve = sem("at_dve")
        mean_var = sem("at_mean_var")
        rstd_done = sem("at_rstd_done")
        xn_done = sem("at_xn_done")
        xt_ps = sem("at_xt_ps")
        xhi_s = sem("at_xhi_s")
        xlo_s = sem("at_xlo_s")
        qk_ps = sem("at_qk_ps")
        v_ps = sem("at_v_ps")
        qk_v = sem("at_qk_v")
        v_v = sem("at_v_v")
        rot1 = sem("at_rot1")
        rot2 = sem("at_rot2")
        rot = sem("at_rot")
        st_hi = sem("at_st_hi")
        st_lo = sem("at_st_lo")
        hd_ps = sem("at_hd_ps")
        hd_q = sem("at_hd_q")
        hd_k = sem("at_hd_k")
        qm_in = sem("at_qm_in")
        km_in = sem("at_km_in")
        mx_ps = sem("at_mx_ps")
        mx_v = sem("at_mx_v")
        cb_v = sem("at_cb_v")
        cz_ps = sem("at_cz_ps")
        cz_a = sem("at_cz_a")
        sc_ps = sem("at_sc_ps")
        ex_a = sem("at_ex_a")
        ex_seen = sem("at_ex_seen")
        msk_g = sem("at_msk_g")
        pv_ps = sem("at_pv_ps")
        ot_a = sem("at_ot_a")
        ot_ps = sem("at_ot_ps")
        rc_v = sem("at_rc_v")
        y_v = sem("at_y_v")
        yt_ps = sem("at_yt_ps")
        yhi_s = sem("at_yhi_s")
        ylo_s = sem("at_ylo_s")
        o_ps = sem("at_o_ps")
        hb_g = sem("at_hb_g")
        o_v = sem("at_o_v")

        block = ctx.enter_context(nc.Block())

        SCORE, PV_BANK, WORK = 0, 4, 5
        UNITS = 3 * NG

        def steps(eng, step):
            step(-1, 1, True, False, False)
            step(0, 0, True, True, False)
            with eng.Fori(0, (NB - 2) // 2) as i:
                step(i * 2 + 1, 1, True, True, True)
                step(i * 2 + 2, 0, True, True, True)
            step(NB - 1, (NB - 1) % 2, False, True, True)
            step(NB, NB % 2, False, False, True)

        def flat(t):
            return t.rearrange("p a b -> p (a b)")

        @block.sync
        def _(sp):
            for b in range(NB):
                sp.dma_start(h_all[:, 2 * b:2 * b + 2, :],
                             h_dram[b].rearrange("(t p) l -> p t l", p=P)).then_inc(h_in, 16)
            for dst, src in ((idn[:], ident), (idb[:], ident_b), (maskb[:], mask_b), (cs[:], rope),
                             (selb[:], select_b),
                             (w_in[:, :, 0:3 * DM], w_qkv.rearrange("(k p) n -> p k n", p=P)),
                             (w_in[:, :, 3 * DM:], w_o.rearrange("(k p) n -> p k n", p=P)),
                             (bq[:], b_qkv.unsqueeze(0).to_broadcast([P, 3 * DM])),
                             (bo[:], b_o.unsqueeze(0).to_broadcast([P, DM]))):
                sp.dma_start(dst, src).then_inc(const_in, 16)
            sp.wait_ge(prep, PREP)

            def step(b, par, front, back, tail):
                if not front:
                    return
                f, new = b + 1, 1 - par
                for copied, count, out, src, landed in ((hd_k, 4, km, ka[new], km_in), (hd_q, 2, qm[new], qc, qm_in)):
                    sp.wait_ge(copied, count * f + count)
                    for j in range(4):
                        rows = slice(32 * j, 32 * j + 32)
                        sp.dma_start(out[rows, :, j, :].bitcast(F32), src[rows].bitcast(F32)).then_inc(landed, 16)

            steps(sp, step)

        @block.gpsimd
        def _(g):
            g.memset(mhalf[:], -0.5).then_inc(prep, 1)
            g.wait_ge(mean_var, 1)
            g.wait_ge(prep, 1)
            g.tensor_tensor(rstd[:], vare[:], mhalf[:], ALU.pow).then_inc(rstd_done, 1)
            g.memset(cz[:], 0.0).then_inc(prep, 1)
            g.memset(st_kb[:, :, :, 1, :], 0.0).then_inc(prep, 1)
            for t in vx:
                g.memset(t[:, :, :, HS:32], 1.0).then_inc(prep, 1)
            for t in qm + [km]:
                g.memset(t[:].bitcast(F32), 0.0).then_inc(prep, 1)
            g.wait_ge(const_in, 16 * 9)

            def step(b, par, front, back, tail):
                f = b + 1
                if front:
                    for t in range(NT):
                        g.wait_ge(qk_v, NT * f + t + 1)
                        sgn = cs[:, t, 1, :].rearrange("p (i e) -> p i e", e=2)
                        src = qk[:, t].rearrange("p h (i e) -> p h i e", e=2)
                        dst = m2[:, t].rearrange("p h (i e) -> p h i e", e=2)
                        for e in range(2):
                            g.tensor_tensor(dst[:, :, :, e], src[:, :, :, 1 - e],
                                            sgn[:, :, e].unsqueeze(1).to_broadcast([P, 2 * NH, HS // 2]),
                                            ALU.mult).then_inc(rot2, 1)
                    g.wait_ge(xn_done, NT * f + NT)
                    tok = h_all[:, bass.ds(NT * f, NT), :]
                    g.tensor_tensor(tok, tok, bo[:].unsqueeze(1).to_broadcast([P, NT, DM]), ALU.add).then_inc(hb_g, 1)
                if back:
                    for n in range(NG):
                        for banks, ofs, width in ((2, 0, SEQ), (3, GW, P)):
                            g.wait_ge(ex_a, UNITS * b + 3 * n + banks)
                            g.sem_inc(ex_seen, 1)
                            d = pt[n % 2][:, ofs:ofs + 4 * width].rearrange("p (h q) -> p h q", h=4)[:, :, 0:P]
                            g.affine_select(out=d, in_=d, compare_op=ALU.is_ge, fill=0.0, base=0,
                                            pattern=[[0, 4], [1, P]], channel_multiplier=-1).then_inc(msk_g, 1)

            steps(g, step)

        @block.scalar
        def _(act):
            act.wait_ge(const_in, 16 * 9)
            act.copy(w_hi[:], w_in[:]).then_inc(w_split, 1)

            def step(b, par, front, back, tail):
                f, z, new = b + 1, b - 1, 1 - par

                def copy_group(s, n):
                    act.wait_ge(pv_ps, NG * s + n + 1)
                    act.copy(ot[:, n, :], ps[:, PV_BANK, 0:SEQ]).then_inc(ot_a, 1)

                def stage(t):
                    act.wait_ge(rot, NT * f + t + 1)
                    q, k = m1[:, t, 0:NH, :], m1[:, t, NH:, :]
                    act.copy(st_q[:, t, :, 0, :].bitcast(F32R), q).then_inc(st_hi, 1)
                    act.copy(st_ka[:, t].bitcast(F32R), k.unsqueeze(2).to_broadcast([P, NH, 2, HS])).then_inc(st_hi, 1)

                def copy_k(t):
                    for i, dst in ((1, ka[new]), (2, kb[new])):
                        act.wait_ge(hd_ps, 6 * f + 3 * t + i + 1)
                        act.copy(dst[:, :, t * P:(t + 1) * P],
                                 ps[:, WORK + i].rearrange("p (g t) -> p g t", g=NG)).then_inc(hd_k, 1)

                def exponentials(n):
                    for c in range(3):
                        u = 3 * n + c
                        act.wait_ge(sc_ps, UNITS * b + u + 1)
                        if c == 0:
                            wait_reuse(act, pv_ps, NG * b + n - 1)
                        act.activation(pt[n % 2][:, c * 512:(c + 1) * 512], ps[:, SCORE + u % 4, :],
                                       ACT.Exp, scale=1.0 / math.sqrt(HS)).then_inc(ex_a, 1)

                if front:
                    act.wait_ge(xt_ps, f + 1)
                    act.copy(flat(x_hi[:]), ps[:, WORK, :]).then_inc(xhi_s, 1)
                if tail:
                    copy_group(z, NG - 1)
                if front:
                    stage(0)
                if tail:
                    act.wait_ge(yt_ps, z + 1)
                    act.copy(flat(y_hi[:]), ps[:, WORK + 1, :]).then_inc(yhi_s, 1)
                if back:
                    act.wait_ge(cz_ps, b + 1)
                    act.copy(cz[0:32, :], ps[0:32, PV_BANK, 0:P].bitcast(BF16)).then_inc(cz_a, 1)
                if front:
                    copy_k(0)
                    stage(1)
                if back:
                    exponentials(0)
                    exponentials(1)
                    copy_group(b, 0)
                if front:
                    copy_k(1)
                if back:
                    exponentials(2)
                    copy_group(b, 1)
                    exponentials(3)
                    copy_group(b, 2)

            steps(act, step)

        @block.vector
        def _(v):
            count = [0]

            def link(ins):
                count[0] += 1
                ins.then_inc(dve, 1)
                v.wait_ge(dve, count[0])

            for b in range(NB):
                v.wait_ge(h_in, 16 * NB)
                for t in range(NT):
                    ins = v.bn_stats(stats[:, 2 * b + t, :], h_all[:, 2 * b + t, :])
            link(ins)
            for n in range(TILES):
                ins = v.bn_aggr(mv[:, n, :], stats[:, n, :])
            link(ins)
            v.tensor_scalar(vare[:], mv[:, :, 1], EPS, None, ALU.add).then_inc(mean_var, 1)
            v.wait_ge(const_in, 16 * 9)
            v.wait_ge(w_split, 1)
            v.tensor_tensor(w_lo[:], w_in[:], w_hi[:].bitcast(F32), ALU.subtract).then_inc(w_split, 1)
            v.wait_ge(rstd_done, 1)
            v.wait_ge(prep, PREP)

            def normalise(s):
                for t in range(NT):
                    n = NT * s + t
                    ht = h_all[:, bass.ds(n, 1), :].rearrange("p o d -> p (o d)")
                    v.tensor_scalar(xn[:, t, :], ht, mv[:, bass.ds(n, 1), 0:1].rearrange("p o d -> p (o d)"),
                                    rstd[:, bass.ds(n, 1)], ALU.subtract, ALU.mult).then_inc(xn_done, 1)

            def step(b, par, front, back, tail):
                f, z, new = b + 1, b - 1, 1 - par

                def maxima(n):
                    for c in range(3):
                        u = 3 * n + c
                        v.wait_ge(mx_ps, UNITS * b + u + 1)
                        dst = cm[:, 0, 4 * n:4 * n + 4] if c == 0 else cm[:, 1, 4 * n + 2 * c - 2:4 * n + 2 * c]
                        v.tensor_reduce(dst, ps[:, SCORE + u % 4].rearrange("p (h k) -> p h k", h=4 if c == 0 else 2),
                                        AX_X, ALU.max).then_inc(mx_v, 1)

                def qkv_out(t):
                    v.wait_ge(qk_ps, NT * f + t + 1)
                    v.tensor_tensor(qk[:, t].rearrange("p h d -> p (h d)"), ps[:, WORK + (2 if t else 1), :],
                                    bq[:, 0:2 * DM], ALU.add).then_inc(qk_v, 1)
                    v.wait_ge(v_ps, NT * f + t + 1)
                    v.tensor_tensor(vx[new][:, t, :, 0:HS],
                                    ps[:, WORK + (0 if t else 2), 0:DM].rearrange("p (h d) -> p h d", h=NH),
                                    bq[:, 2 * DM:].rearrange("p (h d) -> p h d", h=NH), ALU.add).then_inc(v_v, 1)
                    v.wait_ge(qk_v, NT * f + t + 1)
                    v.tensor_tensor(m1[:, t], qk[:, t], cs[:, t, 0, :].unsqueeze(1).to_broadcast([P, 2 * NH, HS]),
                                    ALU.mult).then_inc(rot1, 1)

                def rotate(t):
                    v.wait_ge(rot1, NT * f + t + 1)
                    v.wait_ge(rot2, 4 * f + 2 * t + 2)
                    v.tensor_tensor(m1[:, t], m1[:, t], m2[:, t], ALU.add).then_inc(rot, 1)

                def stage_low(t):
                    v.wait_ge(st_hi, 4 * f + 2 * t + 2)
                    v.tensor_tensor(st_q[:, t, :, 1, :].bitcast(F32R), m1[:, t, 0:NH, :], st_q[:, t, :, 0, :],
                                    ALU.subtract).then_inc(st_lo, 1)
                    v.tensor_tensor(st_kb[:, t, :, 0, :].bitcast(F32R), m1[:, t, NH:, :], st_ka[:, t, :, 0, :],
                                    ALU.subtract).then_inc(st_lo, 1)

                def copy_q(t):
                    v.wait_ge(hd_ps, 6 * f + 3 * t + 1)
                    v.tensor_copy(qc[:, :, t * P:(t + 1) * P],
                                  ps[:, WORK].rearrange("p (g t) -> p g t", g=NG)).then_inc(hd_q, 1)

                if front:
                    normalise(f)
                if back:
                    maxima(0)
                if front:
                    v.wait_ge(xhi_s, f + 1)
                    v.tensor_tensor(flat(x_lo[:]), ps[:, WORK, :], flat(x_hi[:]).bitcast(F32),
                                    ALU.subtract).then_inc(xlo_s, 1)
                if back:
                    maxima(1)
                if front:
                    qkv_out(0)
                if tail:
                    for t in range(NT):
                        v.wait_ge(ot_ps, NT * z + t + 1)
                        acc = ps[:, WORK + t].rearrange("p (h d) -> p h d", h=NH)
                        v.reciprocal(rc[:, t], acc[:, :, HS]).then_inc(rc_v, 1)
                    for t in range(NT):
                        acc = ps[:, WORK + t].rearrange("p (h d) -> p h d", h=NH)
                        v.wait_ge(rc_v, NT * z + t + 1)
                        v.tensor_tensor(yv[:, t].rearrange("p (h d) -> p h d", h=NH), acc[:, :, 0:HS],
                                        rc[:, t].unsqueeze(2).to_broadcast([P, NH, HS]), ALU.mult).then_inc(y_v, 1)
                if back:
                    maxima(2)
                if front:
                    rotate(0)
                    qkv_out(1)
                if tail:
                    v.wait_ge(yhi_s, z + 1)
                    v.tensor_tensor(flat(y_lo[:]), ps[:, WORK + 1, :], flat(y_hi[:]).bitcast(F32),
                                    ALU.subtract).then_inc(ylo_s, 1)
                if front:
                    stage_low(0)
                if back:
                    maxima(3)
                    v.wait_ge(mx_v, UNITS * b + UNITS)
                    v.tensor_scalar(cb[:, :, 0, :], cm[:], -1.0, None, ALU.mult).then_inc(cb_v, 1)
                    v.wait_ge(cb_v, 2 * b + 1)
                    v.scalar_tensor_tensor(out=cb[:, :, 1, :], in0=cm[:], scalar=-1.0, in1=cb[:, :, 0, :],
                                           op0=ALU.mult, op1=ALU.subtract).then_inc(cb_v, 1)
                if tail:
                    v.wait_ge(o_ps, z + 1)
                    v.wait_ge(hb_g, z + 1)
                    tok = h_all[:, bass.ds(NT * z, NT), :]
                    v.tensor_tensor(tok, ps[:, WORK + 2, :].rearrange("p (t d) -> p t d", t=NT), tok,
                                    ALU.add).then_inc(o_v, 1)
                if front:
                    rotate(1)
                    copy_q(0)
                    stage_low(1)
                    copy_q(1)

            steps(v, step)

        @block.tensor
        def _(pe):
            def split_product(out, pairs):
                n = len(pairs)
                for i, (x, y) in enumerate(pairs):
                    last = pe.matmul(out, x, y, start=i == 0, stop=i == n - 1)
                return last

            pe.wait_ge(const_in, 16 * 9)
            pe.wait_ge(w_split, 2)
            pe.wait_ge(prep, PREP)

            def step(b, par, front, back, tail):
                f, z, old = b + 1, b - 1, 1 - par

                def turn_x():
                    pe.wait_ge(xn_done, NT * f + NT)
                    wait_reuse(pe, hd_q, 2 * b + 2)
                    for k in range(KC):
                        for t in range(NT):
                            last = pe.transpose(ps[:, WORK, k * SEQ + t * P:k * SEQ + (t + 1) * P],
                                                xn[:, t, k * P:(k + 1) * P], idn[:])
                    last.then_inc(xt_ps, 1)

                def qkv(t):
                    pe.wait_ge(xhi_s, f + 1)
                    pe.wait_ge(xlo_s, f + 1)
                    if t == 0:
                        wait_reuse(pe, hd_k, 4 * b + 4)
                    else:
                        pe.wait_ge(v_v, NT * f + 1)
                    rows = slice(t * P, (t + 1) * P)
                    for bank, n, cols, done in ((2 if t else 1, 512, slice(0, 2 * DM), qk_ps),
                                                (0 if t else 2, DM, slice(2 * DM, 3 * DM), v_ps)):
                        if t and bank == 0:
                            wait_reuse(pe, y_v, NT * z + 1)
                        split_product(ps[:, WORK + bank, 0:n],
                                      [(x[:, k, rows], w[:, k, cols]) for k in range(KC)
                                       for x, w in ((x_hi, w_hi), (x_hi, w_lo), (x_lo, w_hi))]).then_inc(done, 1)

                def heads(t):
                    pe.wait_ge(st_hi, 4 * f + 2 * t + 2)
                    pe.wait_ge(st_lo, 4 * f + 2 * t + 2)
                    for i, st in enumerate((st_q, st_ka, st_kb)):
                        if t == 0:
                            if i == 0:
                                pe.wait_ge(v_v, NT * f + 2)
                            elif i == 1:
                                wait_reuse(pe, ylo_s, z + 1)
                            else:
                                pe.wait_ge(qk_v, NT * f + 2)
                                wait_reuse(pe, o_v, z + 1)
                        elif i == 0:
                            pe.wait_ge(hd_q, 2 * f + 1)
                        else:
                            pe.wait_ge(hd_k, 4 * f + i)
                        for n in range(NG):
                            last = pe.transpose(ps[:, WORK + i, n * P:(n + 1) * P],
                                                st[:, t, 4 * n:4 * n + 4].rearrange("p h c d -> p (h c d)"), idn[:])
                        last.then_inc(hd_ps, 1)

                def score_bank(u):
                    n, c = u // 3, u % 3
                    out = ps[:, SCORE + u % 4, :]
                    if u < 4:
                        wait_reuse(pe, ex_a, UNITS * b - 3 + u)
                    else:
                        pe.wait_ge(mx_v, UNITS * b + u - 3)
                    if c == 0:
                        pe.matmul(out, qc[:, n, 0:P], km[:, n, :, 0:P], start=True, stop=False)
                        last = pe.matmul(out, idb[:], maskb[:], start=False, stop=True)
                    else:
                        pe.matmul(out, qc[:, n, P:SEQ], km[:, n, 2 * c - 2:2 * c, :], start=True, stop=False)
                        last = pe.matmul(out.rearrange("p (h k) -> p h k", h=2)[:, :, P:SEQ], idb[:],
                                         maskb[:, 0:2 * P].rearrange("p (h k) -> p h k", h=2), start=False, stop=True)
                    last.then_inc(mx_ps, 1)

                def maxima(n):
                    for c in range(3):
                        score_bank(3 * n + c)

                def scores(n):
                    for c in range(3):
                        u = 3 * n + c
                        if u >= 4:
                            pe.wait_ge(ex_a, UNITS * b + u - 3)
                        out = ps[:, SCORE + u % 4, :]
                        keys = slice(0, P) if c < 2 else slice(P, SEQ)
                        x = qm[par][:, n, 2 * c:2 * c + 2, :] if c < 2 else qm[par][:, n, :, P:SEQ]
                        heads_ = (2 * c, 2 * c + 1) if c < 2 else range(4)
                        width = SEQ if c < 2 else P
                        for i, j in enumerate(heads_):
                            pe.matmul(out[:, i * width:(i + 1) * width], selb[:, 4 * n + j, :],
                                      cz[:, SEQ - width:SEQ], start=i == 0, stop=False, skip_group_check=True)
                        pe.matmul(out, ka[par][:, n, keys], x, start=False, stop=False, skip_group_check=True)
                        pe.matmul(out, kb[par][:, n, keys], x, start=False, stop=True,
                                  skip_group_check=True).then_inc(sc_ps, 1)

                def weigh(s, vals, n):
                    pe.wait_ge(msk_g, 2 * NG * s + 2 * n + 2)
                    if n == 0:
                        pe.wait_ge(cz_a, s + 1)
                    else:
                        pe.wait_ge(ot_a, NG * s + n)
                    for t in range(NT):
                        width = SEQ if t == 0 else P
                        for j in range(4):
                            ofs = t * GW + j * width
                            last = pe.matmul(ps[32 * j:32 * j + 32, PV_BANK, SEQ - width:SEQ],
                                             vals[:, t, 4 * n + j, :], pt[n % 2][:, ofs:ofs + width],
                                             start=t == 0, stop=t == 1, skip_group_check=True)
                    last.then_inc(pv_ps, 1)

                if back:
                    pe.wait_ge(hd_q, 2 * b + 2)
                    pe.wait_ge(hd_k, 4 * b + 4)
                    pe.wait_ge(km_in, 64 * b + 64)
                    pe.wait_ge(qm_in, 64 * b + 64)
                    maxima(0)
                if front:
                    turn_x()
                if tail:
                    weigh(z, vx[old], NG - 1)
                if back:
                    maxima(1)
                if front:
                    qkv(0)
                if tail:
                    pe.wait_ge(ot_a, NG * z + NG)
                    if front:
                        pe.wait_ge(qk_v, NT * f + 1)
                    for t in range(NT):
                        for n in range(NG):
                            last = pe.transpose(ps[:, WORK + t, n * P:(n + 1) * P], ot[:, n, t * P:(t + 1) * P], idn[:])
                        last.then_inc(ot_ps, 1)
                if back:
                    maxima(2)
                if front:
                    qkv(1)
                if tail:
                    pe.wait_ge(y_v, NT * z + NT)
                    for k in range(KC):
                        for t in range(NT):
                            last = pe.transpose(ps[:, WORK + 1, k * SEQ + t * P:k * SEQ + (t + 1) * P],
                                                yv[:, t, k * P:(k + 1) * P], idn[:])
                    last.then_inc(yt_ps, 1)
                if back:
                    maxima(3)
                if tail:
                    pe.wait_ge(yhi_s, z + 1)
                    pe.wait_ge(ylo_s, z + 1)
                    if front:
                        pe.wait_ge(qk_v, NT * f + 2)
                    else:
                        pe.wait_ge(o_v, z)
                    for t in range(NT):
                        rows = slice(t * P, (t + 1) * P)
                        last = split_product(ps[:, WORK + 2, t * DM:(t + 1) * DM],
                                             [(x[:, k, rows], w[:, k, 3 * DM:]) for k in range(KC)
                                              for x, w in ((y_hi, w_hi), (y_hi, w_lo), (y_lo, w_hi))])
                    last.then_inc(o_ps, 1)
                if back:
                    pe.wait_ge(cb_v, b * 2 + 2)
                    wait_reuse(pe, ot_a, NG * b)
                    for t in range(NT):
                        last = pe.transpose(ps[0:32, PV_BANK, t * P // 2:(t + 1) * P // 2].bitcast(BF16),
                                            cb[:, t].rearrange("p c h -> p (c h)"), idb[:])
                    last.then_inc(cz_ps, 1)
                if front:
                    heads(0)
                if back:
                    pe.wait_ge(cz_a, b + 1)
                    scores(0)
                    scores(1)
                    weigh(b, vx[par], 0)
                if front:
                    heads(1)
                if back:
                    scores(2)
                    weigh(b, vx[par], 1)
                    scores(3)
                    weigh(b, vx[par], 2)

            steps(pe, step)


NE = 8
FF = 512
FC = FF // P
SLOT_TILES = (2 * NB * SEQ + NE * (P - 1)) // P
NSTEP = TILES + SLOT_TILES
TOK = NB * SEQ
BIG = 4.0
U32 = mybir.dt.uint32


def routing_phase(nc, h_all, h2_dram, slots_dram, router_w, router_b, ident, tri_b, rank8, tile_no,
                  w1_all, w2_all, w1, w2, pos_i, w_top, step_expert):
    with ExitStack() as ctx:
        def sb(name, shape, dt=F32):
            return ctx.enter_context(nc.sbuf_tensor(name, shape, dt))

        def sem(name):
            return ctx.enter_context(nc.semaphore(name))

        idn = sb("ro_ident", [P, P])
        tri = sb("ro_tri", [P, P], BF16)
        ones = sb("ro_ones", [P, P], BF16)
        rk = sb("ro_rank8", [P, NE])
        tno = sb("ro_tile_no", [P, SLOT_TILES])
        zero = sb("ro_zero", [P, DM])
        rw_in = sb("ro_rw_in", [P, KC, NE])
        rw_hi = sb("ro_rw_hi", [P, KC, NE], F32R)
        rw_lo = sb("ro_rw_lo", [P, KC, NE], F32R)
        rb = sb("ro_rb", [NE, 1])
        stats = sb("ro_stats", [P, TILES, 6])
        mv = sb("ro_mv", [P, TILES, 2])
        vare = sb("ro_vare", [P, TILES])
        rstd = sb("ro_rstd", [P, TILES])
        mhalf = sb("ro_mhalf", [P, TILES])
        xn = sb("ro_xn", [P, TILES, DM])
        x_hi = sb("ro_x_hi", [P, KC, 512], F32R)
        x_lo = sb("ro_x_lo", [P, KC, 512], F32R)
        lg_t = sb("ro_lg_t", [NE, 2, 512])
        S3 = [P, TILES, NE]
        pr, a3, b3, c3, oh1, oh2 = (sb(f"ro_m{i}", S3) for i in range(6))
        sel_b = sb("ro_sel_b", S3, BF16)
        s1 = sb("ro_s1", [P, TILES])
        s2 = sb("ro_s2", [P, TILES])
        e1, e2, e3 = (sb(f"ro_e{i}", [P, NE]) for i in range(3))
        ei = sb("ro_ei", [P, NE], I32)
        te = sb("ro_te", [P, SLOT_TILES, NE])
        tf = sb("ro_tf", [P, SLOT_TILES])
        pf = sb("ro_pf", [P, 2, TILES])
        wst = [sb(f"ro_wst{i}", [P, KC * FF]) for i in range(2)]
        ps = ctx.enter_context(nc.psum_tensor("ro_ps", [P, 8, 512], F32))

        const_in = sem("ro_const_in")
        w_in = [sem(f"ro_w_in{i}") for i in range(2)]
        w_hi_done = sem("ro_w_hi_done")
        w_lo_done = sem("ro_w_lo_done")
        prep = sem("ro_prep")
        dve = sem("ro_dve")
        mean_var = sem("ro_mean_var")
        rstd_done = sem("ro_rstd_done")
        xn_done = sem("ro_xn_done")
        stored = sem("ro_stored")
        xt_ps = sem("ro_xt_ps")
        xhi_s = sem("ro_xhi_s")
        xlo_s = sem("ro_xlo_s")
        rw_s = sem("ro_rw_s")
        lg_ps = sem("ro_lg_ps")
        lg_s = sem("ro_lg_s")
        lgt_ps = sem("ro_lgt_ps")
        sub_done = sem("ro_sub_done")
        exp_done = sem("ro_exp_done")
        sel_done = sem("ro_sel_done")
        rank_ps = sem("ro_rank_ps")
        pos_done = sem("ro_pos_done")
        scat = sem("ro_scat")

        block = ctx.enter_context(nc.Block())

        @block.sync
        def _(sp):
            for dst, src in ((idn[:], ident), (tri[:], tri_b), (rk[:], rank8.unsqueeze(0).to_broadcast([P, NE])),
                             (tno[:], tile_no.unsqueeze(0).to_broadcast([P, SLOT_TILES])),
                             (rw_in[:], router_w.rearrange("(k p) e -> p k e", p=P)),
                             (rb[:], router_b.unsqueeze(1))):
                sp.dma_start(dst, src).then_inc(const_in, 16)
            sp.dma_start(h2_dram.rearrange("(n p) d -> p n d", p=P), h_all[:]).then_inc(stored, 16)
            sp.wait_ge(prep, 1)
            sp.dma_start(slots_dram[TOK:, :].rearrange("(n p) d -> p n d", p=P),
                         zero[:].unsqueeze(1).to_broadcast([P, SLOT_TILES + 1, DM])).then_inc(stored, 16)
            sp.wait_ge(xn_done, TILES)
            sp.dma_start(slots_dram[0:TOK, :].rearrange("(n p) d -> p n d", p=P), xn[:]).then_inc(stored, 16)
            for n in range(2 * (NE + 1)):
                e, second = n // 2, n % 2
                if n >= 2:
                    sp.wait_ge(w_lo_done, n - 1)
                    sp.wait_ge(w_hi_done, n - 1)
                if second:
                    src = w2[e].rearrange("(k p) n -> p k n", p=P)
                    dst = wst[1][:, 0:FC * DM].rearrange("p (k n) -> p k n", k=FC)
                else:
                    src = w1[e].rearrange("(k p) n -> p k n", p=P)
                    dst = wst[0][:, 0:KC * FF].rearrange("p (k n) -> p k n", k=KC)
                sp.dma_start(dst, src).then_inc(w_in[second], 16)
            sp.wait_ge(stored, 48)

        def scatter(g):
            g.wait_ge(pos_done, 2)
            g.wait_ge(stored, 48)
            for n in range(TILES):
                for k in range(2):
                    g.indirect_dma_start(out=slots_dram, out_offset=bass.IndirectOffsetOnAxis(ap=pos_i[:, k, n:n + 1], axis=0),
                                         in_=xn[:, n, :], in_offset=None).then_inc(scat, 16)

        @block.gpsimd
        def _(g):
            g.memset(zero[:], 0.0).then_inc(prep, 1)
            g.memset(mhalf[:], -0.5).then_inc(prep, 1)
            g.memset(ones[:], 1.0).then_inc(prep, 1)
            g.wait_ge(mean_var, 1)
            g.wait_ge(prep, 2)
            g.tensor_tensor(rstd[:], vare[:], mhalf[:], ALU.pow).then_inc(rstd_done, 1)
            for n in range(2 * (NE + 1)):
                e, second = n // 2, n % 2
                if n == 10:
                    scatter(g)
                g.wait_ge(w_in[second], 16 * (n // 2 + 1))
                g.wait_ge(w_hi_done, n + 1)
                w, k = (w2_all, FC) if second else (w1_all, KC)
                g.tensor_tensor(w[:, e, :, 1], wst[second][:].rearrange("p (k n) -> p k n", k=k),
                                w[:, e, :, 0].bitcast(F32), ALU.subtract).then_inc(w_lo_done, 1)
            g.wait_ge(scat, 16 * 2 * TILES)

        @block.scalar
        def _(act):
            act.wait_ge(const_in, 16 * 6)
            act.copy(rw_hi[:], rw_in[:]).then_inc(rw_s, 1)
            for n in range(4):
                act.wait_ge(xt_ps, n + 1)
                if n >= 1:
                    act.wait_ge(lg_ps, n)
                for k in range(KC):
                    act.copy(x_hi[:, k, :], ps[:, 2 * (n % 2) + k, :]).then_inc(xhi_s, 1)
                act.wait_ge(lg_ps, n + 1)
                if n >= 2:
                    act.wait_ge(lgt_ps, n - 1)
                act.activation(lg_t[:, n % 2, :], ps[0:NE, 4 + n % 2, :], ACT.Identity,
                               bias=rb[:, 0:1]).then_inc(lg_s, 1)
            act.wait_ge(sub_done, 1)
            act.activation(pr[:], pr[:], ACT.Exp).then_inc(exp_done, 1)
            for n in range(2 * (NE + 1)):
                e, second = n // 2, n % 2
                act.wait_ge(w_in[second], 16 * (n // 2 + 1))
                w, k = (w2_all, FC) if second else (w1_all, KC)
                act.copy(w[:, e, :, 0], wst[second][:].rearrange("p (k n) -> p k n", k=k)).then_inc(w_hi_done, 1)

        @block.vector
        def _(v):
            count = [0]

            def link(ins):
                count[0] += 1
                ins.then_inc(dve, 1)
                v.wait_ge(dve, count[0])

            for n in range(TILES):
                ins = v.bn_stats(stats[:, n, :], h_all[:, n, :])
            link(ins)
            for n in range(TILES):
                ins = v.bn_aggr(mv[:, n, :], stats[:, n, :])
            link(ins)
            v.tensor_scalar(vare[:], mv[:, :, 1], EPS, None, ALU.add).then_inc(mean_var, 1)
            v.wait_ge(const_in, 16 * 6)
            v.wait_ge(rw_s, 1)
            v.tensor_tensor(rw_lo[:], rw_in[:], rw_hi[:].bitcast(F32), ALU.subtract).then_inc(rw_s, 1)
            v.wait_ge(rstd_done, 1)
            for n in range(TILES):
                v.tensor_scalar(xn[:, n, :], h_all[:, n, :], mv[:, n, 0:1], rstd[:, n:n + 1],
                                ALU.subtract, ALU.mult).then_inc(xn_done, 1)
            for n in range(4):
                v.wait_ge(xhi_s, KC * n + KC)
                if n >= 1:
                    v.wait_ge(lg_ps, n)
                for k in range(KC):
                    v.tensor_tensor(x_lo[:, k, :], ps[:, 2 * (n % 2) + k, :], x_hi[:, k, :].bitcast(F32),
                                    ALU.subtract).then_inc(xlo_s, 1)
            v.wait_ge(lgt_ps, 4)
            lg = ps[:, 6, 0:TILES * NE].rearrange("p (n e) -> p n e", e=NE)
            over = lambda s: s.unsqueeze(2).to_broadcast(S3)
            link(v.tensor_reduce(s1[:], lg, AX_X, ALU.max))
            v.tensor_tensor(pr[:], lg, over(s1[:]), ALU.subtract).then_inc(sub_done, 1)
            v.wait_ge(exp_done, 1)
            link(v.tensor_reduce(s1[:], pr[:], AX_X, ALU.add))
            link(v.reciprocal(s1[:], s1[:]))
            link(v.tensor_tensor(pr[:], pr[:], over(s1[:]), ALU.mult))
            rank = rk[:].unsqueeze(1).to_broadcast(S3)
            cur = pr
            for k, oh in enumerate((oh1, oh2)):
                top = w_top[:, k, :]
                link(v.tensor_reduce(top, cur[:], AX_X, ALU.max))
                link(v.tensor_tensor(b3[:], cur[:], over(top), ALU.is_equal))
                link(v.tensor_tensor(b3[:], b3[:], rank, ALU.mult))
                link(v.tensor_reduce(s2[:], b3[:], AX_X, ALU.max))
                link(v.tensor_tensor(oh[:], b3[:], over(s2[:]), ALU.is_equal))
                if k == 0:
                    link(v.scalar_tensor_tensor(out=a3[:], in0=oh[:], scalar=-BIG, in1=pr[:], op0=ALU.mult, op1=ALU.add))
                    cur = a3
            v.tensor_tensor(sel_b[:], oh1[:], oh2[:], ALU.add).then_inc(sel_done, 1)
            v.wait_ge(rank_ps, 1)
            within = ps[:, 6, 0:TILES * NE].rearrange("p (n e) -> p n e", e=NE)
            totals = ps[:, 7, 0:TILES * NE].rearrange("p (n e) -> p n e", e=NE)
            link(v.tensor_copy(a3[:], totals))
            src, dst = a3, b3
            for k in range(4):
                m = 1 << k
                v.tensor_copy(dst[:, 0:m], src[:, 0:m])
                link(v.tensor_tensor(dst[:, m:], src[:, m:], src[:, 0:TILES - m], ALU.add))
                src, dst = dst, (c3 if k == 0 else src)
            incl = src
            link(v.tensor_tensor(dst[:], incl[:], totals, ALU.subtract))
            link(v.tensor_tensor(dst[:], dst[:], within, ALU.add))
            ranks = dst
            link(v.tensor_scalar(ei[:], incl[:, TILES - 1, :], float(P - 1), None, ALU.add))
            link(v.tensor_scalar(ei[:], ei[:], 7, None, ALU.arith_shift_right))
            link(v.tensor_copy(e1[:], ei[:]))
            src, dst = e1, e2
            for k in range(3):
                m = 1 << k
                v.tensor_copy(dst[:, 0:m], src[:, 0:m])
                link(v.tensor_tensor(dst[:, m:], src[:, m:], src[:, 0:NE - m], ALU.add))
                src, dst = dst, (e3 if k == 0 else src)
            ends = src
            v.tensor_tensor(te[:], tno[:].unsqueeze(2).to_broadcast([P, SLOT_TILES, NE]),
                            ends[:].unsqueeze(1).to_broadcast([P, SLOT_TILES, NE]), ALU.is_ge)
            link(v.tensor_tensor(dst[:], ends[:], e1[:], ALU.subtract))
            link(v.tensor_reduce(tf[:], te[:], AX_X, ALU.add))
            v.memset(step_expert[:, 0:TILES], NE)
            v.tensor_scalar(step_expert[:, TILES:NSTEP], tf[:], float(NE - 1), None, ALU.min)
            link(v.tensor_scalar(dst[:], dst[:], float(P), float(TOK), ALU.mult, ALU.add))
            link(v.tensor_tensor(ranks[:], ranks[:], dst[:].unsqueeze(1).to_broadcast(S3), ALU.add))
            for k, oh in enumerate((oh1, oh2)):
                link(v.tensor_tensor(pr[:], oh[:], ranks[:], ALU.mult))
                link(v.tensor_reduce(pf[:, k, :], pr[:], AX_X, ALU.add))
                v.tensor_copy(pos_i[:, k, :], pf[:, k, :]).then_inc(pos_done, 1)

        @block.tensor
        def _(pe):
            pe.wait_ge(const_in, 16 * 6)
            pe.wait_ge(rw_s, 2)
            for n in range(4):
                pe.wait_ge(xn_done, 4 * n + 4)
                if n >= 2:
                    pe.wait_ge(xlo_s, KC * (n - 1))
                for k in range(KC):
                    for t in range(4):
                        last = pe.transpose(ps[:, 2 * (n % 2) + k, t * P:(t + 1) * P],
                                            xn[:, 4 * n + t, k * P:(k + 1) * P], idn[:])
                last.then_inc(xt_ps, 1)
                if n >= 2:
                    pe.wait_ge(lg_s, n - 1)
                pe.wait_ge(xhi_s, KC * n + KC)
                pe.wait_ge(xlo_s, KC * n + KC)
                pairs = [(x[:, k, :], w[:, k, :]) for k in range(KC)
                         for x, w in ((rw_hi, x_hi), (rw_hi, x_lo), (rw_lo, x_hi))]
                for i, (x, w) in enumerate(pairs):
                    last = pe.matmul(ps[0:NE, 4 + n % 2, :], x, w, start=i == 0, stop=i == 5)
                last.then_inc(lg_ps, 1)
                pe.wait_ge(lg_s, n + 1)
                for t in range(4):
                    m = 4 * n + t
                    last = pe.transpose(ps[:, 6, m * NE:(m + 1) * NE], lg_t[:, n % 2, t * P:(t + 1) * P],
                                        idn[0:NE, 0:NE])
                last.then_inc(lgt_ps, 1)
            pe.wait_ge(sel_done, 1)
            pe.wait_ge(prep, 3)
            sel = sel_b[:].rearrange("p n e -> p (n e)")
            pe.matmul(ps[:, 6, 0:TILES * NE], tri[:], sel, start=True, stop=True)
            pe.matmul(ps[:, 7, 0:TILES * NE], ones[:], sel, start=True, stop=True).then_inc(rank_ps, 1)


def expert_phase(nc, slots_dram, y_dram, b1_all, b2_all, ident, w1_all, w2_all, step_expert):
    with ExitStack() as ctx:
        def sb(name, shape, dt=F32):
            return ctx.enter_context(nc.sbuf_tensor(name, shape, dt))

        def sem(name):
            return ctx.enter_context(nc.semaphore(name))

        idn = sb("ex_ident", [P, P])
        b1 = sb("ex_b1", [P, NE + 1, FF])
        b2 = sb("ex_b2", [P, NE + 1, DM])
        xin = [sb(f"ex_xin{i}", [P, DM]) for i in range(2)]
        x_hi = [sb(f"ex_x_hi{i}", [P, DM], F32R) for i in range(2)]
        x_lo = [sb(f"ex_x_lo{i}", [P, DM], F32R) for i in range(2)]
        hb = [sb(f"ex_hb{i}", [P, FF]) for i in range(2)]
        h_hi = [sb(f"ex_h_hi{i}", [P, FF], F32R) for i in range(2)]
        h_lo = [sb(f"ex_h_lo{i}", [P, FF], F32R) for i in range(2)]
        yo = [sb(f"ex_y{i}", [P, DM]) for i in range(2)]
        ps = ctx.enter_context(nc.psum_tensor("ex_ps", [P, 8, 512], F32))

        const_in = sem("ex_const_in")
        x_in = [sem(f"ex_x_in{i}") for i in range(2)]
        y_out = [sem(f"ex_y_out{i}") for i in range(2)]
        xt_ps = sem("ex_xt_ps")
        xhi_s = sem("ex_xhi_s")
        xlo_s = sem("ex_xlo_s")
        h_ps = sem("ex_h_ps")
        hb_v = sem("ex_hb_v")
        gelu_a = sem("ex_gelu_a")
        ht_ps = sem("ex_ht_ps")
        hhi_a = sem("ex_hhi_a")
        hlo_v = sem("ex_hlo_v")
        y_ps = sem("ex_y_ps")
        y_b = sem("ex_y_b")
        y_v = sem("ex_y_v")

        block = ctx.enter_context(nc.Block())
        PAIRS = (NSTEP - 1) // 2
        assert NSTEP == 1 + 2 * PAIRS

        def in_pairs(eng, body):
            body(1, 1, 0)
            body(2, 0, 1)
            with eng.Fori(1, PAIRS) as n:
                body(n * 2 + 1, 1, n)
                body(n * 2 + 2, 0, n + 1)

        def rows(i):
            return bass.ds(i * P, P)

        def expert_of(eng, i):
            at = slice(i, i + 1) if isinstance(i, int) else bass.ds(i, 1)
            return eng.value_load(step_expert[0:1, at], min_val=0, max_val=NE)

        @block.sync
        def _(sp):
            sp.dma_start(idn[:], ident).then_inc(const_in, 16)
            sp.dma_start(b1[:], b1_all.unsqueeze(0).to_broadcast([P, NE + 1, FF])).then_inc(const_in, 16)
            sp.dma_start(b2[:], b2_all.unsqueeze(0).to_broadcast([P, NE + 1, DM])).then_inc(const_in, 16)
            sp.dma_start(xin[0][:], slots_dram[0:P, :]).then_inc(x_in[0], 16)
            sp.dma_start(xin[1][:], slots_dram[P:2 * P, :]).then_inc(x_in[1], 16)

            def step(i, par, k):
                sp.wait_ge(xt_ps, i)
                sp.dma_start(xin[1 - par][:], slots_dram[rows(i + 1), :]).then_inc(x_in[1 - par], 16)

            in_pairs(sp, step)

        @block.gpsimd
        def _(g):
            def step(i, par, k):
                g.wait_ge(y_v, i)
                g.dma_start(y_dram[rows(i - 1), :], yo[1 - par][:]).then_inc(y_out[1 - par], 16)

            in_pairs(g, step)
            g.wait_ge(y_v, NSTEP)
            g.dma_start(y_dram[(NSTEP - 1) * P:NSTEP * P, :], yo[0][:]).then_inc(y_out[0], 16)
            g.wait_ge(y_out[0], 16 * (PAIRS + 1))
            g.wait_ge(y_out[1], 16 * PAIRS)

        @block.tensor
        def _(pe):
            def turn_x(i, par, k):
                pe.wait_ge(x_in[par], 16 * k + 16)
                for c in range(KC):
                    last = pe.transpose(ps[:, 6 + par, c * P:(c + 1) * P], xin[par][:, c * P:(c + 1) * P], idn[:])
                last.then_inc(xt_ps, 1)

            def first_layer(i, par, free=None):
                e = expert_of(pe, i)
                if free is not None:
                    wait_reuse(pe, hb_v, free)
                pe.wait_ge(xhi_s, i + 1)
                pe.wait_ge(xlo_s, i + 1)
                pairs = [(x[par][:, c * P:(c + 1) * P], w1_all[:, bass.ds(e, 1), c, part, :].rearrange("p o n -> p (o n)"))
                         for c in range(KC) for x, part in ((x_hi, 0), (x_hi, 1), (x_lo, 0))]
                for n, (x, w) in enumerate(pairs):
                    last = pe.matmul(ps[:, par, :], x, w, start=n == 0, stop=n == len(pairs) - 1)
                last.then_inc(h_ps, 1)

            def turn_h(i, par):
                pe.wait_ge(gelu_a, i + 1)
                for c in range(FC):
                    last = pe.transpose(ps[:, 2 + par, c * P:(c + 1) * P], hb[par][:, c * P:(c + 1) * P], idn[:])
                last.then_inc(ht_ps, 1)

            def second_layer(i, par, free=None):
                e = expert_of(pe, i)
                if free is not None:
                    wait_reuse(pe, y_v, free)
                pe.wait_ge(hhi_a, i + 1)
                pe.wait_ge(hlo_v, i + 1)
                for c in range(FC):
                    w = w2_all[:, bass.ds(e, 1), c]
                    pe.matmul(ps[:, 4 + par, :], h_hi[par][:, c * P:(c + 1) * P],
                              w.rearrange("p o s n -> p (o s n)"), start=c == 0, stop=False, skip_group_check=True)
                    last = pe.matmul(ps[:, 4 + par, 0:DM], h_lo[par][:, c * P:(c + 1) * P],
                                     w[:, :, 0, :].rearrange("p o n -> p (o n)"),
                                     start=False, stop=c == FC - 1, skip_group_check=True)
                last.then_inc(y_ps, 1)

            pe.wait_ge(const_in, 48)
            turn_x(0, 0, 0)
            first_layer(0, 0)
            turn_x(1, 1, 0)
            turn_h(0, 0)

            def step(i, par, k):
                first_layer(i, par, i - 1)
                pe.wait_ge(xlo_s, i)
                turn_x(i + 1, 1 - par, k + par)
                second_layer(i - 1, 1 - par, i - 1)
                wait_reuse(pe, hlo_v, i - 1)
                turn_h(i, par)

            in_pairs(pe, step)
            second_layer(NSTEP - 1, 0, NSTEP - 1)

        @block.scalar
        def _(act):
            def x_high(i, par):
                act.wait_ge(xt_ps, i + 1)
                act.copy(x_hi[par][:], ps[:, 6 + par, 0:DM]).then_inc(xhi_s, 1)

            def gelu(i, par):
                act.wait_ge(hb_v, i + 1)
                act.activation(hb[par][:], hb[par][:], ACT.Gelu).then_inc(gelu_a, 1)

            def h_high(i, par):
                act.wait_ge(ht_ps, i + 1)
                act.copy(h_hi[par][:], ps[:, 2 + par, :]).then_inc(hhi_a, 1)

            x_high(0, 0)
            x_high(1, 1)
            gelu(0, 0)
            h_high(0, 0)

            def step(i, par, k):
                act.wait_ge(h_ps, i)
                x_high(i + 1, 1 - par)
                gelu(i, par)
                wait_reuse(act, y_ps, i - 1)
                h_high(i, par)

            in_pairs(act, step)

        @block.vector
        def _(v):
            def bias(b, i):
                return b[:, bass.ds(expert_of(v, i), 1), :].rearrange("p o n -> p (o n)")

            def x_low(i, par):
                v.wait_ge(xhi_s, i + 1)
                v.tensor_tensor(x_lo[par][:], ps[:, 6 + par, 0:DM], x_hi[par][:].bitcast(F32),
                                ALU.subtract).then_inc(xlo_s, 1)

            def h_bias(i, par, turned=None):
                b = bias(b1, i)
                if turned is not None:
                    wait_reuse(v, ht_ps, turned)
                v.wait_ge(h_ps, i + 1)
                v.tensor_tensor(hb[par][:], ps[:, par, :], b, ALU.add).then_inc(hb_v, 1)

            def h_low(i, par):
                v.wait_ge(hhi_a, i + 1)
                v.tensor_tensor(h_lo[par][:], ps[:, 2 + par, :], h_hi[par][:].bitcast(F32),
                                ALU.subtract).then_inc(hlo_v, 1)

            def y_bias(i, par, stored=None):
                b = bias(b2, i)
                if stored is not None:
                    wait_reuse(v, y_out[par], stored)
                v.wait_ge(y_ps, i + 1)
                v.tensor_tensor(yo[par][:], ps[:, 4 + par, DM:], b, ALU.add).then_inc(y_b, 1)
                v.wait_ge(y_b, i + 1)
                v.tensor_tensor(yo[par][:], ps[:, 4 + par, 0:DM], yo[par][:], ALU.add).then_inc(y_v, 1)

            v.wait_ge(const_in, 48)
            x_low(0, 0)
            h_bias(0, 0)
            x_low(1, 1)
            h_low(0, 0)

            def step(i, par, k):
                h_bias(i, par, i - 1)
                v.wait_ge(h_ps, i)
                x_low(i + 1, 1 - par)
                y_bias(i - 1, 1 - par, k * 16 - (0 if par else 16))
                wait_reuse(v, y_ps, i - 1)
                h_low(i, par)

            in_pairs(v, step)
            y_bias(NSTEP - 1, 0, PAIRS * 16)


def combine_phase(nc, h2_dram, y_dram, pos_i, w_top, out):
    with ExitStack() as ctx:
        def sb(name, n):
            return [ctx.enter_context(nc.sbuf_tensor(f"co_{name}{i}", [P, DM], F32)) for i in range(n)]

        BUF = 4
        hh, ys, ya, yb = sb("h", BUF), sb("ys", BUF), sb("ya", BUF), sb("yb", BUF)
        load = [ctx.enter_context(nc.semaphore(f"co_load{i}")) for i in range(BUF)]
        gath = [ctx.enter_context(nc.semaphore(f"co_gather{i}")) for i in range(BUF)]
        store = [ctx.enter_context(nc.semaphore(f"co_store{i}")) for i in range(BUF)]
        added = ctx.enter_context(nc.semaphore("co_added"))
        block = ctx.enter_context(nc.Block())
        tok = out.rearrange("b t d -> (b t) d")

        @block.sync
        def _(sp):
            for n in range(TILES):
                if n >= BUF:
                    sp.wait_ge(store[n % BUF], 16 * (n // BUF))
                rows = slice(n * P, (n + 1) * P)
                sp.dma_start(hh[n % BUF][:], h2_dram[rows, :]).then_inc(load[n % BUF], 16)
                sp.dma_start(ys[n % BUF][:], y_dram[rows, :]).then_inc(load[n % BUF], 16)

        @block.gpsimd
        def _(g):
            for n in range(TILES):
                if n >= BUF:
                    g.wait_ge(added, 3 * (n - BUF + 1))
                for k, dst in enumerate((ya, yb)):
                    g.indirect_dma_start(out=dst[n % BUF][:], out_offset=None, in_=y_dram,
                                         in_offset=bass.IndirectOffsetOnAxis(ap=pos_i[:, k, n:n + 1], axis=0)
                                         ).then_inc(gath[n % BUF], 16)

        @block.scalar
        def _(act):
            for n in range(TILES):
                act.wait_ge(added, 3 * n + 3)
                act.dma_start(tok[n * P:(n + 1) * P, :], hh[n % BUF][:]).then_inc(store[n % BUF], 16)
            for i in range(BUF):
                act.wait_ge(store[i], 16 * (TILES // BUF))

        @block.vector
        def _(v):
            for n in range(TILES):
                i = n % BUF
                v.wait_ge(load[i], 32 * (n // BUF + 1))
                v.tensor_tensor(hh[i][:], hh[i][:], ys[i][:], ALU.add).then_inc(added, 1)
                v.wait_ge(added, 3 * n + 1)
                v.wait_ge(gath[i], 32 * (n // BUF + 1))
                v.scalar_tensor_tensor(out=hh[i][:], in0=ya[i][:], scalar=w_top[:, 0, n:n + 1], in1=hh[i][:],
                                       op0=ALU.mult, op1=ALU.add).then_inc(added, 1)
                v.wait_ge(added, 3 * n + 2)
                v.scalar_tensor_tensor(out=hh[i][:], in0=yb[i][:], scalar=w_top[:, 1, n:n + 1], in1=hh[i][:],
                                       op0=ALU.mult, op1=ALU.add).then_inc(added, 1)


def tower_kernel(nc, x_t, a_real_t, a_imag_t, b_t, log_dt, w_qkv, b_qkv, w_o, b_o, router_w, router_b,
                 sw1, sw2, rw1, rw2, b1_all, b2_all, rope, ident, ident_b, mask_b, select_b, tri_b,
                 rank8, tile_no, out):
    h_dram = nc.dram_tensor("h_scratch", (NB, SEQ, DM), F32, kind="Internal").ap()
    h2_dram = nc.dram_tensor("h2_scratch", (TOK, DM), F32, kind="Internal").ap()
    slots_dram = nc.dram_tensor("slots_scratch", ((NSTEP + 1) * P, DM), F32, kind="Internal").ap()
    y_dram = nc.dram_tensor("y_scratch", (NSTEP * P, DM), F32, kind="Internal").ap()
    w1 = [rw1[e] for e in range(NE)] + [sw1]
    w2 = [rw2[e] for e in range(NE)] + [sw2]

    s4d_phase(nc, x_t, a_real_t, a_imag_t, b_t, log_dt, ident, h_dram)
    with ExitStack() as ctx:
        def sb(name, shape, dt=F32):
            return ctx.enter_context(nc.sbuf_tensor(name, shape, dt))

        pos_i = sb("pos_i", [P, 2, TILES], U32)
        w_top = sb("w_top", [P, 2, TILES])
        step_expert = sb("step_expert", [P, NSTEP], I32)
        with ExitStack() as early:
            h_all = early.enter_context(nc.sbuf_tensor("h_all", [P, TILES, DM], F32, side="right"))
            attention_phase(nc, h_dram, w_qkv, w_o, b_qkv, b_o, rope, ident, ident_b, mask_b, select_b, h_all)
            w1_all = sb("w1_all", [P, NE + 1, KC, 2, FF], F32R)
            w2_all = sb("w2_all", [P, NE + 1, FC, 2, DM], F32R)
            routing_phase(nc, h_all, h2_dram, slots_dram, router_w, router_b, ident, tri_b, rank8, tile_no,
                          w1_all, w2_all, w1, w2, pos_i, w_top, step_expert)
        expert_phase(nc, slots_dram, y_dram, b1_all, b2_all, ident, w1_all, w2_all, step_expert)
        combine_phase(nc, h2_dram, y_dram, pos_i, w_top, out)


def kernel(**inputs):
    import ml_dtypes
    import numpy as np
    import concourse.bacc as bacc
    from concourse.bass_utils import run_bass_kernel_spmd

    def channels(a):
        return a.reshape(4, SEQ // 4, *a.shape[1:]).swapaxes(0, 1).reshape(a.shape)

    i = {name: np.asarray(a) for name, a in inputs.items()}
    bf16 = ml_dtypes.bfloat16
    freq = 1.0 / 1000.0 ** (np.arange(0, HS, 2, dtype=np.float32) / HS)
    angle = np.arange(SEQ, dtype=np.float32)[:, None] * freq[None]
    rope = np.empty((SEQ, 2, HS), np.float32)
    rope[:, 0, 0::2] = rope[:, 0, 1::2] = np.cos(angle)
    rope[:, 1, 0::2] = -np.sin(angle)
    rope[:, 1, 1::2] = np.sin(angle)
    causal = np.triu(np.full((P, P), -1e30, np.float32), 1)
    select = np.zeros((P, NH, P), np.float32)
    for h in range(NH):
        select[[h, NH + h], h] = 1.0
    arrays = dict(
        x_t=channels(i["x"].transpose(1, 2, 3, 0)).transpose(1, 2, 0, 3),
        a_real_t=channels(i["L0_tok_inv_A_real"]).T,
        a_imag_t=channels(i["L0_tok_A_imag"]).T,
        b_t=channels(i["L0_tok_B_ri"]).transpose(1, 2, 0),
        log_dt=channels(i["L0_tok_log_dt"]),
        w_qkv=i["L0_attn_W_attn"].T, b_qkv=i["L0_attn_b_attn"],
        w_o=i["L0_attn_W_o"].T, b_o=i["L0_attn_b_o"],
        router_w=i["L0_ffn_router_w"], router_b=i["L0_ffn_router_b"],
        sw1=i["L0_ffn_sw1"], sw2=i["L0_ffn_sw2"], rw1=i["L0_ffn_rw1"], rw2=i["L0_ffn_rw2"],
        b1_all=np.concatenate([i["L0_ffn_rb1"], i["L0_ffn_sb1"][None]]),
        b2_all=np.concatenate([i["L0_ffn_rb2"], i["L0_ffn_sb2"][None]]),
        rope=rope.reshape(NT, P, 2, HS).transpose(1, 0, 2, 3),
        ident=np.eye(P, dtype=np.float32), ident_b=np.eye(P).astype(bf16),
        mask_b=np.tile(causal, (1, 4)).astype(bf16), select_b=select.astype(bf16),
        tri_b=np.triu(np.ones((P, P)), 1).astype(bf16),
        rank8=(NE - np.arange(NE)).astype(np.float32),
        tile_no=np.arange(SLOT_TILES).astype(np.float32))
    arrays = {f"in_{name}": np.ascontiguousarray(a) for name, a in arrays.items()}

    nc = bacc.Bacc("TRN2", target_bir_lowering=False, num_devices=1)
    args = [nc.dram_tensor(name, a.shape, mybir.dt.from_np(a.dtype), kind="ExternalInput").ap()
            for name, a in arrays.items()]
    out = nc.dram_tensor("out", (NB, SEQ, DM), F32, kind="ExternalOutput").ap()
    tower_kernel(nc, *args, out)
    result = run_bass_kernel_spmd(nc, [arrays], core_ids=[0])
    return result.results[0]["out"]
```

```python
import math
from contextlib import ExitStack

import concourse.bass as bass
from concourse import mybir

F32 = mybir.dt.float32
F32R = mybir.dt.float32r
BF16 = mybir.dt.bfloat16
I32 = mybir.dt.int32
ALU = mybir.AluOpType
ACT = mybir.ActivationFunctionType
AX_X = mybir.AxisListType.X

P = 128
NB = 8
SEQ = 256
DM = 256
L0 = 32
L1 = DM // L0
CHUNK = 32
NCHUNK = SEQ // CHUNK
QUADS = CHUNK // 4
AHEAD = 2

LOG2E = 1.0 / math.log(2.0)
LN2_HI = 355.0 / 512.0
LN2_LO = math.log(2.0) - LN2_HI


def s4d_phase(nc, x_t, a_real_t, a_imag_t, b_t, log_dt, ident, w_qkv, w_o, idn, w_in, h_all):
    HALF = P // 2
    with ExitStack() as ctx:
        def sb(name, shape, dt=F32):
            return ctx.enter_context(nc.sbuf_tensor(name, shape, dt))

        def sem(name):
            return ctx.enter_context(nc.semaphore(name))

        c_re = sb("s4_c_re", [P, SEQ, NB])
        c_im = sb("s4_c_im", [P, SEQ, NB])
        logs = sb("s4_logs", [P, 2, SEQ])
        aimag = sb("s4_aimag", [P, SEQ])
        tmp = [sb(f"s4_tmp{i}", [P, SEQ]) for i in range(4)]
        b_r = sb("s4_b_r", [P, SEQ])
        b_i = sb("s4_b_i", [P, SEQ])
        zr = sb("s4_zr", [P, 8, SEQ])
        zi = sb("s4_zi", [P, 8, SEQ])
        u = sb("s4_u", [P, SEQ, 16])
        w = sb("s4_w", [P, SEQ, 16])
        p1 = sb("s4_p1", [P, SEQ, L1])
        p2 = sb("s4_p2", [P, SEQ, L1])
        t_dve = [sb(f"s4_tdve{i}", [P, 2 * CHUNK * 8]) for i in range(4)]
        t_pool = [sb(f"s4_tpool{i}", [P, 2 * CHUNK * 4]) for i in range(4)]
        t_fin = [sb(f"s4_tfin{i}", [P, CHUNK, 16]) for i in range(2)]
        zc = [sb(f"s4_zc{i}", [P, CHUNK, L0]) for i in range(2)]
        a_re = [sb(f"s4_a_re{i}", [P, CHUNK, NB, L1]) for i in range(2)]
        a_im = [sb(f"s4_a_im{i}", [P, CHUNK, NB, L1]) for i in range(2)]
        ex = [a_re[0][:].rearrange("p h b l -> p (h b l)")[:, i * 2 * SEQ:(i + 1) * 2 * SEQ]
              .rearrange("p (c h) -> p c h", c=2) for i in range(4)]
        ex_int = ex.pop().bitcast(I32)
        k_sb = sb("s4_k", [P, NB // 2, L1, 2, SEQ // 4])
        ps = [ctx.enter_context(nc.psum_tensor(f"s4_ps{i}", [P, 512], F32)) for i in range(8)]

        par_in = sem("s4_par_in")
        log_in = sem("s4_log_in")
        x_in = sem("s4_x_in")
        idn_in = sem("s4_idn_in")
        w_landed = sem("s4_w_landed")
        dve = sem("s4_dve")
        pool = sem("s4_pool")
        squares = sem("s4_squares")
        b_ready = sem("s4_b_ready")
        u_done = sem("s4_u_done")
        p_done = sem("s4_p_done")
        z_low = sem("s4_z_low")
        z_high = sem("s4_z_high")
        are_done = sem("s4_are_done")
        aim_done = sem("s4_aim_done")
        mm_done = sem("s4_mm_done")
        k_done = sem("s4_k_done")
        tr_done = sem("s4_tr_done")
        h_v = sem("s4_h_v")
        h_a = sem("s4_h_a")

        block = ctx.enter_context(nc.Block())

        def bank_out(copy, n, done):
            bp, g = n // 2, n % 2
            h_tiles = h_all[:, :, g * 128:(g + 1) * 128].rearrange("p (b t) (k l) -> p b k t l", t=2, l=32)
            for s in range(2):
                for odd in range(2):
                    src = ps[n][HALF * s:HALF * (s + 1)].rearrange("p (k t o l) -> p k t o l", k=4, t=2, o=2)
                    last = copy(h_tiles[HALF * odd:HALF * (odd + 1), 2 * bp + s], src[:, :, :, odd])
            last.then_inc(done, 1)

        @block.sync
        def _(sp):
            sp.dma_start(logs[:, 0], log_dt.unsqueeze(0).to_broadcast([P, SEQ])).then_inc(log_in, 16)
            for d in range(2):
                rows = slice(HALF * d, HALF * (d + 1))
                sp.dma_start(logs[rows, 1], a_real_t).then_inc(log_in, 16)
            for d in range(2):
                rows = slice(HALF * d, HALF * (d + 1))
                sp.dma_start(b_r[rows, :], b_t[:, d]).then_inc(par_in, 16)
                sp.dma_start(b_i[rows, :], b_t[:, 1 - d]).then_inc(par_in, 16)
                sp.dma_start(aimag[rows, :], a_imag_t).then_inc(par_in, 16)
            for d in range(2):
                rows = slice(HALF * d, HALF * (d + 1))
                sp.dma_start(c_re[rows], x_t[:, 0]).then_inc(x_in, 16)
                sp.dma_start(c_im[rows], x_t[:, 1]).then_inc(x_in, 16)
            sp.dma_start(idn[:], ident).then_inc(idn_in, 16)
            sp.dma_start(w_in[:, :, 0:3 * DM], w_qkv.rearrange("(k p) n -> p k n", p=P)).then_inc(w_landed, 16)
            sp.dma_start(w_in[:, :, 3 * DM:], w_o.rearrange("(k p) n -> p k n", p=P)).then_inc(w_landed, 16)
            sp.wait_ge(w_landed, 32)

        @block.scalar
        def _(act):
            act.sem_inc(k_done, 2 * AHEAD)

            def z_copy(c, half):
                act.copy(zc[half][:, :, 0:16], u[:, bass.ds(c * CHUNK, CHUNK), :]).then_inc(z_low, 1)

            def k_copy(c, half):
                src = ps[half][:].rearrange("p (q b s l) -> p q b s l", q=QUADS, s=2, l=L1)
                for s in range(2):
                    dst = k_sb[:, :, :, s, bass.ds(c * QUADS, QUADS)].rearrange("p b l q -> p q b l")
                    act.copy(dst, src[:, :, :, s, :]).then_inc(k_done, 1)

            act.wait_ge(u_done, 1)
            z_copy(0, 0)
            z_copy(1, 1)
            with act.Fori(0, NCHUNK // 2 - 1) as i:
                for half in range(2):
                    c = i * 2 + half
                    act.wait_ge(mm_done, c + 1 + AHEAD)
                    act.wait_ge(u_done, i + 2)
                    z_copy(c + 2, half)
                    k_copy(c, half)
            for half in range(2):
                c = NCHUNK - 2 + half
                act.wait_ge(mm_done, c + 1 + AHEAD)
                k_copy(c, half)
            for n in range(1, 8, 2):
                act.wait_ge(tr_done, n + 1)
                bank_out(act.copy, n, h_a)

        @block.vector
        def _(v):
            count = [0]

            def link(ins):
                count[0] += 1
                ins.then_inc(dve, 1)
                v.wait_ge(dve, count[0])

            hdt, xr, y, t = tmp
            one_x, n2 = t_dve[0][:, 0:SEQ], t_dve[1][:, 0:SEQ]
            v.memset(u[0:HALF, :, 0:1], 1.0)
            v.memset(u[HALF:P, :, 0:1], 0.0)
            v.memset(w[0:HALF, :, 0:1], 0.0)
            link(v.memset(w[HALF:P, :, 0:1], 1.0))
            v.wait_ge(log_in, 16 * 3)
            x_, r_, e_ = ex
            link(v.tensor_scalar(x_, logs[:], -87.0, 88.0, ALU.max, ALU.min))
            link(v.tensor_scalar(ex_int, x_, LOG2E, None, ALU.mult))
            link(v.tensor_copy(e_, ex_int))
            link(v.scalar_tensor_tensor(out=r_, in0=e_, scalar=-LN2_HI, in1=x_,
                                        op0=ALU.mult, op1=ALU.add))
            link(v.scalar_tensor_tensor(out=r_, in0=e_, scalar=-LN2_LO, in1=r_,
                                        op0=ALU.mult, op1=ALU.add))
            v.tensor_scalar(ex_int, e_, 127.0, float(1 << 23), ALU.add, ALU.mult)
            link(v.tensor_scalar(x_, r_, 1.0 / math.factorial(7), None, ALU.mult))
            for k in range(6, 0, -1):
                link(v.scalar_tensor_tensor(out=x_, in0=x_, scalar=1.0 / math.factorial(k), in1=r_,
                                            op0=ALU.add, op1=ALU.mult))
            link(v.scalar_tensor_tensor(out=x_, in0=x_, scalar=1.0, in1=ex_int.bitcast(F32),
                                        op0=ALU.add, op1=ALU.mult))
            dt_, areal = x_[:, 0], x_[:, 1]
            v.wait_ge(par_in, 16 * 6)
            v.tensor_scalar(p1[:, :, 0], b_r[:], 2.0, None, ALU.mult)
            v.tensor_scalar(p2[0:HALF, :, 0], b_i[0:HALF, :], -2.0, None, ALU.mult)
            v.tensor_scalar(p2[HALF:P, :, 0], b_i[HALF:P, :], 2.0, None, ALU.mult).then_inc(b_ready, 1)
            link(v.tensor_scalar(hdt[:], dt_, 0.5, None, ALU.mult))
            v.tensor_tensor(y[:], aimag[:], hdt[:], ALU.mult)
            link(v.scalar_tensor_tensor(out=xr[:], in0=areal, scalar=-1.0, in1=hdt[:],
                                        op0=ALU.mult, op1=ALU.mult))
            v.tensor_scalar(one_x, xr[:], -1.0, 1.0, ALU.mult, ALU.add)
            v.tensor_tensor(t[:], y[:], y[:], ALU.mult)
            link(v.tensor_tensor(n2, xr[:], xr[:], ALU.mult))
            link(v.tensor_tensor(one_x, one_x, one_x, ALU.mult))
            v.tensor_tensor(n2, n2, t[:], ALU.add)
            link(v.tensor_tensor(one_x, one_x, t[:], ALU.add))
            v.tensor_scalar(n2, n2, -1.0, 1.0, ALU.mult, ALU.add)
            link(v.reciprocal(one_x, one_x))
            v.tensor_tensor(zr[:, 0], n2, one_x, ALU.mult)
            link(v.scalar_tensor_tensor(out=zi[:, 0], in0=y[:], scalar=2.0, in1=one_x,
                                        op0=ALU.mult, op1=ALU.mult))
            for k in range(7):
                v.tensor_tensor(xr[:], zr[:, k], zr[:, k], ALU.mult)
                v.tensor_tensor(y[:], zi[:, k], zi[:, k], ALU.mult)
                link(v.scalar_tensor_tensor(out=zi[:, k + 1], in0=zr[:, k], scalar=2.0, in1=zi[:, k],
                                            op0=ALU.mult, op1=ALU.mult))
                ins = v.tensor_tensor(zr[:, k + 1], xr[:], y[:], ALU.subtract)
                link(ins)
            v.sem_inc(squares, 1)
            start = count[0]
            v.sem_inc(z_high, 1)

            def squares_of(i, k):
                m, pair = 1 << k, bass.ds(i * (2 * CHUNK), 2 * CHUNK)
                return (m, pair, [t[:, 0:2 * CHUNK * m].rearrange("p (h l) -> p h l", l=m) for t in t_dve],
                        zr[:, k, pair].unsqueeze(2).to_broadcast([P, 2 * CHUNK, m]),
                        zi[:, k, pair].unsqueeze(2).to_broadcast([P, 2 * CHUNK, m]))

            def multiply(i, k):
                m, pair, (ta, tb, tc, td), zr_m, zi_m = squares_of(i, k)
                v.tensor_tensor(ta, u[:, pair, 0:m], zr_m, ALU.mult)
                v.tensor_tensor(tb, w[:, pair, 0:m], zi_m, ALU.mult)
                v.tensor_tensor(tc, u[:, pair, 0:m], zi_m, ALU.mult)
                v.tensor_tensor(td, w[:, pair, 0:m], zr_m, ALU.mult).then_inc(dve, 1)

            def add(i, k):
                m, pair, (ta, tb, tc, td), _, _ = squares_of(i, k)
                v.tensor_tensor(u[:, pair, m:2 * m], ta, tb, ALU.subtract)
                v.tensor_tensor(w[:, pair, m:2 * m], tc, td, ALU.add).then_inc(u_done if k == 3 else dve, 1)

            def high_products(c):
                hs = bass.ds(c * CHUNK, CHUNK)
                v.wait_ge(z_high, c + 1)
                v.tensor_tensor(t_fin[0][:], u[:, hs, :], zr[:, 4, hs].unsqueeze(2).to_broadcast([P, CHUNK, 16]), ALU.mult)
                v.tensor_tensor(t_fin[1][:], w[:, hs, :], zi[:, 4, hs].unsqueeze(2).to_broadcast([P, CHUNK, 16]),
                                ALU.mult).then_inc(dve, 1)

            def high_part(c, half):
                v.wait_ge(mm_done, c + 1)
                v.tensor_tensor(zc[half][:, :, 16:32], t_fin[0][:], t_fin[1][:], ALU.subtract).then_inc(z_high, 1)

            def a_real_part(i, c, half):
                hs = bass.ds(c * CHUNK, CHUNK)
                v.wait_ge(p_done, i + 1)
                v.tensor_tensor(a_re[half][:], c_re[:, hs, :].unsqueeze(3).to_broadcast([P, CHUNK, NB, L1]),
                                p1[:, hs, :].unsqueeze(2).to_broadcast([P, CHUNK, NB, L1]), ALU.mult).then_inc(are_done, 1)

            for k in range(4):
                multiply(0, k)
                v.wait_ge(dve, start + 2 * k + 1)
                add(0, k)
                if k < 3:
                    v.wait_ge(dve, start + 2 * k + 2)
            v.wait_ge(x_in, 64)
            start += 7
            per = 9
            with v.Fori(0, NCHUNK // 2 - 1) as i:
                c0, c1, at = i * 2, i * 2 + 1, i * per + start
                v.wait_ge(u_done, i + 1)
                multiply(i + 1, 0)
                high_products(c0)
                v.wait_ge(dve, at + 1)
                add(i + 1, 0)
                v.wait_ge(dve, at + 2)
                high_part(c0, 0)
                v.wait_ge(dve, at + 3)
                multiply(i + 1, 1)
                a_real_part(i, c0, 0)
                v.wait_ge(dve, at + 4)
                add(i + 1, 1)
                high_products(c1)
                v.wait_ge(dve, at + 5)
                multiply(i + 1, 2)
                v.wait_ge(dve, at + 6)
                high_part(c1, 1)
                v.wait_ge(dve, at + 7)
                add(i + 1, 2)
                a_real_part(i, c1, 1)
                v.wait_ge(dve, at + 8)
                multiply(i + 1, 3)
                v.wait_ge(dve, at + 9)
                add(i + 1, 3)
            at = start + per * (NCHUNK // 2 - 1)
            v.wait_ge(u_done, NCHUNK // 2)
            for half in range(2):
                c = NCHUNK - 2 + half
                high_products(c)
                v.wait_ge(dve, at + half + 1)
                high_part(c, half)
                a_real_part(NCHUNK // 2 - 1, c, half)
            for n in range(0, 8, 2):
                v.wait_ge(tr_done, n + 1)
                bank_out(v.tensor_copy, n, h_v)

        @block.gpsimd
        def _(g):
            count = [0]

            def link(ins):
                count[0] += 1
                ins.then_inc(pool, 1)
                g.wait_ge(pool, count[0])

            g.wait_ge(b_ready, 1)
            g.wait_ge(squares, 1)
            g.wait_ge(x_in, 64)
            per = 2 * 3
            with g.Fori(0, NCHUNK // 2) as i:
                pair = bass.ds(i * (2 * CHUNK), 2 * CHUNK)
                for k in range(3):
                    m = 1 << k
                    ta, tb, tc, td = (t[:, 0:2 * CHUNK * m].rearrange("p (h l) -> p h l", l=m) for t in t_pool)
                    zr_m = zr[:, k + 5, pair].unsqueeze(2).to_broadcast([P, 2 * CHUNK, m])
                    zi_m = zi[:, k + 5, pair].unsqueeze(2).to_broadcast([P, 2 * CHUNK, m])
                    g.tensor_tensor(ta, p1[:, pair, 0:m], zr_m, ALU.mult)
                    g.tensor_tensor(tb, p2[:, pair, 0:m], zi_m, ALU.mult)
                    g.tensor_tensor(tc, p2[:, pair, 0:m], zr_m, ALU.mult)
                    g.tensor_tensor(td, p1[:, pair, 0:m], zi_m, ALU.mult).then_inc(pool, 1)
                    g.wait_ge(pool, i * per + 2 * k + 1)
                    g.tensor_tensor(p1[:, pair, m:2 * m], ta, tb, ALU.add)
                    g.tensor_tensor(p2[:, pair, m:2 * m], tc, td, ALU.subtract).then_inc(pool, 1)
                    g.wait_ge(pool, i * per + 2 * k + 2)
                g.sem_inc(p_done, 1)
                for half in range(2):
                    c = i * 2 + half
                    hs = bass.ds(c * CHUNK, CHUNK)
                    g.wait_ge(mm_done, c + 1)
                    g.tensor_tensor(
                        a_im[half][:],
                        c_im[:, hs, :].unsqueeze(3).to_broadcast([P, CHUNK, NB, L1]),
                        p2[:, hs, :].unsqueeze(2).to_broadcast([P, CHUNK, NB, L1]),
                        ALU.mult).then_inc(aim_done, 1)

        @block.tensor
        def _(pe):
            pe.sem_inc(mm_done, AHEAD)
            with pe.Fori(0, NCHUNK // 2) as i:
                for half in range(2):
                    c = i * 2 + half
                    pe.wait_ge(z_low, c + 1)
                    pe.wait_ge(z_high, c + 2)
                    pe.wait_ge(are_done, c + 1)
                    pe.wait_ge(aim_done, c + 1)
                    pe.wait_ge(k_done, 2 * c + 2)
                    for q in range(QUADS):
                        for a in (a_re, a_im):
                            for j in range(4):
                                last = pe.matmul(ps[half][32 * j:32 * j + 32, 64 * q:64 * q + 64],
                                                 zc[half][:, 4 * q + j, :],
                                                 a[half][:, 4 * q + j].rearrange("p b l -> p (b l)"),
                                                 start=a is a_re, stop=a is a_im)
                    last.then_inc(mm_done, 1)
            pe.wait_ge(k_done, 2 * (NCHUNK + AHEAD))
            pe.wait_ge(idn_in, 16)
            for n in range(8):
                bp, g = n // 2, n % 2
                for k in range(4):
                    last = pe.transpose(ps[n][:, 128 * k:128 * k + 128],
                                        k_sb[:, bp, 4 * g + k].rearrange("p s q -> p (s q)"), idn[:])
                last.then_inc(tr_done, 1)


NH = 16
HS = DM // NH
NT = SEQ // P
TILES = NB * NT
KC = DM // P
NG = NH // 4
EPS = 1e-5
GW = 4 * SEQ
PREP = 6


def wait_reuse(eng, semaphore, value):
    if not isinstance(value, int) or value > 0:
        eng.wait_ge(semaphore, value)


def attention_phase(nc, w_in, b_qkv, b_o, rope, idn, ident_b, mask_b, select_b, slots_dram, h_all, stats2):
    with ExitStack() as ctx:
        def sb(name, shape, dt=F32):
            return ctx.enter_context(nc.sbuf_tensor(name, shape, dt))

        def sem(name):
            return ctx.enter_context(nc.semaphore(name))

        idb = sb("at_ident_b", [P, P], BF16)
        maskb = sb("at_mask_b", [P, 4 * P], BF16)
        selb = sb("at_select_b", [P, NH, P], BF16)
        cs = sb("at_rope", [P, NT, 2, HS])
        bq = sb("at_b_qkv", [P, 3 * DM])
        bo = sb("at_b_o", [P, DM])
        w_hi = sb("at_w_hi", [P, KC, 4 * DM], F32R)
        w_lo = sb("at_w_lo", [P, KC, 4 * DM], F32R)
        xn = sb("at_xn", [P, NT, DM])
        stats = sb("at_stats", [P, TILES, 6])
        mv = sb("at_mv", [P, TILES, 2])
        rstd = sb("at_rstd", [P, TILES])
        vare = sb("at_vare", [P, TILES])
        mhalf = sb("at_mhalf", [P, TILES])
        x_hi = sb("at_x_hi", [P, KC, SEQ], F32R)
        x_lo = sb("at_x_lo", [P, KC, SEQ], F32R)
        qk = sb("at_qk", [P, NT, 2 * NH, HS])
        m1 = sb("at_m1", [P, NT, 2 * NH, HS])
        m2 = sb("at_m2", [P, NT, 2 * NH, HS])
        vx = [sb(f"at_v{i}", [P, NT, NH, 32]) for i in range(2)]
        st_q = sb("at_st_q", [P, NT, NH, 2, HS])
        st_ka = sb("at_st_ka", [P, NT, NH, 2, HS])
        st_kb = sb("at_st_kb", [P, NT, NH, 2, HS])
        qc = sb("at_qc", [P, NG, SEQ], F32R)
        ka = [sb(f"at_ka{i}", [P, NG, SEQ], F32R) for i in range(2)]
        kb = [sb(f"at_kb{i}", [P, NG, SEQ], F32R) for i in range(2)]
        qm = [sb(f"at_qm{i}", [P, NG, 4, SEQ], F32R) for i in range(2)]
        km = sb("at_km", [P, NG, 4, SEQ], F32R)
        cm = sb("at_cm", [P, NT, NH])
        cb = sb("at_cb", [P, NT, 2, NH], BF16)
        cz = sb("at_cz", [P, SEQ], BF16)
        pt = [sb(f"at_pt{i}", [P, 3 * 512]) for i in range(2)]
        ot = sb("at_ot", [P, NG, SEQ])
        rc = sb("at_rc", [P, NT, NH])
        yv = sb("at_y", [P, NT, DM])
        y_hi = sb("at_y_hi", [P, KC, SEQ], F32R)
        y_lo = sb("at_y_lo", [P, KC, SEQ], F32R)
        zero = sb("at_zero", [P, DM])
        ps = ctx.enter_context(nc.psum_tensor("at_ps", [P, 8, 512], F32))

        const_in = sem("at_const_in")
        w_high = sem("at_w_high")
        w_low_g = sem("at_w_low_g")
        w_low_v = sem("at_w_low_v")
        zeroed = sem("at_zeroed")
        prep = sem("at_prep")
        masks = sem("at_masks")
        dve = sem("at_dve")
        mean_var = sem("at_mean_var")
        rstd_done = sem("at_rstd_done")
        xn_done = sem("at_xn_done")
        xt_ps = sem("at_xt_ps")
        xhi_s = sem("at_xhi_s")
        xlo_s = sem("at_xlo_s")
        qk_ps = sem("at_qk_ps")
        v_ps = sem("at_v_ps")
        qk_v = sem("at_qk_v")
        v_v = sem("at_v_v")
        rot1 = sem("at_rot1")
        rot2 = sem("at_rot2")
        rot = sem("at_rot")
        st_hi = sem("at_st_hi")
        st_lo = (sem("at_st_lo0"), sem("at_st_lo1"))
        hd_ps = sem("at_hd_ps")
        hd_q = sem("at_hd_q")
        hd_k = sem("at_hd_k")
        qm_in = sem("at_qm_in")
        km_in = sem("at_km_in")
        mx_ps = sem("at_mx_ps")
        mx_v = sem("at_mx_v")
        cb_v = sem("at_cb_v")
        cz_ps = sem("at_cz_ps")
        cz_a = sem("at_cz_a")
        sc_ps = sem("at_sc_ps")
        ex_a = sem("at_ex_a")
        ex_seen = sem("at_ex_seen")
        msk_g = sem("at_msk_g")
        pv_ps = sem("at_pv_ps")
        ot_a = sem("at_ot_a")
        ot_ps = sem("at_ot_ps")
        rc_v = sem("at_rc_v")
        y_v = sem("at_y_v")
        yt_ps = sem("at_yt_ps")
        yhi_s = sem("at_yhi_s")
        ylo_s = sem("at_ylo_s")
        o_ps = sem("at_o_ps")
        hb_g = sem("at_hb_g")
        stats_v = sem("at_stats_v")
        o_v = sem("at_o_v")

        block = ctx.enter_context(nc.Block())

        SCORE, PV_BANK, WORK = 0, 4, 5
        UNITS = 3 * NG

        def steps(eng, step):
            step(-1, 1, True, False, False)
            step(0, 0, True, True, False)
            with eng.Fori(0, (NB - 2) // 2) as i:
                step(i * 2 + 1, 1, True, True, True)
                step(i * 2 + 2, 0, True, True, True)
            step(NB - 1, (NB - 1) % 2, False, True, True)
            step(NB, NB % 2, False, False, True)

        def flat(t):
            return t.rearrange("p a b -> p (a b)")

        def stage_low(eng, f, t):
            eng.wait_ge(st_hi, 4 * f + 2 * t + 2)
            eng.tensor_tensor(st_q[:, t, :, 1, :].bitcast(F32R), m1[:, t, 0:NH, :], st_q[:, t, :, 0, :],
                              ALU.subtract).then_inc(st_lo[t], 1)
            eng.tensor_tensor(st_kb[:, t, :, 0, :].bitcast(F32R), m1[:, t, NH:, :], st_ka[:, t, :, 0, :],
                              ALU.subtract).then_inc(st_lo[t], 1)

        @block.sync
        def _(sp):
            for dst, src in ((bq[:], b_qkv.unsqueeze(0).to_broadcast([P, 3 * DM])), (cs[:], rope), (idb[:], ident_b),
                             (maskb[:], mask_b), (selb[:], select_b), (bo[:], b_o.unsqueeze(0).to_broadcast([P, DM]))):
                sp.dma_start(dst, src).then_inc(const_in, 16)
            sp.wait_ge(prep, PREP)
            sp.wait_ge(masks, 1)
            slots = slots_dram.rearrange("(n p) d -> p n d", p=P)
            share = slots.shape[1] // NB
            assert slots.shape[1] == share * NB

            def step(b, par, front, back, tail):
                if not front:
                    return
                f, new = b + 1, 1 - par
                for copied, count, out, src, landed in ((hd_k, 4, km, ka[new], km_in), (hd_q, 2, qm[new], qc, qm_in)):
                    sp.wait_ge(copied, count * f + count)
                    if isinstance(b, int) and copied is hd_q:
                        sp.wait_ge(masks, f + 2)
                    for j in range(4):
                        rows = slice(32 * j, 32 * j + 32)
                        sp.dma_start(out[rows, :, j, :].bitcast(F32), src[rows].bitcast(F32)).then_inc(landed, 16)
                sp.dma_start(slots[:, bass.ds(f * share, share), :],
                             zero[:].unsqueeze(1).to_broadcast([P, share, DM])).then_inc(zeroed, 16)

            steps(sp, step)
            sp.wait_ge(zeroed, 16 * NB)

        @block.gpsimd
        def _(g):
            g.memset(mhalf[:], -0.5).then_inc(prep, 1)
            g.memset(cz[:], 0.0).then_inc(prep, 1)
            g.memset(zero[:], 0.0).then_inc(prep, 1)
            g.memset(st_kb[:, :, :, 1, :], 0.0).then_inc(prep, 1)
            for t in vx:
                g.memset(t[:, :, :, HS:32], 1.0).then_inc(prep, 1)
            g.wait_ge(mean_var, 1)
            g.wait_ge(prep, 1)
            g.tensor_tensor(rstd[:, 0:NT], vare[:, 0:NT], mhalf[:, 0:NT], ALU.pow).then_inc(rstd_done, 1)
            g.wait_ge(w_high, 1)
            qkv_cols = slice(0, 3 * DM)
            g.tensor_tensor(w_lo[:, :, qkv_cols], w_in[:, :, qkv_cols], w_hi[:, :, qkv_cols].bitcast(F32),
                            ALU.subtract).then_inc(w_low_g, 1)
            g.memset(km[:].bitcast(F32), 0.0).then_inc(masks, 1)
            g.wait_ge(const_in, 16 * 6)

            def step(b, par, front, back, tail):
                f = b + 1
                if front:
                    for t in range(NT):
                        if t == 1:
                            stage_low(g, f, 0)
                        g.wait_ge(qk_v, NT * f + t + 1)
                        sgn = cs[:, t, 1, :].rearrange("p (i e) -> p i e", e=2)
                        src = qk[:, t].rearrange("p h (i e) -> p h i e", e=2)
                        dst = m2[:, t].rearrange("p h (i e) -> p h i e", e=2)
                        for e in range(2):
                            g.tensor_tensor(dst[:, :, :, e], src[:, :, :, 1 - e],
                                            sgn[:, :, e].unsqueeze(1).to_broadcast([P, 2 * NH, HS // 2]),
                                            ALU.mult).then_inc(rot2, 1)
                    if isinstance(b, int) and b < 0:
                        g.wait_ge(mean_var, 3)
                        g.tensor_tensor(rstd[:, NT:], vare[:, NT:], mhalf[:, NT:], ALU.pow).then_inc(rstd_done, 1)
                    if isinstance(b, int):
                        g.memset(qm[1 - par][:].bitcast(F32), 0.0).then_inc(masks, 1)
                    g.wait_ge(xn_done, NT * f + NT)
                    tok = h_all[:, bass.ds(NT * f, NT), :]
                    g.tensor_tensor(tok, tok, bo[:].unsqueeze(1).to_broadcast([P, NT, DM]), ALU.add).then_inc(hb_g, 1)
                if back:
                    for n in range(NG):
                        for banks, ofs, width in ((2, 0, SEQ), (3, GW, P)):
                            g.wait_ge(ex_a, UNITS * b + 3 * n + banks)
                            g.sem_inc(ex_seen, 1)
                            d = pt[n % 2][:, ofs:ofs + 4 * width].rearrange("p (h q) -> p h q", h=4)[:, :, 0:P]
                            g.affine_select(out=d, in_=d, compare_op=ALU.is_ge, fill=0.0, base=0,
                                            pattern=[[0, 4], [1, P]], channel_multiplier=-1).then_inc(msk_g, 1)

            steps(g, step)

        @block.scalar
        def _(act):
            def weights_high(cols):
                act.copy(w_hi[:, :, cols], w_in[:, :, cols]).then_inc(w_high, 1)

            weights_high(slice(0, 3 * DM))

            def step(b, par, front, back, tail):
                f, z, new = b + 1, b - 1, 1 - par

                def copy_group(s, n):
                    act.wait_ge(pv_ps, NG * s + n + 1)
                    act.copy(ot[:, n, :], ps[:, PV_BANK, 0:SEQ]).then_inc(ot_a, 1)

                def stage(t):
                    act.wait_ge(rot, NT * f + t + 1)
                    q, k = m1[:, t, 0:NH, :], m1[:, t, NH:, :]
                    act.copy(st_q[:, t, :, 0, :].bitcast(F32R), q).then_inc(st_hi, 1)
                    act.copy(st_ka[:, t].bitcast(F32R), k.unsqueeze(2).to_broadcast([P, NH, 2, HS])).then_inc(st_hi, 1)

                def copy_k(t):
                    for i, dst in ((1, ka[new]), (2, kb[new])):
                        act.wait_ge(hd_ps, 6 * f + 3 * t + i + 1)
                        act.copy(dst[:, :, t * P:(t + 1) * P],
                                 ps[:, WORK + i].rearrange("p (g t) -> p g t", g=NG)).then_inc(hd_k, 1)

                def exponentials(n):
                    for c in range(3):
                        u = 3 * n + c
                        act.wait_ge(sc_ps, UNITS * b + u + 1)
                        if c == 0:
                            wait_reuse(act, pv_ps, NG * b + n - 1)
                        act.activation(pt[n % 2][:, c * 512:(c + 1) * 512], ps[:, SCORE + u % 4, :],
                                       ACT.Exp, scale=1.0 / math.sqrt(HS)).then_inc(ex_a, 1)

                if front:
                    act.wait_ge(xt_ps, f + 1)
                    act.copy(flat(x_hi[:]), ps[:, WORK, :]).then_inc(xhi_s, 1)
                if isinstance(b, int) and b < 0:
                    weights_high(slice(3 * DM, 4 * DM))
                if tail:
                    copy_group(z, NG - 1)
                if tail:
                    act.wait_ge(yt_ps, z + 1)
                    act.copy(flat(y_hi[:]), ps[:, WORK + 1, :]).then_inc(yhi_s, 1)
                if front:
                    stage(0)
                if back:
                    act.wait_ge(cz_ps, b + 1)
                    act.copy(cz[0:32, :], ps[0:32, PV_BANK, 0:P].bitcast(BF16)).then_inc(cz_a, 1)
                    exponentials(0)
                if front:
                    copy_k(0)
                    stage(1)
                if back:
                    exponentials(1)
                    copy_group(b, 0)
                if front:
                    copy_k(1)
                if back:
                    exponentials(2)
                    copy_group(b, 1)
                    exponentials(3)
                    copy_group(b, 2)

            steps(act, step)

        @block.vector
        def _(v):
            count = [0]

            def link(ins):
                count[0] += 1
                ins.then_inc(dve, 1)
                v.wait_ge(dve, count[0])

            VAR_FIRST = 3 * TILES // 4

            def variances(tiles):
                for n in tiles:
                    ins = v.bn_stats(stats[:, n, :], h_all[:, n, :])
                link(ins)
                for n in tiles:
                    ins = v.bn_aggr(mv[:, n, :], stats[:, n, :])
                link(ins)
                part = slice(tiles[0], tiles[-1] + 1)
                v.tensor_scalar(vare[:, part], mv[:, part, 1], EPS, None, ALU.add).then_inc(mean_var, 1)

            def normalise(s):
                for t in range(NT):
                    n = NT * s + t
                    ht = h_all[:, bass.ds(n, 1), :].rearrange("p o d -> p (o d)")
                    v.tensor_scalar(xn[:, t, :], ht, mv[:, bass.ds(n, 1), 0:1].rearrange("p o d -> p (o d)"),
                                    rstd[:, bass.ds(n, 1)], ALU.subtract, ALU.mult).then_inc(xn_done, 1)

            def step(b, par, front, back, tail):
                f, z, new = b + 1, b - 1, 1 - par

                def maxima(n):
                    for c in range(3):
                        u = 3 * n + c
                        v.wait_ge(mx_ps, UNITS * b + u + 1)
                        dst = cm[:, 0, 4 * n:4 * n + 4] if c == 0 else cm[:, 1, 4 * n + 2 * c - 2:4 * n + 2 * c]
                        v.tensor_reduce(dst, ps[:, SCORE + u % 4].rearrange("p (h k) -> p h k", h=4 if c == 0 else 2),
                                        AX_X, ALU.max).then_inc(mx_v, 1)

                def qkv_out(t):
                    if isinstance(b, int):
                        v.wait_ge(const_in, 16 * 6)
                    v.wait_ge(qk_ps, NT * f + t + 1)
                    v.tensor_tensor(qk[:, t].rearrange("p h d -> p (h d)"), ps[:, WORK + (2 if t else 1), :],
                                    bq[:, 0:2 * DM], ALU.add).then_inc(qk_v, 1)
                    v.wait_ge(v_ps, NT * f + t + 1)
                    v.tensor_tensor(vx[new][:, t, :, 0:HS],
                                    ps[:, WORK + (0 if t else 2), 0:DM].rearrange("p (h d) -> p h d", h=NH),
                                    bq[:, 2 * DM:].rearrange("p (h d) -> p h d", h=NH), ALU.add).then_inc(v_v, 1)
                    v.wait_ge(qk_v, NT * f + t + 1)
                    v.tensor_tensor(m1[:, t], qk[:, t], cs[:, t, 0, :].unsqueeze(1).to_broadcast([P, 2 * NH, HS]),
                                    ALU.mult).then_inc(rot1, 1)

                def rotate(t):
                    v.wait_ge(rot1, NT * f + t + 1)
                    v.wait_ge(rot2, 4 * f + 2 * t + 2)
                    v.tensor_tensor(m1[:, t], m1[:, t], m2[:, t], ALU.add).then_inc(rot, 1)

                def copy_q(t):
                    v.wait_ge(hd_ps, 6 * f + 3 * t + 1)
                    v.tensor_copy(qc[:, :, t * P:(t + 1) * P],
                                  ps[:, WORK].rearrange("p (g t) -> p g t", g=NG)).then_inc(hd_q, 1)

                if front and not (isinstance(b, int) and b < 0):
                    if isinstance(b, int):
                        v.wait_ge(rstd_done, 2)
                    normalise(f)
                if back:
                    maxima(0)
                if front:
                    v.wait_ge(xhi_s, f + 1)
                    v.tensor_tensor(flat(x_lo[:]), ps[:, WORK, :], flat(x_hi[:]).bitcast(F32),
                                    ALU.subtract).then_inc(xlo_s, 1)
                if isinstance(b, int) and b < 0:
                    variances(range(NT, VAR_FIRST))
                if back:
                    maxima(1)
                if front:
                    qkv_out(0)
                if tail:
                    for t in range(NT):
                        v.wait_ge(ot_ps, NT * z + t + 1)
                        acc = ps[:, WORK + t].rearrange("p (h d) -> p h d", h=NH)
                        v.reciprocal(rc[:, t], acc[:, :, HS]).then_inc(rc_v, 1)
                    for t in range(NT):
                        acc = ps[:, WORK + t].rearrange("p (h d) -> p h d", h=NH)
                        v.wait_ge(rc_v, NT * z + t + 1)
                        v.tensor_tensor(yv[:, t].rearrange("p (h d) -> p h d", h=NH), acc[:, :, 0:HS],
                                        rc[:, t].unsqueeze(2).to_broadcast([P, NH, HS]), ALU.mult).then_inc(y_v, 1)
                if back:
                    maxima(2)
                if front:
                    rotate(0)
                if isinstance(b, int) and b < 0:
                    variances(range(VAR_FIRST, TILES))
                    o_cols = slice(3 * DM, 4 * DM)
                    v.wait_ge(w_high, 2)
                    v.tensor_tensor(w_lo[:, :, o_cols], w_in[:, :, o_cols], w_hi[:, :, o_cols].bitcast(F32),
                                    ALU.subtract).then_inc(w_low_v, 1)
                if tail:
                    v.wait_ge(yhi_s, z + 1)
                    v.tensor_tensor(flat(y_lo[:]), ps[:, WORK + 1, :], flat(y_hi[:]).bitcast(F32),
                                    ALU.subtract).then_inc(ylo_s, 1)
                if back:
                    maxima(3)
                    v.wait_ge(mx_v, UNITS * b + UNITS)
                    v.tensor_scalar(cb[:, :, 0, :], cm[:], -1.0, None, ALU.mult).then_inc(cb_v, 1)
                    v.wait_ge(cb_v, 2 * b + 1)
                    v.scalar_tensor_tensor(out=cb[:, :, 1, :], in0=cm[:], scalar=-1.0, in1=cb[:, :, 0, :],
                                           op0=ALU.mult, op1=ALU.subtract).then_inc(cb_v, 1)
                if front:
                    qkv_out(1)
                if tail:
                    v.wait_ge(o_ps, z + 1)
                    v.wait_ge(hb_g, z + 1)
                    tok = h_all[:, bass.ds(NT * z, NT), :]
                    v.tensor_tensor(tok, ps[:, WORK + 1, :].rearrange("p (t d) -> p t d", t=NT), tok,
                                    ALU.add).then_inc(o_v, 1)
                if front:
                    rotate(1)
                    copy_q(0)
                if tail:
                    v.wait_ge(o_v, z + 1)
                    for t in range(NT):
                        n = NT * z + t
                        v.bn_stats(stats2[:, bass.ds(n, 1), :].rearrange("p o s -> p (o s)"),
                                   h_all[:, bass.ds(n, 1), :].rearrange("p o d -> p (o d)")).then_inc(stats_v, 1)
                if front:
                    stage_low(v, f, 1)
                    copy_q(1)

            variances(range(NT))
            v.wait_ge(rstd_done, 1)
            normalise(0)
            steps(v, step)

        @block.tensor
        def _(pe):
            def split_product(out, pairs):
                n = len(pairs)
                for i, (x, y) in enumerate(pairs):
                    last = pe.matmul(out, x, y, start=i == 0, stop=i == n - 1)
                return last

            pe.wait_ge(prep, PREP)

            def step(b, par, front, back, tail):
                f, z, old = b + 1, b - 1, 1 - par

                def turn_x():
                    pe.wait_ge(xn_done, NT * f + NT)
                    wait_reuse(pe, hd_q, 2 * b + 2)
                    for k in range(KC):
                        for t in range(NT):
                            last = pe.transpose(ps[:, WORK, k * SEQ + t * P:k * SEQ + (t + 1) * P],
                                                xn[:, t, k * P:(k + 1) * P], idn[:])
                    last.then_inc(xt_ps, 1)

                def qkv(t):
                    if isinstance(b, int):
                        pe.wait_ge(w_low_g, 1)
                        pe.wait_ge(const_in, 16 * 6)
                    pe.wait_ge(xhi_s, f + 1)
                    pe.wait_ge(xlo_s, f + 1)
                    if t == 0:
                        wait_reuse(pe, hd_k, 4 * b + 4)
                    else:
                        pe.wait_ge(v_v, NT * f + 1)
                    rows = slice(t * P, (t + 1) * P)
                    for bank, n, cols, done in ((2 if t else 1, 512, slice(0, 2 * DM), qk_ps),
                                                (0 if t else 2, DM, slice(2 * DM, 3 * DM), v_ps)):
                        if t and bank == 0:
                            wait_reuse(pe, y_v, NT * z + 1)
                        split_product(ps[:, WORK + bank, 0:n],
                                      [(x[:, k, rows], w[:, k, cols]) for k in range(KC)
                                       for x, w in ((x_hi, w_hi), (x_hi, w_lo), (x_lo, w_hi))]).then_inc(done, 1)

                def heads(t):
                    pe.wait_ge(st_hi, 4 * f + 2 * t + 2)
                    pe.wait_ge(st_lo[t], 2 * f + 2)
                    for i, st in enumerate((st_q, st_ka, st_kb)):
                        if t == 0:
                            if i == 0:
                                pe.wait_ge(v_v, NT * f + 2)
                            elif i == 1:
                                wait_reuse(pe, o_v, z + 1)
                            else:
                                pe.wait_ge(qk_v, NT * f + 2)
                        elif i == 0:
                            pe.wait_ge(hd_q, 2 * f + 1)
                        else:
                            pe.wait_ge(hd_k, 4 * f + i)
                        for n in range(NG):
                            last = pe.transpose(ps[:, WORK + i, n * P:(n + 1) * P],
                                                st[:, t, 4 * n:4 * n + 4].rearrange("p h c d -> p (h c d)"), idn[:])
                        last.then_inc(hd_ps, 1)

                def score_bank(u):
                    n, c = u // 3, u % 3
                    out = ps[:, SCORE + u % 4, :]
                    if u < 4:
                        wait_reuse(pe, ex_a, UNITS * b - 3 + u)
                    else:
                        pe.wait_ge(mx_v, UNITS * b + u - 3)
                    if c == 0:
                        pe.matmul(out, qc[:, n, 0:P], km[:, n, :, 0:P], start=True, stop=False)
                        last = pe.matmul(out, idb[:], maskb[:], start=False, stop=True)
                    else:
                        pe.matmul(out, qc[:, n, P:SEQ], km[:, n, 2 * c - 2:2 * c, :], start=True, stop=False)
                        last = pe.matmul(out.rearrange("p (h k) -> p h k", h=2)[:, :, P:SEQ], idb[:],
                                         maskb[:, 0:2 * P].rearrange("p (h k) -> p h k", h=2), start=False, stop=True)
                    last.then_inc(mx_ps, 1)

                def maxima(n):
                    for c in range(3):
                        score_bank(3 * n + c)

                def scores(n):
                    for c in range(3):
                        u = 3 * n + c
                        if u >= 4:
                            pe.wait_ge(ex_a, UNITS * b + u - 3)
                        out = ps[:, SCORE + u % 4, :]
                        keys = slice(0, P) if c < 2 else slice(P, SEQ)
                        x = qm[par][:, n, 2 * c:2 * c + 2, :] if c < 2 else qm[par][:, n, :, P:SEQ]
                        heads_ = (2 * c, 2 * c + 1) if c < 2 else range(4)
                        width = SEQ if c < 2 else P
                        for i, j in enumerate(heads_):
                            pe.matmul(out[:, i * width:(i + 1) * width], selb[:, 4 * n + j, :],
                                      cz[:, SEQ - width:SEQ], start=i == 0, stop=False, skip_group_check=True)
                        pe.matmul(out, ka[par][:, n, keys], x, start=False, stop=False, skip_group_check=True)
                        pe.matmul(out, kb[par][:, n, keys], x, start=False, stop=True,
                                  skip_group_check=True).then_inc(sc_ps, 1)

                def weigh(s, vals, n):
                    pe.wait_ge(msk_g, 2 * NG * s + 2 * n + 2)
                    if n == 0:
                        pe.wait_ge(cz_a, s + 1)
                    else:
                        pe.wait_ge(ot_a, NG * s + n)
                    for t in range(NT):
                        width = SEQ if t == 0 else P
                        for j in range(4):
                            ofs = t * GW + j * width
                            last = pe.matmul(ps[32 * j:32 * j + 32, PV_BANK, SEQ - width:SEQ],
                                             vals[:, t, 4 * n + j, :], pt[n % 2][:, ofs:ofs + width],
                                             start=t == 0, stop=t == 1, skip_group_check=True)
                    last.then_inc(pv_ps, 1)

                if back:
                    pe.wait_ge(hd_q, 2 * b + 2)
                    pe.wait_ge(hd_k, 4 * b + 4)
                    pe.wait_ge(km_in, 64 * b + 64)
                    maxima(0)
                if front:
                    turn_x()
                if tail:
                    weigh(z, vx[old], NG - 1)
                if back:
                    maxima(1)
                if front:
                    qkv(0)
                if tail:
                    pe.wait_ge(ot_a, NG * z + NG)
                    if front:
                        pe.wait_ge(qk_v, NT * f + 1)
                    else:
                        pe.wait_ge(o_v, z)
                    for t in range(NT):
                        for n in range(NG):
                            last = pe.transpose(ps[:, WORK + t, n * P:(n + 1) * P], ot[:, n, t * P:(t + 1) * P], idn[:])
                        last.then_inc(ot_ps, 1)
                if back:
                    maxima(2)
                if tail:
                    pe.wait_ge(y_v, NT * z + NT)
                    for k in range(KC):
                        for t in range(NT):
                            last = pe.transpose(ps[:, WORK + 1, k * SEQ + t * P:k * SEQ + (t + 1) * P],
                                                yv[:, t, k * P:(k + 1) * P], idn[:])
                    last.then_inc(yt_ps, 1)
                if back:
                    maxima(3)
                if front:
                    qkv(1)
                if tail:
                    pe.wait_ge(yhi_s, z + 1)
                    pe.wait_ge(ylo_s, z + 1)
                    pe.wait_ge(w_low_v, 1)
                    for t in range(NT):
                        rows = slice(t * P, (t + 1) * P)
                        last = split_product(ps[:, WORK + 1, t * DM:(t + 1) * DM],
                                             [(x[:, k, rows], w[:, k, 3 * DM:]) for k in range(KC)
                                              for x, w in ((y_hi, w_hi), (y_hi, w_lo), (y_lo, w_hi))])
                    last.then_inc(o_ps, 1)
                if back:
                    pe.wait_ge(cb_v, b * 2 + 2)
                    wait_reuse(pe, ot_a, NG * b)
                    for t in range(NT):
                        last = pe.transpose(ps[0:32, PV_BANK, t * P // 2:(t + 1) * P // 2].bitcast(BF16),
                                            cb[:, t].rearrange("p c h -> p (c h)"), idb[:])
                    last.then_inc(cz_ps, 1)
                    pe.wait_ge(qm_in, 64 * b + 64)
                if back:
                    pe.wait_ge(cz_a, b + 1)
                    scores(0)
                if front:
                    heads(0)
                if back:
                    scores(1)
                    weigh(b, vx[par], 0)
                if front:
                    heads(1)
                if back:
                    scores(2)
                    weigh(b, vx[par], 1)
                    scores(3)
                    weigh(b, vx[par], 2)

            steps(pe, step)


NE = 8
FF = 512
FC = FF // P
SLOT_TILES = (2 * NB * SEQ + NE * (P - 1)) // P
BIG = 4.0
U32 = mybir.dt.uint32


def shared_and_routing_phase(nc, h_all, slots_dram, router_w, router_b, sw1, sw2, sb1_t, sb2_t, idn, tri_b,
                             rank8, tile_no, w1_all, w2_all, w1, w2, stats, pos_i, w_top, step_code, shared_place, b1_all):
    CH = 4
    HALVES = 2 * CH
    HW = 256
    JOBS = CH * FC
    HELD = NE - 1
    POOL_JOBS = 5
    with ExitStack() as ctx:
        def sb(name, shape, dt=F32):
            return ctx.enter_context(nc.sbuf_tensor(name, shape, dt))

        def sem(name):
            return ctx.enter_context(nc.semaphore(name))

        tri = sb("ro_tri", [P, P], BF16)
        ones = sb("ro_ones", [P, P], BF16)
        rk = sb("ro_rank8", [P, NE])
        tno = sb("ro_tile_no", [P, SLOT_TILES])
        rw_in = sb("ro_rw_in", [P, KC, NE])
        rw_hi = sb("ro_rw_hi", [P, KC, NE], F32R)
        rw_lo = sb("ro_rw_lo", [P, KC, NE], F32R)
        rb = sb("ro_rb", [NE, 1])
        b1c = sb("ro_b1", [P, FC])
        b2c = sb("ro_b2", [P, KC])
        mv = sb("ro_mv", [P, TILES, 2])
        vare = sb("ro_vare", [P, TILES])
        rstd = sb("ro_rstd", [P, TILES])
        mhalf = sb("ro_mhalf", [P, TILES])
        xn = shared_place[:].rearrange("p (n d) -> p n d", n=TILES)
        x_hi = sb("ro_x_hi", [P, KC, 512], F32R)
        x_lo = sb("ro_x_lo", [P, KC, 512], F32R)
        wst = [sb(f"ro_wst{i}", [P, KC * FF]) for i in range(2)]
        gl = [sb(f"ro_gelu{i}", [P, 512]) for i in range(2)]
        g_hi = [sb(f"ro_g_hi{i}", [P, 512], F32R) for i in range(3)]
        g_lo = [sb(f"ro_g_lo{i}", [P, 512], F32R) for i in range(3)]
        yt = sb("ro_yt", [P, KC, 512])
        lg_t = gl[0][0:NE, :]
        S3 = [P, TILES, NE]
        pr, a3, b3, c3, oh1, oh2 = (sb(f"ro_m{i}", S3) for i in range(6))
        sel_b = sb("ro_sel_b", S3, BF16)
        s1 = sb("ro_s1", [P, TILES])
        s2 = sb("ro_s2", [P, TILES])
        e1, e2, e3 = (sb(f"ro_e{i}", [P, NE]) for i in range(3))
        ei = sb("ro_ei", [P, NE], I32)
        te = sb("ro_te", [P, SLOT_TILES, NE])
        tf = sb("ro_tf", [P, SLOT_TILES])
        tc = sb("ro_tc", [P, SLOT_TILES + 4])
        code = sb("ro_code", [P, SLOT_TILES + 1])
        pf = sb("ro_pf", [P, 2, TILES])
        ps = ctx.enter_context(nc.psum_tensor("ro_ps", [P, 8, 512], F32))
        T_BANK, BACK_BANK, RANK_BANK, H_BANK, Y_BANK = 0, 2, 3, 4, 6
        LGT, WITHIN, TOTALS = (slice(i * TILES * NE, (i + 1) * TILES * NE) for i in range(3))

        const_in = sem("ro_const_in")
        w_in = [sem(f"ro_w_in{i}") for i in range(2)]
        w_hi_done = sem("ro_w_hi_done")
        w_lo_done = sem("ro_w_lo_done")
        prep = sem("ro_prep")
        dve = sem("ro_dve")
        mean_var = sem("ro_mean_var")
        rstd_done = sem("ro_rstd_done")
        xn_done = sem("ro_xn_done")
        xt_ps = sem("ro_xt_ps")
        xhi_s = sem("ro_xhi_s")
        xlo_s = sem("ro_xlo_s")
        rw_s = sem("ro_rw_s")
        lg_ps = sem("ro_lg_ps")
        lg_s = sem("ro_lg_s")
        lgt_ps = sem("ro_lgt_ps")
        sub_done = sem("ro_sub_done")
        exp_done = sem("ro_exp_done")
        sel_done = sem("ro_sel_done")
        rank_ps = sem("ro_rank_ps")
        code_done = sem("ro_code_done")
        pos_done = sem("ro_pos_done")
        b1_in = sem("ro_b1_in")
        scat = sem("ro_scat")
        h_ps = sem("ro_h_ps")
        g_a = sem("ro_g_a")
        ghi_a = sem("ro_ghi_a")
        glo_g = sem("ro_glo_g")
        glo_v = sem("ro_glo_v")
        y_acc = sem("ro_y_acc")
        yt_a = sem("ro_yt_a")
        yb_ps = sem("ro_yb_ps")
        h_v = sem("ro_h_v")

        MATS = [(HELD, 0, sw1), (HELD, 1, sw2)] + [(e, s, (w2 if s else w1)[e]) for e in range(NE) for s in range(2)]

        def parts(m):
            e, second, _ = MATS[m]
            w, k = (w2_all, FC) if second else (w1_all, KC)
            return wst[m % 2][:].rearrange("p (k n) -> p k n", k=k), w[:, e, :, 0], w[:, e, :, 1]

        def matrices_at(j):
            if j < 4:
                return [j] if j >= 2 else []
            return [] if j == 4 else [j - 1] if j < 12 else [11, 12] if j == 12 else [j]

        block = ctx.enter_context(nc.Block())

        @block.sync
        def _(sp):
            for dst, src in ((tri[:], tri_b), (rk[:], rank8.unsqueeze(0).to_broadcast([P, NE])),
                             (tno[:], tile_no.unsqueeze(0).to_broadcast([P, SLOT_TILES])),
                             (rw_in[:], router_w.rearrange("(k p) e -> p k e", p=P)),
                             (rb[:], router_b.unsqueeze(1)), (b1c[:], sb1_t), (b2c[:], sb2_t)):
                sp.dma_start(dst, src).then_inc(const_in, 16)
            for m, (_, _, src) in enumerate(MATS):
                if m >= 2:
                    sp.wait_ge(w_lo_done, m - 1)
                sp.dma_start(parts(m)[0], src.rearrange("(k p) n -> p k n", p=P)).then_inc(w_in[m % 2], 16)

        @block.gpsimd
        def _(g):
            g.memset(mhalf[:], -0.5).then_inc(prep, 1)
            g.memset(ones[:], 1.0).then_inc(prep, 1)
            g.wait_ge(prep, 2)
            for n, tiles in enumerate((slice(0, 4), slice(4, TILES))):
                g.wait_ge(mean_var, n + 1)
                g.tensor_tensor(rstd[:, tiles], vare[:, tiles], mhalf[:, tiles], ALU.pow).then_inc(rstd_done, 1)
            for j in range(POOL_JOBS):
                g.wait_ge(ghi_a, j + 1)
                if j >= 3:
                    g.wait_ge(y_acc, j - 2)
                g.tensor_tensor(g_lo[j % 3][:], gl[j % 2][:], g_hi[j % 3][:].bitcast(F32), ALU.subtract).then_inc(glo_g, 1)
            g.wait_ge(pos_done, 2)
            for n in range(TILES):
                for k in range(2):
                    g.indirect_dma_start(out=slots_dram, out_offset=bass.IndirectOffsetOnAxis(ap=pos_i[:, k, n:n + 1], axis=0),
                                         in_=xn[:, n, :], in_offset=None).then_inc(scat, 16)
            g.wait_ge(xt_ps, HALVES + CH)
            g.wait_ge(scat, 16 * 2 * TILES)
            g.dma_start(shared_place[:].rearrange("p (e f) -> p e f", e=NE),
                         b1_all.unsqueeze(0).to_broadcast([P, NE, FF])).then_inc(b1_in, 16)
            g.wait_ge(b1_in, 16)

        def output(act, n):
            act.wait_ge(y_acc, FC * n + FC)
            if n >= 1:
                act.wait_ge(yb_ps, 2 * n)
            for k in range(KC):
                act.activation(yt[:, k, :], ps[:, Y_BANK + k, :], ACT.Identity, bias=b2c[:, k:k + 1]).then_inc(yt_a, 1)

        @block.scalar
        def _(act):
            def x_high_half(h):
                act.wait_ge(xt_ps, h + 1)
                if h >= 2:
                    act.wait_ge(lg_ps, h - 1)
                act.copy(x_hi[:, :, (h % 2) * HW:(h % 2 + 1) * HW],
                         ps[:, T_BANK + h % 2, :].rearrange("p (k t) -> p k t", k=KC)).then_inc(xhi_s, 1)

            def logits_out(h):
                act.wait_ge(lg_ps, h + 1)
                if h >= 2:
                    act.wait_ge(lgt_ps, h - 1)
                act.activation(lg_t[:, (h % 2) * HW:(h % 2 + 1) * HW], ps[0:NE, H_BANK + h % 2, 0:HW],
                               ACT.Identity, bias=rb[:, 0:1]).then_inc(lg_s, 1)

            def x_high(n):
                act.wait_ge(xt_ps, HALVES + n + 1)
                if n == 0:
                    act.wait_ge(lg_ps, HALVES)
                else:
                    act.wait_ge(h_ps, FC * n)
                for k in range(KC):
                    act.copy(x_hi[:, k, :], ps[:, T_BANK + k, :]).then_inc(xhi_s, 1)

            def weights_high(m):
                raw, hi, _ = parts(m)
                act.wait_ge(w_in[m % 2], 16 * (m // 2 + 1))
                if m == 2 * NE:
                    act.wait_ge(y_acc, JOBS)
                act.copy(hi, raw).then_inc(w_hi_done, 1)

            act.wait_ge(const_in, 16 * 7)
            act.copy(rw_hi[:], rw_in[:]).then_inc(rw_s, 1)
            x_high_half(0)
            for h in range(1, HALVES):
                x_high_half(h)
                logits_out(h - 1)
                if h in (3, 5):
                    weights_high(h // 2 - 1)
            logits_out(HALVES - 1)
            x_high(0)
            act.wait_ge(sub_done, 1)
            act.activation(pr[:], pr[:], ACT.Exp).then_inc(exp_done, 1)
            for n in range(CH):
                for c in range(FC):
                    j = FC * n + c
                    act.wait_ge(h_ps, j + 1)
                    if c == FC - 1 and n + 1 < CH:
                        x_high(n + 1)
                    if j == 0:
                        act.wait_ge(lgt_ps, HALVES)
                    if j >= 2:
                        if j - 2 < POOL_JOBS:
                            act.wait_ge(glo_g, j - 1)
                        else:
                            act.wait_ge(glo_v, j - 1 - POOL_JOBS)
                    act.activation(gl[j % 2][:], ps[:, H_BANK + j % 2, :], ACT.Gelu, bias=b1c[:, c:c + 1]).then_inc(g_a, 1)
                    act.wait_ge(g_a, j + 1)
                    if j >= 3:
                        act.wait_ge(y_acc, j - 2)
                    act.copy(g_hi[j % 3][:], gl[j % 2][:]).then_inc(ghi_a, 1)
                    if c == 1 and n >= 1:
                        output(act, n - 1)
                    for m in matrices_at(j):
                        weights_high(m)
            output(act, CH - 1)
            weights_high(2 * NE)
            weights_high(2 * NE + 1)

        @block.vector
        def _(v):
            count = [0]

            def link(ins):
                count[0] += 1
                ins.then_inc(dve, 1)
                v.wait_ge(dve, count[0])

            def x_low_half(h):
                v.wait_ge(xhi_s, h + 1)
                part = slice((h % 2) * HW, (h % 2 + 1) * HW)
                v.tensor_tensor(x_lo[:, :, part], ps[:, T_BANK + h % 2, :].rearrange("p (k t) -> p k t", k=KC),
                                x_hi[:, :, part].bitcast(F32), ALU.subtract).then_inc(xlo_s, 1)

            def x_low(n):
                v.wait_ge(xhi_s, HALVES + KC * n + KC)
                for k in range(KC):
                    v.tensor_tensor(x_lo[:, k, :], ps[:, T_BANK + k, :], x_hi[:, k, :].bitcast(F32),
                                    ALU.subtract).then_inc(xlo_s, 1)

            def normalise(tiles):
                for n in tiles:
                    v.tensor_scalar(xn[:, n, :], h_all[:, n, :], mv[:, n, 0:1], rstd[:, n:n + 1],
                                    ALU.subtract, ALU.mult).then_inc(xn_done, 1)

            def weights_low(m):
                raw, hi, lo = parts(m)
                v.wait_ge(w_hi_done, m + 1)
                v.tensor_tensor(lo, raw, hi.bitcast(F32), ALU.subtract).then_inc(w_lo_done, 1)

            def add_to_h(n):
                for half in range(2):
                    v.wait_ge(yb_ps, 2 * n + half + 1)
                    tok = h_all[:, 4 * n + 2 * half:4 * n + 2 * half + 2, :]
                    v.tensor_tensor(tok, ps[:, RANK_BANK if half else BACK_BANK, :].rearrange("p (t d) -> p t d", t=2), tok,
                                    ALU.add).then_inc(h_v, 1)

            for first, last in ((0, 4), (4, TILES)):
                for n in range(first, last):
                    ins = v.bn_aggr(mv[:, n, :], stats[:, n, :])
                link(ins)
                v.tensor_scalar(vare[:, first:last], mv[:, first:last, 1], EPS, None, ALU.add).then_inc(mean_var, 1)
            v.wait_ge(const_in, 16 * 7)
            v.wait_ge(rw_s, 1)
            v.tensor_tensor(rw_lo[:], rw_in[:], rw_hi[:].bitcast(F32), ALU.subtract).then_inc(rw_s, 1)
            v.wait_ge(rstd_done, 1)
            normalise(range(4))
            for h in range(HALVES):
                x_low_half(h)
                if h == 0:
                    v.wait_ge(rstd_done, 2)
                normalise(range(2 * h + 4, min(2 * h + 6, TILES)))
            weights_low(0)
            weights_low(1)
            x_low(0)
            v.wait_ge(lgt_ps, HALVES)
            lg = ps[:, RANK_BANK, LGT].rearrange("p (n e) -> p n e", e=NE)
            over = lambda s: s.unsqueeze(2).to_broadcast(S3)
            link(v.tensor_reduce(s1[:], lg, AX_X, ALU.max))
            v.tensor_tensor(pr[:], lg, over(s1[:]), ALU.subtract).then_inc(sub_done, 1)
            v.wait_ge(exp_done, 1)
            link(v.tensor_reduce(s1[:], pr[:], AX_X, ALU.add))
            link(v.reciprocal(s1[:], s1[:]))
            link(v.tensor_tensor(pr[:], pr[:], over(s1[:]), ALU.mult))
            rank = rk[:].unsqueeze(1).to_broadcast(S3)
            cur = pr
            for k, oh in enumerate((oh1, oh2)):
                top = w_top[:, k, :]
                link(v.tensor_reduce(top, cur[:], AX_X, ALU.max))
                link(v.tensor_tensor(b3[:], cur[:], over(top), ALU.is_equal))
                link(v.tensor_tensor(b3[:], b3[:], rank, ALU.mult))
                link(v.tensor_reduce(s2[:], b3[:], AX_X, ALU.max))
                link(v.tensor_tensor(oh[:], b3[:], over(s2[:]), ALU.is_equal))
                if k == 0:
                    link(v.scalar_tensor_tensor(out=a3[:], in0=oh[:], scalar=-BIG, in1=pr[:], op0=ALU.mult, op1=ALU.add))
                    cur = a3
            v.tensor_tensor(sel_b[:], oh1[:], oh2[:], ALU.add).then_inc(sel_done, 1)
            v.wait_ge(rank_ps, 1)
            within = ps[:, RANK_BANK, WITHIN].rearrange("p (n e) -> p n e", e=NE)
            totals = ps[:, RANK_BANK, TOTALS].rearrange("p (n e) -> p n e", e=NE)
            link(v.tensor_copy(a3[:], totals))
            src, dst = a3, b3
            for k in range(4):
                m = 1 << k
                v.tensor_copy(dst[:, 0:m], src[:, 0:m])
                link(v.tensor_tensor(dst[:, m:], src[:, m:], src[:, 0:TILES - m], ALU.add))
                src, dst = dst, (c3 if k == 0 else src)
            incl = src
            link(v.tensor_tensor(dst[:], incl[:], totals, ALU.subtract))
            link(v.tensor_tensor(dst[:], dst[:], within, ALU.add))
            ranks = dst
            link(v.tensor_scalar(ei[:], incl[:, TILES - 1, :], float(P - 1), None, ALU.add))
            link(v.tensor_scalar(ei[:], ei[:], 7, None, ALU.arith_shift_right))
            link(v.tensor_copy(e1[:], ei[:]))
            src, dst = e1, e2
            for k in range(3):
                m = 1 << k
                v.tensor_copy(dst[:, 0:m], src[:, 0:m])
                link(v.tensor_tensor(dst[:, m:], src[:, m:], src[:, 0:NE - m], ALU.add))
                src, dst = dst, (e3 if k == 0 else src)
            ends = src
            x_low(1)
            v.tensor_tensor(te[:], tno[:].unsqueeze(2).to_broadcast([P, SLOT_TILES, NE]),
                            ends[:].unsqueeze(1).to_broadcast([P, SLOT_TILES, NE]), ALU.is_ge)
            link(v.tensor_tensor(dst[:], ends[:], e1[:], ALU.subtract))
            link(v.tensor_reduce(tf[:], te[:], AX_X, ALU.add))
            link(v.tensor_scalar(dst[:], dst[:], float(P), None, ALU.mult))
            link(v.tensor_tensor(ranks[:], ranks[:], dst[:].unsqueeze(1).to_broadcast(S3), ALU.add))
            v.tensor_scalar(tc[:, 2:2 + SLOT_TILES], tf[:], float(NE - 1), None, ALU.min)
            link(v.memset(tc[:, 0:2], 0.0))
            link(v.memset(tc[:, 2 + SLOT_TILES:], 0.0))
            for k, ofs in ((3, 1), (2, 0), (1, 3)):
                link(v.scalar_tensor_tensor(out=code[:], in0=tc[:, ofs:ofs + SLOT_TILES + 1], scalar=float(NE ** k),
                                            in1=tc[:, 2:3 + SLOT_TILES] if k == 3 else code[:], op0=ALU.mult, op1=ALU.add))
            v.tensor_copy(step_code[:], code[:]).then_inc(code_done, 1)
            for k, oh in enumerate((oh1, oh2)):
                link(v.tensor_tensor(pr[:], oh[:], ranks[:], ALU.mult))
                link(v.tensor_reduce(pf[:, k, :], pr[:], AX_X, ALU.add))
                v.tensor_copy(pos_i[:, k, :], pf[:, k, :]).then_inc(pos_done, 1)
            for n in range(CH):
                for c in range(FC):
                    j = FC * n + c
                    if c == FC - 1 and 1 <= n < CH - 1:
                        x_low(n + 1)
                    if j >= POOL_JOBS:
                        v.wait_ge(ghi_a, j + 1)
                        v.wait_ge(y_acc, j - 2)
                        v.tensor_tensor(g_lo[j % 3][:], gl[j % 2][:], g_hi[j % 3][:].bitcast(F32),
                                        ALU.subtract).then_inc(glo_v, 1)
                    for m in matrices_at(j):
                        weights_low(m)
                    if c == FC - 1 and n >= 1:
                        add_to_h(n - 1)
            weights_low(2 * NE)
            add_to_h(CH - 1)
            weights_low(2 * NE + 1)

        @block.tensor
        def _(pe):
            def turn_half(h):
                pe.wait_ge(xn_done, 2 * h + 2)
                if h >= 2:
                    pe.wait_ge(xlo_s, h - 1)
                for k in range(KC):
                    for t in range(2):
                        last = pe.transpose(ps[:, T_BANK + h % 2, k * HW + t * P:k * HW + (t + 1) * P],
                                            xn[:, 2 * h + t, k * P:(k + 1) * P], idn[:])
                last.then_inc(xt_ps, 1)

            def logits(h):
                pe.wait_ge(xhi_s, h + 1)
                pe.wait_ge(xlo_s, h + 1)
                if h >= 2:
                    pe.wait_ge(lg_s, h - 1)
                part = slice((h % 2) * HW, (h % 2 + 1) * HW)
                pairs = [(w[:, k, :], x[:, k, part]) for k in range(KC)
                         for w, x in ((rw_hi, x_hi), (rw_hi, x_lo), (rw_lo, x_hi))]
                for i, (w, x) in enumerate(pairs):
                    last = pe.matmul(ps[0:NE, H_BANK + h % 2, 0:HW], w, x, start=i == 0, stop=i == len(pairs) - 1)
                last.then_inc(lg_ps, 1)

            def turn_logits(h):
                pe.wait_ge(lg_s, h + 1)
                for t in range(2):
                    m = 2 * h + t
                    ofs = (h % 2) * HW + t * P
                    last = pe.transpose(ps[:, RANK_BANK, m * NE:(m + 1) * NE], lg_t[:, ofs:ofs + P], idn[0:NE, 0:NE])
                last.then_inc(lgt_ps, 1)

            def turn_x(n):
                pe.wait_ge(xlo_s, HALVES + KC * n)
                for k in range(KC):
                    for t in range(4):
                        last = pe.transpose(ps[:, T_BANK + k, t * P:(t + 1) * P],
                                            xn[:, 4 * n + t, k * P:(k + 1) * P], idn[:])
                last.then_inc(xt_ps, 1)

            def first_layer(j):
                n, c = j // FC, j % FC
                if c == 0:
                    pe.wait_ge(xhi_s, HALVES + KC * n + KC)
                    pe.wait_ge(xlo_s, HALVES + KC * n + KC)
                if j >= 2:
                    pe.wait_ge(g_a, j - 1)
                pairs = [(w1_all[:, HELD, k, s, c * P:(c + 1) * P], x[:, k, :]) for k in range(KC)
                         for s, x in ((0, x_hi), (0, x_lo), (1, x_hi))]
                for i, (w, x) in enumerate(pairs):
                    last = pe.matmul(ps[:, H_BANK + j % 2, :], w, x, start=i == 0, stop=i == len(pairs) - 1)
                last.then_inc(h_ps, 1)

            def second_layer(j):
                n, c = j // FC, j % FC
                if j < POOL_JOBS:
                    pe.wait_ge(glo_g, j + 1)
                else:
                    pe.wait_ge(glo_v, j + 1 - POOL_JOBS)
                pe.wait_ge(ghi_a, j + 1)
                if c == 0 and n >= 1:
                    pe.wait_ge(yt_a, KC * n)
                for k in range(KC):
                    for i, (s, x) in enumerate(((0, g_hi), (0, g_lo), (1, g_hi))):
                        last = pe.matmul(ps[:, Y_BANK + k, :], w2_all[:, HELD, c, s, k * P:(k + 1) * P], x[j % 3][:],
                                         start=c == 0 and i == 0, stop=c == FC - 1 and i == 2)
                last.then_inc(y_acc, 1)

            def turn_back(n):
                pe.wait_ge(yt_a, KC * n + KC)
                for half in range(2):
                    bank = RANK_BANK if half else BACK_BANK
                    if n >= 1:
                        pe.wait_ge(h_v, 2 * n - 1 + half)
                    elif half:
                        pe.wait_ge(pos_done, 2)
                    for t in range(2):
                        for k in range(KC):
                            last = pe.transpose(ps[:, bank, t * DM + k * P:t * DM + (k + 1) * P],
                                                yt[:, k, (2 * half + t) * P:(2 * half + t + 1) * P], idn[:])
                    last.then_inc(yb_ps, 1)

            pe.wait_ge(const_in, 16 * 7)
            pe.wait_ge(rw_s, 2)
            turn_half(0)
            turn_half(1)
            for h in range(HALVES):
                logits(h)
                if h + 2 < HALVES:
                    turn_half(h + 2)
                if h >= 1:
                    turn_logits(h - 1)
            turn_x(0)
            turn_logits(HALVES - 1)
            pe.wait_ge(w_lo_done, 2)
            for j in range(JOBS):
                n, c = j // FC, j % FC
                first_layer(j)
                if c == FC - 1 and n >= 1:
                    turn_back(n - 1)
                if j >= 2:
                    second_layer(j - 2)
                if c == 0 and n + 1 < CH:
                    turn_x(n + 1)
                if j == 2:
                    pe.wait_ge(sel_done, 1)
                    pe.wait_ge(prep, 2)
                    sel = sel_b[:].rearrange("p n e -> p (n e)")
                    pe.matmul(ps[:, RANK_BANK, WITHIN], tri[:], sel, start=True, stop=True)
                    pe.matmul(ps[:, RANK_BANK, TOTALS], ones[:], sel, start=True, stop=True).then_inc(rank_ps, 1)
            second_layer(JOBS - 2)
            second_layer(JOBS - 1)
            turn_back(CH - 1)


def expert_phase(nc, slots_dram, y_dram, shared_place, b2_all, idn, w1_all, w2_all, step_code):
    with ExitStack() as ctx:
        def sb(name, shape, dt=F32):
            return ctx.enter_context(nc.sbuf_tensor(name, shape, dt))

        def sem(name):
            return ctx.enter_context(nc.semaphore(name))

        b1 = shared_place[:].rearrange("p (e f) -> p e f", e=NE)
        b2 = sb("ex_b2", [P, NE, DM])
        xin = [sb(f"ex_xin{i}", [P, DM]) for i in range(2)]
        x_hi = [sb(f"ex_x_hi{i}", [P, DM], F32R) for i in range(2)]
        x_lo = [sb(f"ex_x_lo{i}", [P, DM], F32R) for i in range(2)]
        hb = [sb(f"ex_hb{i}", [P, FF]) for i in range(2)]
        h_hi = [sb(f"ex_h_hi{i}", [P, FF], F32R) for i in range(2)]
        h_lo = [sb(f"ex_h_lo{i}", [P, FF], F32R) for i in range(2)]
        yo = [sb(f"ex_y{i}", [P, DM]) for i in range(2)]
        ps = ctx.enter_context(nc.psum_tensor("ex_ps", [P, 8, 512], F32))

        bias_in = sem("ex_bias_in")
        x_in = [sem(f"ex_x_in{i}") for i in range(2)]
        y_out = [sem(f"ex_y_out{i}") for i in range(2)]
        xt_ps = sem("ex_xt_ps")
        xhi_s = sem("ex_xhi_s")
        xlo_s = sem("ex_xlo_s")
        h_ps = sem("ex_h_ps")
        hb_v = sem("ex_hb_v")
        gelu_a = sem("ex_gelu_a")
        ht_ps = sem("ex_ht_ps")
        hhi_a = sem("ex_hhi_a")
        hlo_v = sem("ex_hlo_v")
        y_ps = sem("ex_y_ps")
        y_b = sem("ex_y_b")
        y_v = sem("ex_y_v")

        block = ctx.enter_context(nc.Block())
        PEEL = 5
        PAIRS = (SLOT_TILES - PEEL) // 2
        assert SLOT_TILES == PEEL + 2 * PAIRS

        def in_pairs(eng, body):
            for i in range(PEEL):
                body(i, i % 2, i // 2)
            with eng.Fori(0, PAIRS - 1) as n:
                body(n * 2 + PEEL, 1, n + PEEL // 2)
                body(n * 2 + PEEL + 1, 0, n + PEEL // 2 + 1)
            for i in range(SLOT_TILES - 2, SLOT_TILES + 2):
                body(i, i % 2, i // 2)

        def in_pairs_by_expert(eng, body):
            def experts(i):
                at = slice(i, i + 1) if isinstance(i, int) else bass.ds(i, 1)
                code = eng.value_load(step_code[0:1, at], min_val=0, max_val=NE ** 4 - 1)
                return [(code // NE ** k) % NE for k in range(4)]

            def pair(i, k):
                e = experts(i)
                body(i, 1, k, e[0], e[2])
                body(i + 1, 0, k + 1, e[1], e[3])

            body(0, 0, 0, experts(0)[0], None)
            for i in range(1, PEEL, 2):
                pair(i, i // 2)
            with eng.Fori(0, PAIRS - 1) as n:
                pair(n * 2 + PEEL, n + PEEL // 2)
            pair(SLOT_TILES - 2, (SLOT_TILES - 2) // 2)
            pair(SLOT_TILES, SLOT_TILES // 2)

        def fetched(i):
            return not isinstance(i, int) or i < SLOT_TILES

        def runs(i):
            return not isinstance(i, int) or 0 <= i < SLOT_TILES

        def rows(i):
            return bass.ds(i * P, P)

        @block.sync
        def _(sp):
            sp.dma_start(xin[0][:], slots_dram[0:P, :]).then_inc(x_in[0], 16)
            sp.dma_start(xin[1][:], slots_dram[P:2 * P, :]).then_inc(x_in[1], 16)
            sp.wait_ge(x_in[1], 16)
            sp.dma_start(b2[:], b2_all.unsqueeze(0).to_broadcast([P, NE, DM])).then_inc(bias_in, 16)

            def step(i, par, k):
                sp.wait_ge(xt_ps, i + 1)
                sp.dma_start(xin[par][:], slots_dram[rows(i + 2), :]).then_inc(x_in[par], 16)

            for i in range(PEEL):
                step(i, i % 2, i // 2)
            with sp.Fori(0, PAIRS - 1) as n:
                step(n * 2 + PEEL, 1, 0)
                step(n * 2 + PEEL + 1, 0, 0)

        @block.gpsimd
        def _(g):
            def step(i, par, k):
                if runs(i):
                    g.wait_ge(y_v, i + 1)
                    g.dma_start(y_dram[rows(i), :], yo[par][:]).then_inc(y_out[par], 16)

            in_pairs(g, step)
            g.wait_ge(y_out[0], 16 * ((SLOT_TILES + 1) // 2))
            g.wait_ge(y_out[1], 16 * (SLOT_TILES // 2))

        @block.tensor
        def _(pe):
            def turn_x(i, par, k):
                pe.wait_ge(x_in[par], 16 * k + 16)
                wait_reuse(pe, xlo_s, i - 1)
                for c in range(KC):
                    last = pe.transpose(ps[:, 6 + par, c * P:(c + 1) * P], xin[par][:, c * P:(c + 1) * P], idn[:])
                last.then_inc(xt_ps, 1)

            def first_layer(i, par, e):
                pe.wait_ge(xhi_s, i + 1)
                pe.wait_ge(xlo_s, i + 1)
                wait_reuse(pe, hb_v, i - 1)
                pairs = [(x[par][:, c * P:(c + 1) * P], w1_all[:, bass.ds(e, 1), c, part, :].rearrange("p o n -> p (o n)"))
                         for c in range(KC) for x, part in ((x_hi, 0), (x_hi, 1), (x_lo, 0))]
                for n, (x, w) in enumerate(pairs):
                    last = pe.matmul(ps[:, par, :], x, w, start=n == 0, stop=n == len(pairs) - 1)
                last.then_inc(h_ps, 1)

            def turn_h(i, par):
                pe.wait_ge(gelu_a, i + 1)
                wait_reuse(pe, hlo_v, i - 1)
                for c in range(FC):
                    last = pe.transpose(ps[:, 2 + par, c * P:(c + 1) * P], hb[par][:, c * P:(c + 1) * P], idn[:])
                last.then_inc(ht_ps, 1)

            def second_layer(i, par, e):
                pe.wait_ge(hhi_a, i + 1)
                pe.wait_ge(hlo_v, i + 1)
                wait_reuse(pe, y_v, i - 1)
                for c in range(FC):
                    w = w2_all[:, bass.ds(e, 1), c]
                    pe.matmul(ps[:, 4 + par, :], h_hi[par][:, c * P:(c + 1) * P],
                              w.rearrange("p o s n -> p (o s n)"), start=c == 0, stop=False, skip_group_check=True)
                    last = pe.matmul(ps[:, 4 + par, 0:DM], h_lo[par][:, c * P:(c + 1) * P],
                                     w[:, :, 0, :].rearrange("p o n -> p (o n)"),
                                     start=False, stop=c == FC - 1, skip_group_check=True)
                last.then_inc(y_ps, 1)

            turn_x(0, 0, 0)
            turn_x(1, 1, 0)

            def step(i, par, k, e1, e2):
                if runs(i):
                    first_layer(i, par, e1)
                if runs(i - 1):
                    turn_h(i - 1, 1 - par)
                if fetched(i + 2):
                    turn_x(i + 2, par, k + 1)
                if runs(i - 2):
                    second_layer(i - 2, par, e2)

            in_pairs_by_expert(pe, step)

        @block.scalar
        def _(act):
            def x_high(i, par):
                act.wait_ge(xt_ps, i + 1)
                wait_reuse(act, h_ps, i - 1)
                act.copy(x_hi[par][:], ps[:, 6 + par, 0:DM]).then_inc(xhi_s, 1)

            x_high(0, 0)
            x_high(1, 1)

            def step(i, par, k):
                if runs(i - 1):
                    act.wait_ge(ht_ps, i)
                    wait_reuse(act, y_ps, i - 2)
                    act.copy(h_hi[1 - par][:], ps[:, 3 - par, :]).then_inc(hhi_a, 1)
                if runs(i):
                    if fetched(i + 2):
                        x_high(i + 2, par)
                    act.wait_ge(hb_v, i + 1)
                    act.activation(hb[par][:], hb[par][:], ACT.Gelu).then_inc(gelu_a, 1)

            in_pairs(act, step)

        @block.vector
        def _(v):
            def bias(b, e):
                return b[:, bass.ds(e, 1), :].rearrange("p o n -> p (o n)")

            def x_low(i, par):
                v.wait_ge(xhi_s, i + 1)
                wait_reuse(v, h_ps, i - 1)
                v.tensor_tensor(x_lo[par][:], ps[:, 6 + par, 0:DM], x_hi[par][:].bitcast(F32),
                                ALU.subtract).then_inc(xlo_s, 1)

            x_low(0, 0)
            x_low(1, 1)

            def step(i, par, k, e1, e2):
                if runs(i):
                    v.wait_ge(h_ps, i + 1)
                    wait_reuse(v, ht_ps, i - 1)
                    v.tensor_tensor(hb[par][:], ps[:, par, :], bias(b1, e1), ALU.add).then_inc(hb_v, 1)
                if runs(i - 1):
                    v.wait_ge(hhi_a, i)
                    wait_reuse(v, y_ps, i - 2)
                    v.tensor_tensor(h_lo[1 - par][:], ps[:, 3 - par, :], h_hi[1 - par][:].bitcast(F32),
                                    ALU.subtract).then_inc(hlo_v, 1)
                if fetched(i + 2):
                    x_low(i + 2, par)
                if runs(i - 2):
                    v.wait_ge(y_ps, i - 1)
                    if isinstance(i, int):
                        v.wait_ge(bias_in, 16)
                    wait_reuse(v, y_out[par], 16 * (k - 1))
                    v.tensor_tensor(yo[par][:], ps[:, 4 + par, DM:], bias(b2, e2), ALU.add).then_inc(y_b, 1)
                    v.wait_ge(y_b, i - 1)
                    v.tensor_tensor(yo[par][:], ps[:, 4 + par, 0:DM], yo[par][:], ALU.add).then_inc(y_v, 1)

            in_pairs_by_expert(v, step)


def combine_phase(nc, h_all, y_dram, pos_i, w_top, out):
    BUF = 4
    with ExitStack() as ctx:
        ya, yb = ([ctx.enter_context(nc.sbuf_tensor(f"co_{name}{i}", [P, DM], F32)) for i in range(BUF)]
                  for name in ("ya", "yb"))
        gath = [ctx.enter_context(nc.semaphore(f"co_gather{i}")) for i in range(BUF)]
        store = ctx.enter_context(nc.semaphore("co_store"))
        added = ctx.enter_context(nc.semaphore("co_added"))
        block = ctx.enter_context(nc.Block())
        tok = out.rearrange("b t d -> (b t) d")

        @block.gpsimd
        def _(g):
            for n in range(TILES):
                if n >= BUF:
                    g.wait_ge(added, 2 * (n - BUF + 1))
                for k, dst in enumerate((ya, yb)):
                    g.indirect_dma_start(out=dst[n % BUF][:], out_offset=None, in_=y_dram,
                                         in_offset=bass.IndirectOffsetOnAxis(ap=pos_i[:, k, n:n + 1], axis=0)
                                         ).then_inc(gath[n % BUF], 16)

        @block.sync
        def _(sp):
            for n in range(TILES):
                sp.wait_ge(added, 2 * n + 2)
                sp.dma_start(tok[n * P:(n + 1) * P, :], h_all[:, n, :]).then_inc(store, 16)
            sp.wait_ge(store, 16 * TILES)

        @block.vector
        def _(v):
            for n in range(TILES):
                v.wait_ge(gath[n % BUF], 32 * (n // BUF + 1))
                for k, y in enumerate((ya, yb)):
                    if k:
                        v.wait_ge(added, 2 * n + 1)
                    v.scalar_tensor_tensor(out=h_all[:, n, :], in0=y[n % BUF][:], scalar=w_top[:, k, n:n + 1],
                                           in1=h_all[:, n, :], op0=ALU.mult, op1=ALU.add).then_inc(added, 1)


def tower_kernel(nc, x_t, a_real_t, a_imag_t, b_t, log_dt, w_qkv, b_qkv, w_o, b_o, router_w, router_b,
                 sw1, sw2, sb1_t, sb2_t, rw1, rw2, b1_all, b2_all, rope, ident, ident_b, mask_b, select_b, tri_b,
                 rank8, tile_no, out):
    slots_dram = nc.dram_tensor("slots_scratch", (-(-SLOT_TILES // NB) * NB * P, DM), F32, kind="Internal").ap()
    y_dram = nc.dram_tensor("y_scratch", (SLOT_TILES * P, DM), F32, kind="Internal").ap()
    w1, w2 = ([w[e] for e in range(NE)] for w in (rw1, rw2))

    with ExitStack() as ctx:
        def sb(name, shape, dt=F32):
            return ctx.enter_context(nc.sbuf_tensor(name, shape, dt))

        h_all = sb("h_all", [P, TILES, DM])
        stats = sb("stats", [P, TILES, 6])
        pos_i = sb("pos_i", [P, 2, TILES], U32)
        w_top = sb("w_top", [P, 2, TILES])
        step_code = sb("step_code", [P, SLOT_TILES + 1], I32)
        idn = sb("ident", [P, P])
        with nc.sbuf_tensor("w_in", [P, KC, 4 * DM], F32) as w_in:
            s4d_phase(nc, x_t, a_real_t, a_imag_t, b_t, log_dt, ident, w_qkv, w_o, idn, w_in, h_all)
            attention_phase(nc, w_in, b_qkv, b_o, rope, idn, ident_b, mask_b, select_b,
                            slots_dram, h_all, stats)
        shared_place = sb("shared_place", [P, TILES * DM])
        w1_all = sb("w1_all", [P, NE, KC, 2, FF], F32R)
        w2_all = sb("w2_all", [P, NE, FC, 2, DM], F32R)
        shared_and_routing_phase(nc, h_all, slots_dram, router_w, router_b, sw1, sw2, sb1_t, sb2_t, idn,
                                 tri_b, rank8, tile_no, w1_all, w2_all, w1, w2, stats,
                                 pos_i, w_top, step_code, shared_place, b1_all)
        expert_phase(nc, slots_dram, y_dram, shared_place, b2_all, idn, w1_all, w2_all, step_code)
        combine_phase(nc, h_all, y_dram, pos_i, w_top, out)


def kernel(**inputs):
    import ml_dtypes
    import numpy as np
    import concourse.bacc as bacc
    from concourse.bass_utils import run_bass_kernel_spmd

    def channels(a):
        return a.reshape(4, SEQ // 4, *a.shape[1:]).swapaxes(0, 1).reshape(a.shape)

    i = {name: np.asarray(a) for name, a in inputs.items()}
    bf16 = ml_dtypes.bfloat16
    freq = 1.0 / 1000.0 ** (np.arange(0, HS, 2, dtype=np.float32) / HS)
    angle = np.arange(SEQ, dtype=np.float32)[:, None] * freq[None]
    rope = np.empty((SEQ, 2, HS), np.float32)
    rope[:, 0, 0::2] = rope[:, 0, 1::2] = np.cos(angle)
    rope[:, 1, 0::2] = -np.sin(angle)
    rope[:, 1, 1::2] = np.sin(angle)
    causal = np.triu(np.full((P, P), -1e30, np.float32), 1)
    select = np.zeros((P, NH, P), np.float32)
    for h in range(NH):
        select[[h, NH + h], h] = 1.0
    arrays = dict(
        x_t=channels(i["x"].transpose(1, 2, 3, 0)).transpose(1, 2, 0, 3),
        a_real_t=channels(i["L0_tok_inv_A_real"]).T,
        a_imag_t=channels(i["L0_tok_A_imag"]).T,
        b_t=channels(i["L0_tok_B_ri"]).transpose(1, 2, 0),
        log_dt=channels(i["L0_tok_log_dt"]),
        w_qkv=i["L0_attn_W_attn"].T, b_qkv=i["L0_attn_b_attn"],
        w_o=i["L0_attn_W_o"].T, b_o=i["L0_attn_b_o"],
        router_w=i["L0_ffn_router_w"], router_b=i["L0_ffn_router_b"],
        sw1=i["L0_ffn_sw1"], sw2=i["L0_ffn_sw2"],
        sb1_t=i["L0_ffn_sb1"].reshape(FC, P).T, sb2_t=i["L0_ffn_sb2"].reshape(KC, P).T,
        rw1=i["L0_ffn_rw1"], rw2=i["L0_ffn_rw2"],
        b1_all=i["L0_ffn_rb1"],
        b2_all=i["L0_ffn_rb2"],
        rope=rope.reshape(NT, P, 2, HS).transpose(1, 0, 2, 3),
        ident=np.eye(P, dtype=np.float32), ident_b=np.eye(P).astype(bf16),
        mask_b=np.tile(causal, (1, 4)).astype(bf16), select_b=select.astype(bf16),
        tri_b=np.triu(np.ones((P, P)), 1).astype(bf16),
        rank8=(NE - np.arange(NE)).astype(np.float32),
        tile_no=np.arange(SLOT_TILES).astype(np.float32))
    arrays = {f"in_{name}": np.ascontiguousarray(a) for name, a in arrays.items()}

    nc = bacc.Bacc("TRN2", target_bir_lowering=False, num_devices=1)
    args = [nc.dram_tensor(name, a.shape, mybir.dt.from_np(a.dtype), kind="ExternalInput").ap()
            for name, a in arrays.items()]
    out = nc.dram_tensor("out", (NB, SEQ, DM), F32, kind="ExternalOutput").ap()
    tower_kernel(nc, *args, out)
    result = run_bass_kernel_spmd(nc, [arrays], core_ids=[0])
    return result.results[0]["out"]
```
